# Optimizing a Trainium2 kernel written in Bass

```python
import numpy as np
import jax
import jax.numpy as jnp

def _softmax(x, axis=-1):
    return jax.nn.softmax(x, axis=axis)

def _gelu(x):
    return jax.nn.gelu(x, approximate=True)

def _silu(x):
    return jax.nn.silu(x)

def _sigmoid(x):
    return jax.nn.sigmoid(x)

def _layernorm(x, axis=-1, eps=1e-05):
    m = jnp.mean(x, axis=axis, keepdims=True)
    v = jnp.var(x, axis=axis, keepdims=True)
    return (x - m) / jnp.sqrt(v + eps)

def _scatter_add(tgt, idx, src, axis=0):
    return tgt.at[idx].add(src)

def _segment_sum(src, seg, n):
    return jax.ops.segment_sum(src, seg, n)
kernel_name = 'mk_decoder_preln_d1_seqx_r8_5079a6'

def setup_inputs(seed: int=0):
    np.random.seed(seed)
    _w = jnp.asarray

    def _rec_inputs():
        import jax
        import jax.numpy as jnp
        _rk = jax.random.key(seed)
        x = -0.0002928 + 1 * jax.random.normal(jax.random.fold_in(_rk, 1), (64, 64, 128), jnp.float32)
        _lenS = 64 - jax.random.randint(jax.random.fold_in(_rk, 7), (64,), 0, max(1, 64 // 4) + 1, jnp.int32)
        _lenS2 = 64 - jax.random.randint(jax.random.fold_in(_rk, 8), (64,), 0, max(1, 64 // 4) + 1, jnp.int32)
        _ctx_1024P = jax.random.normal(jax.random.fold_in(_rk, 11), (64, 16, 128), jnp.float32)
        _ctx_1024c = jax.random.dirichlet(jax.random.fold_in(_rk, 511), 0.3 * jnp.ones((16,), jnp.float32), (64, 64))
        _ctx_1024t = jnp.einsum('bsk,bkd->bsd', _ctx_1024c, _ctx_1024P)
        _ctx_1024t = _ctx_1024t * jax.lax.rsqrt(jnp.mean(jnp.square(_ctx_1024t)) + 1e-12) * 0.953939
        ctx_1024 = -1.39393e-06 + 0.999914 * (_ctx_1024t + 0.3 * jax.random.normal(jax.random.fold_in(_rk, 611), (64, 64, 128), jnp.float32))
        return (x, ctx_1024)
    x, ctx_1024 = _rec_inputs()

    def _L0_attn_setup():
        import jax, jax.numpy as jnp
        import numpy as np
        DIM = 128
        key = jax.random.key(seed)
        ks = jax.random.split(key, 10)
        d = DIM
        return {'x': jax.random.normal(ks[0], (8, 512, d), dtype=jnp.float32), 'A': jax.random.normal(ks[1], (d, d), dtype=jnp.float32) * 0.1, 'B': jax.random.normal(ks[2], (d, d), dtype=jnp.float32) * 0.1, 'W_in': jax.random.normal(ks[3], (d, d), dtype=jnp.float32) * (1.0 / np.sqrt(d)), 'b_in': jax.random.normal(ks[4], (d,), dtype=jnp.float32) * 0.01, 'W_gate': jax.random.normal(ks[5], (d, d), dtype=jnp.float32) * (1.0 / np.sqrt(d)), 'b_gate': jax.random.normal(ks[6], (d,), dtype=jnp.float32) * 0.01, 'W_out': jax.random.normal(ks[7], (d, d), dtype=jnp.float32) * (1.0 / np.sqrt(d)), 'b_out': jax.random.normal(ks[8], (d,), dtype=jnp.float32) * 0.01}
    _L0_attn_all = _L0_attn_setup()
    _L0_attn_in = {k: v for k, v in _L0_attn_all.items() if k in ('A', 'B', 'W_in', 'b_in', 'W_gate', 'b_gate', 'W_out', 'b_out')}
    del _L0_attn_all

    def _L0_xattn_setup():
        import jax, jax.numpy as jnp
        import numpy as np
        import math
        EPS = 1e-08
        LN_EPS = 1e-05
        B, S, E, NH = (2, 256, 128, 4)
        DH = E // NH

        def _mlstm_cell(q, k, v, igate_w, igate_b, fgate_w, fgate_b, out_w):
            Bq, Sq, Eq = q.shape
            if_in = jnp.concatenate([q, k, v], axis=-1)
            ig = jnp.einsum('bsf,hf->bsh', if_in, igate_w) + igate_b
            fg = jnp.einsum('bsf,hf->bsh', if_in, fgate_w) + fgate_b
            ig = jnp.transpose(ig, (0, 2, 1))[..., None]
            fg = jnp.transpose(fg, (0, 2, 1))[..., None]
            qh = q.reshape(Bq, Sq, NH, DH).transpose(0, 2, 1, 3)
            kh = k.reshape(Bq, Sq, NH, DH).transpose(0, 2, 1, 3)
            vh = v.reshape(Bq, Sq, NH, DH).transpose(0, 2, 1, 3)
            log_fg = jax.nn.log_sigmoid(fg)
            cs = jnp.cumsum(log_fg, axis=2)
            cs_shift = jnp.concatenate([jnp.zeros_like(cs[:, :, :1]), cs[:, :, :-1]], axis=2)
            logfg_mat = cs - jnp.swapaxes(cs_shift, -2, -1)
            ltr = jnp.tril(jnp.ones((Sq, Sq), dtype=bool))
            logfg_mat = jnp.where(ltr, logfg_mat, -jnp.inf)
            log_D = logfg_mat + jnp.swapaxes(ig, -2, -1)
            max_log_D = jnp.max(log_D, axis=-1, keepdims=True)
            D = jnp.exp(log_D - max_log_D)
            qk = jnp.einsum('bhsd,bhtd->bhst', qh, kh / math.sqrt(DH))
            C = qk * D
            sum_C_abs = jnp.abs(jnp.sum(C, axis=-1, keepdims=True))
            normaliser = jnp.maximum(sum_C_abs, jnp.exp(-max_log_D))
            C_norm = C / (normaliser + EPS)
            h = jnp.einsum('bhst,bhtd->bhsd', C_norm, vh)
            mean = jnp.mean(h, axis=-1, keepdims=True)
            var = jnp.mean((h - mean) ** 2, axis=-1, keepdims=True)
            h_norm = (h - mean) / jnp.sqrt(var + LN_EPS)
            scale = (1.0 + out_w).reshape(1, NH, 1, DH)
            h_norm = h_norm * scale
            return h_norm.transpose(0, 2, 1, 3).reshape(Bq, Sq, Eq)
        key = jax.random.key(seed)
        ks = jax.random.split(key, 7)
        std_g = math.sqrt(2.0 / (5.0 * 3 * E))
        return {'q': jax.random.normal(ks[0], (B, S, E), dtype=jnp.float32), 'k': jax.random.normal(ks[1], (B, S, E), dtype=jnp.float32), 'v': jax.random.normal(ks[2], (B, S, E), dtype=jnp.float32), 'igate_w': jax.random.normal(ks[3], (NH, 3 * E), dtype=jnp.float32) * std_g, 'igate_b': jax.random.normal(ks[4], (NH,), dtype=jnp.float32) * 0.1, 'fgate_w': jax.random.normal(ks[5], (NH, 3 * E), dtype=jnp.float32) * std_g, 'fgate_b': jnp.linspace(3.4, 6.0, NH, dtype=jnp.float32), 'out_w': jnp.zeros((E,), dtype=jnp.float32)}
    _L0_xattn_all = _L0_xattn_setup()
    _L0_xattn_in = {k: v for k, v in _L0_xattn_all.items() if k in ('igate_w', 'igate_b', 'fgate_w', 'fgate_b', 'out_w')}
    del _L0_xattn_all

    def _L0_ffn_setup():
        import jax, jax.numpy as jnp
        import numpy as np
        D_MODEL = 128
        HIDDEN = 512
        N_ROUTING = 2
        key = jax.random.key(seed)
        ks = jax.random.split(key, 10)
        s = 0.02
        x = jax.random.normal(ks[0], (4, 512, D_MODEL), dtype=jnp.float32)
        gate_w = jax.random.normal(ks[1], (N_ROUTING, D_MODEL), dtype=jnp.float32) * s
        w1 = jax.random.normal(ks[2], (N_ROUTING, D_MODEL, HIDDEN), dtype=jnp.float32) * s
        b1 = jax.random.normal(ks[3], (N_ROUTING, HIDDEN), dtype=jnp.float32) * s
        w2 = jax.random.normal(ks[4], (N_ROUTING, HIDDEN, D_MODEL), dtype=jnp.float32) * s
        b2 = jax.random.normal(ks[5], (N_ROUTING, D_MODEL), dtype=jnp.float32) * s
        sw1 = jax.random.normal(ks[6], (D_MODEL, HIDDEN), dtype=jnp.float32) * s
        sb1 = jax.random.normal(ks[7], (HIDDEN,), dtype=jnp.float32) * s
        sw2 = jax.random.normal(ks[8], (HIDDEN, D_MODEL), dtype=jnp.float32) * s
        sb2 = jax.random.normal(ks[9], (D_MODEL,), dtype=jnp.float32) * s
        return {'x': x, 'gate_w': gate_w, 'w1': w1, 'b1': b1, 'w2': w2, 'b2': b2, 'sw1': sw1, 'sb1': sb1, 'sw2': sw2, 'sb2': sb2}
    _L0_ffn_all = _L0_ffn_setup()
    _L0_ffn_in = {k: v for k, v in _L0_ffn_all.items() if k in ('gate_w', 'w1', 'b1', 'w2', 'b2', 'sw1', 'sb1', 'sw2', 'sb2')}
    del _L0_ffn_all
    return {'x': x, 'ctx_1024': ctx_1024, 'L0_attn_A': _L0_attn_in['A'], 'L0_attn_B': _L0_attn_in['B'], 'L0_attn_W_in': _L0_attn_in['W_in'], 'L0_attn_b_in': _L0_attn_in['b_in'], 'L0_attn_W_gate': _L0_attn_in['W_gate'], 'L0_attn_b_gate': _L0_attn_in['b_gate'], 'L0_attn_W_out': _L0_attn_in['W_out'], 'L0_attn_b_out': _L0_attn_in['b_out'], 'L0_xattn_igate_w': _L0_xattn_in['igate_w'], 'L0_xattn_igate_b': _L0_xattn_in['igate_b'], 'L0_xattn_fgate_w': _L0_xattn_in['fgate_w'], 'L0_xattn_fgate_b': _L0_xattn_in['fgate_b'], 'L0_xattn_out_w': _L0_xattn_in['out_w'], 'L0_ffn_gate_w': _L0_ffn_in['gate_w'], 'L0_ffn_w1': _L0_ffn_in['w1'], 'L0_ffn_b1': _L0_ffn_in['b1'], 'L0_ffn_w2': _L0_ffn_in['w2'], 'L0_ffn_b2': _L0_ffn_in['b2'], 'L0_ffn_sw1': _L0_ffn_in['sw1'], 'L0_ffn_sb1': _L0_ffn_in['sb1'], 'L0_ffn_sw2': _L0_ffn_in['sw2'], 'L0_ffn_sb2': _L0_ffn_in['sb2']}

def reference(x, ctx_1024, L0_attn_A, L0_attn_B, L0_attn_W_in, L0_attn_b_in, L0_attn_W_gate, L0_attn_b_gate, L0_attn_W_out, L0_attn_b_out, L0_xattn_igate_w, L0_xattn_igate_b, L0_xattn_fgate_w, L0_xattn_fgate_b, L0_xattn_out_w, L0_ffn_gate_w, L0_ffn_w1, L0_ffn_b1, L0_ffn_w2, L0_ffn_b2, L0_ffn_sw1, L0_ffn_sb1, L0_ffn_sw2, L0_ffn_sb2):
    import jax
    import jax.numpy as jnp

    def _L0_attn_ref(x, A, B, W_in, b_in, W_gate, b_gate, W_out, b_out):
        import jax, jax.numpy as jnp
        import numpy as np
        DIM = 128
        batch, seq, dim = x.shape
        inp = jnp.einsum('bsd,ed->bse', x, W_in) + b_in
        gate = jax.nn.sigmoid(jnp.einsum('bsd,ed->bse', inp, W_gate) + b_gate)
        u = jnp.einsum('bsd,ed->bse', inp, B)

        def step(state, t):
            inp_t, gate_t, u_t = t
            s = jnp.tanh(state @ A.T + u_t)
            s = gate_t * s + (1.0 - gate_t) * inp_t
            return (s, s)
        init = jnp.zeros((batch, dim), dtype=x.dtype)
        xs = (jnp.swapaxes(inp, 0, 1), jnp.swapaxes(gate, 0, 1), jnp.swapaxes(u, 0, 1))
        _, states = jax.lax.scan(step, init, xs)
        out = jnp.einsum('sbd,ed->sbe', states, W_out) + b_out
        return jnp.swapaxes(out, 0, 1)

    def _L0_xattn_ref(q, k, v, igate_w, igate_b, fgate_w, fgate_b, out_w):
        import jax, jax.numpy as jnp
        import numpy as np
        import math
        EPS = 1e-08
        LN_EPS = 1e-05
        B, S, E, NH = (2, 256, 128, 4)
        DH = E // NH

        def _mlstm_cell(q, k, v, igate_w, igate_b, fgate_w, fgate_b, out_w):
            Bq, Sq, Eq = q.shape
            if_in = jnp.concatenate([q, k, v], axis=-1)
            ig = jnp.einsum('bsf,hf->bsh', if_in, igate_w) + igate_b
            fg = jnp.einsum('bsf,hf->bsh', if_in, fgate_w) + fgate_b
            ig = jnp.transpose(ig, (0, 2, 1))[..., None]
            fg = jnp.transpose(fg, (0, 2, 1))[..., None]
            qh = q.reshape(Bq, Sq, NH, DH).transpose(0, 2, 1, 3)
            kh = k.reshape(Bq, Sq, NH, DH).transpose(0, 2, 1, 3)
            vh = v.reshape(Bq, Sq, NH, DH).transpose(0, 2, 1, 3)
            log_fg = jax.nn.log_sigmoid(fg)
            cs = jnp.cumsum(log_fg, axis=2)
            cs_shift = jnp.concatenate([jnp.zeros_like(cs[:, :, :1]), cs[:, :, :-1]], axis=2)
            logfg_mat = cs - jnp.swapaxes(cs_shift, -2, -1)
            ltr = jnp.tril(jnp.ones((Sq, Sq), dtype=bool))
            logfg_mat = jnp.where(ltr, logfg_mat, -jnp.inf)
            log_D = logfg_mat + jnp.swapaxes(ig, -2, -1)
            max_log_D = jnp.max(log_D, axis=-1, keepdims=True)
            D = jnp.exp(log_D - max_log_D)
            qk = jnp.einsum('bhsd,bhtd->bhst', qh, kh / math.sqrt(DH))
            C = qk * D
            sum_C_abs = jnp.abs(jnp.sum(C, axis=-1, keepdims=True))
            normaliser = jnp.maximum(sum_C_abs, jnp.exp(-max_log_D))
            C_norm = C / (normaliser + EPS)
            h = jnp.einsum('bhst,bhtd->bhsd', C_norm, vh)
            mean = jnp.mean(h, axis=-1, keepdims=True)
            var = jnp.mean((h - mean) ** 2, axis=-1, keepdims=True)
            h_norm = (h - mean) / jnp.sqrt(var + LN_EPS)
            scale = (1.0 + out_w).reshape(1, NH, 1, DH)
            h_norm = h_norm * scale
            return h_norm.transpose(0, 2, 1, 3).reshape(Bq, Sq, Eq)
        return _mlstm_cell(q, k, v, igate_w, igate_b, fgate_w, fgate_b, out_w)

    def _L0_ffn_ref(x, gate_w, w1, b1, w2, b2, sw1, sb1, sw2, sb2):
        import jax, jax.numpy as jnp
        import numpy as np
        D_MODEL = 128
        HIDDEN = 512
        N_ROUTING = 2
        B, S, D = x.shape
        xf = x.reshape(-1, D)
        gate_scores = xf @ gate_w.T
        gate_probs = jax.nn.softmax(gate_scores, axis=-1)
        top1 = jnp.argmax(gate_probs, axis=-1)
        one_hot = jax.nn.one_hot(top1, N_ROUTING, dtype=xf.dtype)
        masked = xf[None, :, :] * one_hot.T[:, :, None]
        h = jax.nn.relu(jnp.einsum('end,edh->enh', masked, w1) + b1[:, None, :])
        expert_out = jnp.einsum('enh,ehd->end', h, w2) + b2[:, None, :]
        routing_output = expert_out.sum(axis=0)
        shared = jax.nn.relu(xf @ sw1 + sb1) @ sw2 + sb2
        return (routing_output + shared).reshape(B, S, D)
    x = x + _L0_attn_ref(_layernorm(x, axis=-1), L0_attn_A, L0_attn_B, L0_attn_W_in, L0_attn_b_in, L0_attn_W_gate, L0_attn_b_gate, L0_attn_W_out, L0_attn_b_out)
    x = x + _L0_xattn_ref(_layernorm(x, axis=-1), ctx_1024, ctx_1024, L0_xattn_igate_w, L0_xattn_igate_b, L0_xattn_fgate_w, L0_xattn_fgate_b, L0_xattn_out_w)
    x = x + _L0_ffn_ref(_layernorm(x, axis=-1), L0_ffn_gate_w, L0_ffn_w1, L0_ffn_b1, L0_ffn_w2, L0_ffn_b2, L0_ffn_sw1, L0_ffn_sb1, L0_ffn_sw2, L0_ffn_sb2)
    return x

_drawn_inputs = setup_inputs


def setup_inputs(seed=0):
    import zlib

    import numpy as np

    out = dict(_drawn_inputs(seed))
    spreads = {'L0_xattn_out_w': (0.0, 0.1)}
    factors = {'L0_attn_b_in': 6.979,
     'L0_attn_b_gate': 8.0,
     'L0_attn_b_out': 4.965,
     'L0_xattn_igate_b': 64.0,
     'L0_xattn_fgate_w': 3.189,
     'L0_ffn_b1': 8.0,
     'L0_ffn_b2': 3.454,
     'L0_ffn_sb1': 8.0,
     'L0_ffn_sb2': 4.691}
    for name, (base, spread) in spreads.items():
        noise = np.random.default_rng([zlib.crc32(name.encode()), seed]).standard_normal(out[name].shape)
        drawn = base * np.exp(spread * noise) if base else spread * noise
        out[name] = jnp.asarray(drawn.astype(out[name].dtype))
    for name, factor in factors.items():
        out[name] = (out[name] * factor).astype(out[name].dtype)
    return out
```

```python
from contextlib import ExitStack

import concourse.bass as bass
from concourse import mybir

ALU = mybir.AluOpType
ACT = mybir.ActivationFunctionType
F32 = mybir.dt.float32
AX_X = mybir.AxisListType.X

P = 128
NB, S, D = 64, 64, 128
NH, DH = 4, 32
NE, HID = 3, 512
NHC = HID // P
NK = NE * NHC
CT = 8
NC = S // CT
TOK = CT * NB
SH = S // 2
GB = TOK // SH
NG = NB * S // TOK
NBG = NB // GB
NTL = TOK // P
BPT = P // SH
LN_EPS, N_EPS = 1e-5, 1e-8
NEG = -1e30
SLOT_OP, SLOT_QT, SLOT_GATES, SLOT_ROWS, SLOT_AT, SLOT_QK, SLOT_PV = 0, 2, 3, 5, 7, 8, 10
STEP_SLOTS = (0, 1, 3, 4, 6, 7, 9, 10)


def decoder_layer(nc, x, ctx_in, w_a, w_b, w_in, b_in, w_gate, b_gate, w_out, b_out,
                  ig_w, ig_b, fg_w, fg_b, out_w, gate_w, w1, b1, w2, b2, sw1, sb1, sw2, sb2, out):
    row_scratch = nc.dram_tensor("row_scratch", (2, BPT, NTL * NH, SH), F32).ap()

    with ExitStack() as stack:
        def sb(name, shape, dt=F32):
            return stack.enter_context(nc.sbuf_tensor(name, shape, dt))

        def psum(name, shape):
            return stack.enter_context(nc.psum_tensor(name, shape, F32))

        def sem(name):
            return stack.enter_context(nc.semaphore(name))

        ps_pre = [psum(f"ps_pre{n}", [P, TOK]) for n in range(2)]
        ps_att = psum("ps_att", [P, 2, 512])
        ps_l1 = [psum(f"ps_l1_{n}", [P, TOK]) for n in range(2)]
        ps_l2 = psum("ps_l2", [P, TOK])
        ps_mix = psum("ps_mix", [P, TOK])

        ident = sb("ident", [P, P])
        causal = sb("causal", [P, S])
        seg_keep = sb("seg_keep", [NTL * NH, BPT, SH + 1])
        seg_drop = sb("seg_drop", [NTL * NH, BPT, SH + 1])
        minus_half = sb("minus_half", [P, 16])
        w_nat = sb("w_nat", [P, 5, P])
        gw_nat = sb("gw_nat", [2 * NH, 3 * D])
        bias_rows = sb("bias_rows", [17, P])
        bias_cols = sb("bias_cols", [P, 17])
        half_neg_bgate = sb("half_neg_bgate", [P, 1])
        b2_sum = sb("b2_sum", [P, 1])
        b2_part = sb("b2_part", [P, 1])
        a_pos = sb("a_pos", [P, P])
        a_neg = sb("a_neg", [P, P])
        b_t = sb("b_t", [P, P])
        w_in_t = sb("w_in_t", [P, P])
        w_gate_t = sb("w_gate_t", [P, P])
        w_out_t = sb("w_out_t", [P, P])
        gw_t = sb("gw_t", [P, 3, 2 * NH])
        gw_kv = sb("gw_kv", [P, 2 * NH])
        b_out_rows = sb("b_out_rows", [P, D])
        gate_bias_rows = sb("gate_bias_rows", [P, 2 * NH])
        ow_rows = sb("ow_rows", [P, D])
        ow1_rows = sb("ow1_rows", [P, D])
        route_rows = sb("route_rows", [P, 2, D])
        route_diff = sb("route_diff", [P, D])
        w1_sb = sb("w1_sb", [P, NE, HID])
        w2_sb = sb("w2_sb", [P, NK, D])
        ctx_nat = sb("ctx_nat", [P, 4, NTL, D])
        ctx_t = sb("ctx_t", [P, NB, S])
        v_mean = sb("v_mean", [P, 4 * NH])
        v_ones = sb("v_ones", [P, NB * S // P, NH, DH + 1])
        x_tb = sb("x_tb", [P, 2, NTL, D])
        bn_tb = sb("bn_tb", [P, NTL, 6])
        mv_tb = sb("mv_tb", [P, NTL, 2])
        var_tb = sb("var_tb", [P, NTL])
        rstd_tb = sb("rstd_tb", [P, NTL])
        xn_t = sb("xn_t", [P, 2, TOK])
        inp = sb("inp", [P, S, NB])
        neg_tg = sb("neg_tg", [P, S, NB])
        w2n = neg_tg
        c2 = sb("c2", [P, S + 1, NB])
        th = sb("th", [P, 2, NB])
        x_g = sb("x_g", [P, 2, NTL, D])
        s_t = sb("s_t", [P, GB, SH])
        x1 = sb("x1", [P, 2, NTL, D])
        bn_g = sb("bn_g", [P, NTL, 6])
        mv_g = sb("mv_g", [P, NTL, 2])
        var_g = sb("var_g", [P, NTL])
        rstd_g = sb("rstd_g", [P, NTL])
        q_nat = sb("q_nat", [P, NTL, D])
        q_t = sb("q_t", [P, GB, SH])
        ctx_g = sb("ctx_g", [P, GB, SH])
        q_heads = sb("q_heads", [P, GB, NH, SH])
        g_f = sb("g_f", [P, NTL, NH])
        g_i = sb("g_i", [P, NTL, NH])
        abs_f = sb("abs_f", [P, NTL, NH])
        exp_f = sb("exp_f", [P, NTL, NH])
        ln_f = sb("ln_f", [P, NTL, NH])
        log_f = sb("log_f", [P, NTL, NH])
        R = NTL * NH
        lf_rows = sb("lf_rows", [R, BPT, SH + 1])
        cs_rows = sb("cs_rows", [R, BPT, SH + 1])
        a_rows = sb("a_rows", [R, 2, BPT, SH + 1])
        m_rows = sb("m_rows", [R, BPT, SH + 1])
        nm_rows = sb("nm_rows", [R, 2, BPT, SH])
        nmc_rows = sb("nmc_rows", [R, 2, BPT, SH])
        cs_carry = sb("cs_carry", [R, NBG, BPT])
        m_carry = sb("m_carry", [R, NBG, BPT])
        a_cols = sb("a_cols", [P, NBG, 2 * R])
        floor_exp = sb("floor_exp", [P, R])
        arg = sb("arg", [P, 2, 2 * R, SH])
        decay = sb("decay", [P, 2 * R, SH])
        c_diag = sb("c_diag", [P, 2 * R, 2, SH])
        norm = sb("norm", [P, 4, R])
        h_n = sb("h_n", [P, R, DH])
        h_var = sb("h_var", [P, R])
        h_ve = sb("h_ve", [P, R])
        h_rstd = sb("h_rstd", [P, R])
        h_y = sb("h_y", [P, R, DH])
        h_o = sb("h_o", [P, NTL, D])
        x2 = sb("x2", [P, 2, NTL, D])
        x3 = sb("x3", [P, NTL, D])
        prod3 = sb("prod3", [P, D])
        route = sb("route", [P, NTL])
        pick = sb("pick", [P, NTL])
        x3_e1 = sb("x3_e1", [P, NTL, D])
        x3_t = sb("x3_t", [P, 2, NE, TOK])
        hid = sb("hid", [P, 3, TOK])
        y_t = sb("y_t", [P, TOK])

        w_loaded, f_loaded = sem("w_loaded"), sem("f_loaded")
        x_tb_loaded = [sem(f"x_tb_loaded{n}") for n in range(2)]
        ctx_loaded = [sem(f"ctx_loaded{n}") for n in range(8)]
        x_g_loaded = [sem(f"x_g_loaded{n}") for n in range(2)]
        consts_ready, pool_zero = sem("consts_ready"), sem("pool_zero")
        rows_b_ready = sem("rows_b_ready")
        setup_t_done, setup_copied, bias_derived = sem("setup_t_done"), sem("setup_copied"), sem("bias_derived")
        p_var, p_rstd, xn_ready = sem("p_var"), sem("p_rstd"), sem("xn_ready")
        xn_t_done, xn_t_ready = sem("xn_t_done"), sem("xn_t_ready")
        inp_done, inp_ready, pgate_done, tg_ready, c2_ready = (
            sem("inp_done"), sem("inp_ready"), sem("pgate_done"), sem("tg_ready"), sem("c2_ready"))
        ctx_t_done, ctx_t_ready, v_ready = sem("ctx_t_done"), sem("ctx_t_ready"), sem("v_ready")
        pre_ready, th_ready, w_ready = sem("pre_ready"), sem("th_ready"), sem("w_ready")
        xb_ready, s_ready, op_done, x1_ready = sem("xb_ready"), sem("s_ready"), sem("op_done"), sem("x1_ready")
        ln1_var, ln1_rstd, q_ready, q_t_done, q_t_ready, q_heads_ready = (
            sem("ln1_var"), sem("ln1_rstd"), sem("q_ready"), sem("q_t_done"), sem("q_t_ready"), sem("q_heads_ready"))
        ctx_g_ready, gates_done, gates_ready, ln_f_ready, log_f_ready, rows_done = (
            sem("ctx_g_ready"), sem("gates_done"), sem("gates_ready"), sem("ln_f_ready"), sem("log_f_ready"), sem("rows_done"))
        nm_ready, scans_ready, a_done, floor_ready, a_cols_ready = (
            sem("nm_ready"), sem("scans_ready"), sem("a_done"), sem("floor_ready"), sem("a_cols_ready"))
        nm_stored, arg_loaded = sem("nm_stored"), sem("arg_loaded")
        arg_ready, arg_m_ready, decay_ready = sem("arg_ready"), sem("arg_m_ready"), sem("decay_ready")
        qk_done, c_ready, pv_done, h_n_ready, h_sq_ready = (
            sem("qk_done"), sem("c_ready"), sem("pv_done"), sem("h_n_ready"), sem("h_sq_ready"))
        h_var_ready, h_rstd_ready, h_y_ready, h_o_ready, x2_ready = (
            sem("h_var_ready"), sem("h_rstd_ready"), sem("h_y_ready"), sem("h_o_ready"), sem("x2_ready"))
        ln2_var, ln2_rstd, x3_ready, x3_e1_ready = sem("ln2_var"), sem("ln2_rstd"), sem("x3_ready"), sem("x3_e1_ready")
        x3_t_done, x3_t_ready, e1_t_done, e1_t_ready, e0_t_ready = (
            sem("x3_t_done"), sem("x3_t_ready"), sem("e1_t_done"), sem("e1_t_ready"), sem("e0_t_ready"))
        l1_done, hid_ready, l2_done, y_t_ready, y_done, o_ready = (
            sem("l1_done"), sem("hid_ready"), sem("l2_done"), sem("y_t_ready"), sem("y_done"), sem("o_ready"))
        stored = sem("stored")
        dve_own, pool_own, act_own = sem("dve_own"), sem("pool_own"), sem("act_own")

        N_W_LOADS, N_F_LOADS, N_ROW_LOADS = 17, 4, 0

        def first_batch(i):
            return GB * (i % NBG)

        def half(i):
            return i // NBG

        block = stack.enter_context(nc.Block())

        @block.sync
        def _(sp):
            def load_chunk(c):
                src = x[:, c * CT:(c + 1) * CT, :].rearrange("b (k t) d -> t b k d", t=2)
                for t in range(2):
                    sp.dma_start(x_tb[64 * t:64 * t + 64, c % 2], src[t]).then_inc(x_tb_loaded[c % 2], 16)

            def load_ctx(q):
                src = ctx_in.rearrange("(n j) t d -> (j t) n d", j=2)
                if q >= 4:
                    sp.wait_ge(v_ready, q - 3)
                    sp.wait_ge(ctx_t_done, q - 3)
                sp.dma_start(ctx_nat[:, q % 4], src[:, 4 * q:4 * q + 4, :]).then_inc(ctx_loaded[q], 16)

            def load_group(i):
                if i >= 2:
                    sp.wait_ge(x1_ready, i - 1)
                b0, s0 = first_batch(i), SH * half(i)
                for r in range(BPT):
                    src = x[b0 + r:b0 + GB:BPT, s0:s0 + SH, :].rearrange("k s d -> s k d")
                    sp.dma_start(x_g[SH * r:SH * r + SH, i % 2], src).then_inc(x_g_loaded[i % 2], 16)

            load_chunk(0)
            for n, w in enumerate((w_a, w_b, w_in, w_gate, w_out)):
                sp.dma_start(w_nat[:, n, :], w).then_inc(w_loaded, 16)
            sp.dma_start(bias_rows[0:4, :], sb1.rearrange("(c p) -> c p", p=P)).then_inc(w_loaded, 16)
            sp.dma_start(bias_rows[4:12, :], b1.rearrange("e (c p) -> (e c) p", p=P)).then_inc(w_loaded, 16)
            sp.dma_start(bias_rows[12:13, :], b_in.unsqueeze(0)).then_inc(w_loaded, 16)
            sp.dma_start(bias_rows[13:14, :], b_gate.unsqueeze(0)).then_inc(w_loaded, 16)
            sp.dma_start(bias_rows[14:16, :], b2).then_inc(w_loaded, 16)
            sp.dma_start(bias_rows[16:17, :], sb2.unsqueeze(0)).then_inc(w_loaded, 16)
            sp.dma_start(gw_nat[0:NH, :], fg_w).then_inc(w_loaded, 16)
            sp.dma_start(gw_nat[NH:2 * NH, :], ig_w).then_inc(w_loaded, 16)
            sp.dma_start(b_out_rows[:], b_out.partition_broadcast(P)).then_inc(w_loaded, 16)
            sp.dma_start(gate_bias_rows[:, 0:NH], fg_b.partition_broadcast(P)).then_inc(w_loaded, 16)
            sp.dma_start(gate_bias_rows[:, NH:], ig_b.partition_broadcast(P)).then_inc(w_loaded, 16)
            sp.dma_start(ow_rows[:], out_w.partition_broadcast(P)).then_inc(w_loaded, 16)
            sp.dma_start(route_rows[:], gate_w.partition_broadcast(P)).then_inc(f_loaded, 16)
            load_chunk(1)
            load_ctx(0)
            load_ctx(1)
            for c in range(2, NC):
                sp.wait_ge(xn_t_done, c - 1)
                load_chunk(c)
                load_ctx(c)
            sp.dma_start(w1_sb[:, 0, :], sw1).then_inc(f_loaded, 16)
            sp.dma_start(w1_sb[:, 1:3, :], w1.rearrange("e d h -> d e h")).then_inc(f_loaded, 16)
            sp.dma_start(w2_sb[:, 0:NHC, :], sw2.rearrange("(c p) d -> p c d", p=P)).then_inc(f_loaded, 16)
            sp.dma_start(w2_sb[:, NHC:, :], w2.rearrange("e (c p) d -> p (e c) d", p=P)).then_inc(f_loaded, 16)
            load_group(0)
            load_group(1)

            for i in range(NG + 1):
                if i < NG:
                    sp.wait_ge(nm_ready, i + 1)
                    sp.dma_start(row_scratch[i % 2].rearrange("b r s -> r b s"), nm_rows[:, i % 2]).then_inc(nm_stored, 16)
                    sp.wait_ge(nm_stored, 16 * (i + 1))
                    if i >= 2:
                        sp.wait_ge(arg_m_ready, i - 1)
                    for j in range(2):
                        src = row_scratch[i % 2, j::2].rearrange("b r s -> b (r s)").partition_broadcast(S)
                        dst = arg[S * j:S * j + S, i % 2].rearrange("p (b r) s -> p b (r s)", b=2)
                        sp.dma_start(dst, src).then_inc(arg_loaded, 16)
                    if i + 2 < NG:
                        load_group(i + 2)
                if i >= 1:
                    g = i - 1
                    sp.wait_ge(o_ready, g + 1)
                    b0, s0 = first_batch(g), SH * half(g)
                    for r in range(BPT):
                        dst = out[b0 + r:b0 + GB:BPT, s0:s0 + SH, :].rearrange("k s d -> s k d")
                        sp.dma_start(dst, x2[SH * r:SH * r + SH, g % 2]).then_inc(stored, 16)
            sp.wait_ge(stored, 16 * BPT * NG)
            sp.wait_ge(nm_stored, 16 * NG)

        @block.gpsimd
        def _(pool):
            own = [0]

            def then(ins):
                own[0] += 1
                ins.then_inc(pool_own, 1)

            def settle():
                pool.wait_ge(pool_own, own[0])

            then(pool.memset(ident[:], 0.0))
            then(pool.memset(causal[:], 0.0))
            then(pool.memset(seg_keep[:], 1.0))
            then(pool.memset(seg_drop[:], 0.0))
            then(pool.memset(minus_half[:], -0.5))
            settle()
            then(pool.affine_select(out=ident[:], in_=ident[:], compare_op=ALU.not_equal, fill=1.0, base=0,
                                    pattern=[[-1, P]], channel_multiplier=1))
            for j in range(2):
                part = causal[S * j:S * j + S, :]
                settle()
                then(pool.affine_select(out=part, in_=part, compare_op=ALU.is_ge, fill=NEG, base=0,
                                        pattern=[[1, S]], channel_multiplier=-1))
            settle()
            then(pool.memset(seg_keep[:, :, 0:1], 0.0))
            then(pool.memset(seg_drop[:, :, 0:1], NEG))
            settle()
            pool.memset(c2[:, 0, :], 0.0).then_inc(consts_ready, 1)
            for t, v in ((q_heads, 0.0), (c_diag, 0.0), (a_cols, 0.0), (cs_carry, 0.0), (m_carry, NEG)):
                pool.memset(t[:], v).then_inc(pool_zero, 1)
            pool.memset(v_ones[:, :, :, DH:DH + 1], 1.0).then_inc(pool_zero, 1)

            def rstd(var_in, ve, dst, seen, n, width, scale, signal):
                pool.wait_ge(seen, n)
                then(pool.tensor_scalar(ve, var_in, scale, LN_EPS, ALU.mult, ALU.add))
                settle()
                pool.tensor_tensor(dst, ve, minus_half[:, 0:width], ALU.pow).then_inc(signal, 1)

            for c in range(NC):
                rstd(mv_tb[:, :, 1], var_tb[:], rstd_tb[:], p_var, c + 1, NTL, 1.0, p_rstd)
            pool.wait_ge(w_loaded, 16 * N_W_LOADS)
            pool.wait_ge(f_loaded, 16)
            then(pool.tensor_scalar(ow1_rows[:], ow_rows[:], 1.0, None, ALU.add))
            pool.wait_ge(f_loaded, 16 * 5)
            then(pool.tensor_tensor(route_diff[:], route_rows[:, 1, :], route_rows[:, 0, :], ALU.subtract))
            settle()
            pool.memset(prod3[:], 0.0).then_inc(rows_b_ready, 1)

            for i in range(NG):
                d = i % 2
                pool.wait_ge(x_g_loaded[d], 16 * BPT * (i // 2 + 1))
                pool.tensor_tensor(x_g[:, d], x_g[:, d], b_out_rows[:].unsqueeze(1).to_broadcast([P, NTL, D]),
                                   ALU.add).then_inc(xb_ready, 1)
                b0, t0 = first_batch(i), SH * half(i)
                pool.wait_ge(w_ready, t0 + SH)
                pool.wait_ge(c2_ready, (t0 + SH) // CT)
                if i >= 1:
                    pool.wait_ge(op_done, i)
                pool.tensor_tensor(s_t[:], c2[:, t0 + 1:t0 + SH + 1, b0:b0 + GB].rearrange("p t b -> p b t"),
                                   w2n[:, t0:t0 + SH, b0:b0 + GB].rearrange("p t b -> p b t"),
                                   ALU.subtract).then_inc(s_ready, 1)
                rstd(mv_g[:, :, 1], var_g[:], rstd_g[:], ln1_var, i + 1, NTL, 1.0, ln1_rstd)
                pool.wait_ge(arg_loaded, 32 * (i + 1))
                if i >= 1:
                    pool.wait_ge(c_ready, i)
                h0 = SH * half(i)
                pool.tensor_tensor(decay[:], arg[:, d], causal[:, h0:h0 + SH].unsqueeze(1).to_broadcast([P, 2 * R, SH]),
                                   ALU.add).then_inc(arg_m_ready, 1)
                rstd(h_var[:], h_ve[:], h_rstd[:], h_var_ready, i + 1, R, 1.0 / DH, h_rstd_ready)
                pool.wait_ge(h_y_ready, i + 1)
                if i >= 1:
                    pool.wait_ge(x2_ready, i)
                pool.tensor_tensor(h_o[:], h_y[:].rearrange("p (k h) d -> p k (h d)", k=NTL),
                                   ow1_rows[:].unsqueeze(1).to_broadcast([P, NTL, D]), ALU.mult).then_inc(h_o_ready, 1)
                rstd(mv_g[:, :, 1], var_g[:], rstd_g[:], ln2_var, i + 1, NTL, 1.0, ln2_rstd)

        @block.scalar
        def _(act):
            own = [0]

            def then(ins):
                own[0] += 1
                ins.then_inc(act_own, 1)

            def settle():
                act.wait_ge(act_own, own[0])

            act.wait_ge(setup_t_done, 1)
            wt = ps_att[:, 0, :].rearrange("p (n e) -> p n e", n=4)
            act.activation(w_in_t[:], wt[:, 2, :], ACT.Copy).then_inc(setup_copied, 1)
            act.activation(w_gate_t[:], wt[:, 3, :], ACT.Copy).then_inc(setup_copied, 1)
            act.activation(bias_cols[:], ps_att[:, 1, P + 24:P + 41], ACT.Copy).then_inc(setup_copied, 1)
            act.wait_ge(setup_copied, 3)
            act.activation(half_neg_bgate[:], bias_cols[:, 13:14], ACT.Copy, scale=-0.5).then_inc(setup_copied, 1)
            act.activation(b2_part[:], bias_cols[:, 14:15], ACT.Identity, bias=bias_cols[:, 15:16]).then_inc(setup_copied, 1)
            act.activation(b_t[:], wt[:, 1, :], ACT.Copy).then_inc(setup_copied, 1)
            act.activation(a_pos[:], wt[:, 0, :], ACT.Copy, scale=0.5).then_inc(setup_copied, 1)
            act.activation(a_neg[:], wt[:, 0, :], ACT.Copy, scale=-0.5).then_inc(setup_copied, 1)
            act.activation(w_out_t[:], ps_att[:, 1, 0:P], ACT.Copy, scale=0.5).then_inc(setup_copied, 1)
            act.activation(gw_t[:], ps_att[:, 1, P:P + 24].rearrange("p (n g) -> p n g", n=3), ACT.Copy).then_inc(setup_copied, 1)
            act.wait_ge(setup_copied, 10)
            act.activation(b2_sum[:], b2_part[:], ACT.Identity, bias=bias_cols[:, 16:17]).then_inc(bias_derived, 1)

            def prep_t(c):
                act.wait_ge(xn_t_done, c + 1)
                if c >= 2:
                    act.wait_ge(inp_done, c - 1)
                act.activation(xn_t[:, c % 2, :], ps_l1[0][:], ACT.Copy).then_inc(xn_t_ready, 1)

            def prep_inp(c):
                act.wait_ge(inp_done, c + 1)
                act.activation(inp[:, c * CT:(c + 1) * CT, :].rearrange("p t b -> p (t b)"), ps_l1[1][:], ACT.Identity,
                               bias=bias_cols[:, 12:13]).then_inc(inp_ready, 1)

            def prep_gate(c):
                act.wait_ge(pgate_done, c + 1)
                act.activation(neg_tg[:, c * CT:(c + 1) * CT, :].rearrange("p t b -> p (t b)"), ps_l2[:], ACT.Tanh,
                               bias=half_neg_bgate[:], scale=-0.5).then_inc(tg_ready, 1)

            def ctx_evac(q):
                act.wait_ge(ctx_t_done, q + 1)
                act.activation(ctx_t[:, 8 * q:8 * q + 8, :].rearrange("p b t -> p (b t)"), ps_mix[:],
                               ACT.Copy).then_inc(ctx_t_ready, 1)

            def step(t):
                act.wait_ge(pre_ready, t + 1)
                col = (t % CT) * NB
                act.activation(th[:, t % 2, :], ps_pre[t // CT % 2][:, col:col + NB], ACT.Tanh).then_inc(th_ready, 1)

            prep_t(0)
            prep_inp(0)
            prep_gate(0)
            for c in range(NC // 2):
                for s in range(CT):
                    step(c * CT + s)
                    n = 2 * c + 1 + s // 4
                    if s % 4 == 0:
                        ctx_evac(2 * c + s // 4)
                    elif n < NC:
                        (prep_t, prep_inp, prep_gate)[s % 4 - 1](n)

            for i in range(NG + 1):
                for k in range(NK):
                    if i >= 1:
                        n = NK * (i - 1) + k
                        act.wait_ge(l1_done, n + 1)
                        if n >= 3:
                            act.wait_ge(l2_done, n - 2)
                        act.activation(hid[:, n % 3, :], ps_l1[k % 2][:], ACT.Relu,
                                       bias=bias_cols[:, k:k + 1]).then_inc(hid_ready, 1)
                    if i < NG // 2 and k in STEP_SLOTS:
                        step((NC // 2 + i) * CT + STEP_SLOTS.index(k))
                    if i == NG:
                        continue
                    if k == SLOT_QT:
                        act.wait_ge(q_t_done, i + 1)
                        act.activation(q_t[:].rearrange("p b s -> p (b s)"), ps_mix[:], ACT.Copy).then_inc(q_t_ready, 1)
                    if k == SLOT_GATES:
                        act.wait_ge(gates_ready, i + 1)
                        then(act.activation(abs_f[:], g_f[:], ACT.Abs))
                        settle()
                        then(act.activation(exp_f[:], abs_f[:], ACT.Exp, scale=-1.0))
                        settle()
                        act.activation(ln_f[:], exp_f[:], ACT.Ln, bias=1.0).then_inc(ln_f_ready, 1)
                    if k == SLOT_AT:
                        act.wait_ge(a_done, i + 1)
                        for j in range(2):
                            r0 = S * j + SH * half(i)
                            act.activation(a_cols[r0:r0 + SH, i % NBG, :], ps_mix[r0:r0 + SH, 256:256 + 2 * R],
                                           ACT.Copy).then_inc(a_cols_ready, 1)
                        act.activation(floor_exp[:], ps_mix[:, 320:320 + R], ACT.Exp).then_inc(floor_ready, 1)
                    if k == SLOT_QK:
                        act.wait_ge(arg_ready, i + 1)
                        act.activation(decay[:], decay[:], ACT.Exp).then_inc(decay_ready, 1)
                    if k == SLOT_PV:
                        act.wait_ge(h_n_ready, i + 1)
                        if i >= 1:
                            act.wait_ge(h_o_ready, i)
                        act.activation(h_y[:], h_n[:], ACT.Square).then_inc(h_sq_ready, 1)
                if i >= 1:
                    act.wait_ge(l2_done, NK * i)
                    if i >= 2:
                        act.wait_ge(y_done, i - 1)
                    act.activation(y_t[:], ps_l2[:], ACT.Identity, bias=b2_sum[:]).then_inc(y_t_ready, 1)
                if i < NG:
                    act.wait_ge(x3_t_done, i + 1)
                    if i >= 2:
                        act.wait_ge(l1_done, NK * (i - 1))
                    act.activation(x3_t[:, i % 2, 0, :], ps_mix[:], ACT.Copy).then_inc(x3_t_ready, 1)
                    act.wait_ge(e1_t_done, i + 1)
                    act.activation(x3_t[:, i % 2, 2, :], ps_mix[:], ACT.Copy).then_inc(e1_t_ready, 1)

        @block.tensor
        def _(pe):
            def transposes(dst, src):
                for k in range(NTL):
                    last = pe.transpose(dst[:, k * P:(k + 1) * P], src[:, k, :], ident[:])
                return last

            pe.wait_ge(consts_ready, 1)
            pe.wait_ge(w_loaded, 16 * N_W_LOADS)
            transposes(ps_att[:, 0, :], w_nat)
            pe.transpose(ps_att[:, 1, 0:P], w_nat[:, 4, :], ident[:])
            for n in range(3):
                pe.transpose(ps_att[:, 1, P + 8 * n:P + 8 * n + 8], gw_nat[:, n * P:(n + 1) * P], ident[0:8, 0:8])
            pe.transpose(ps_att[:, 1, P + 24:P + 41], bias_rows[:], ident[0:17, 0:17]).then_inc(setup_t_done, 1)

            def prep_t(c):
                pe.wait_ge(xn_ready, c + 1)
                if c >= 1:
                    pe.wait_ge(xn_t_ready, c)
                transposes(ps_l1[0], x_tb[:, c % 2]).then_inc(xn_t_done, 1)

            def prep_inp(c):
                pe.wait_ge(xn_t_ready, c + 1)
                if c >= 1:
                    pe.wait_ge(inp_ready, c)
                pe.matmul(ps_l1[1][:], w_in_t[:], xn_t[:, c % 2, :], start=True, stop=True).then_inc(inp_done, 1)

            def prep_gate(c):
                pe.wait_ge(inp_ready, c + 1)
                if c >= 1:
                    pe.wait_ge(tg_ready, c)
                pe.matmul(ps_l2[:], w_gate_t[:], inp[:, c * CT:(c + 1) * CT, :].rearrange("p t b -> p (t b)"),
                          start=True, stop=True).then_inc(pgate_done, 1)

            def ctx_trans(q):
                pe.wait_ge(ctx_loaded[q], 16)
                if q >= 1:
                    pe.wait_ge(ctx_t_ready, q)
                transposes(ps_mix, ctx_nat[:, q % 4]).then_inc(ctx_t_done, 1)

            def chunk_base(c):
                pe.wait_ge(inp_ready, c + 1)
                pe.wait_ge(c2_ready, c + 1)
                if c >= 2:
                    pe.wait_ge(th_ready, CT * (c - 1))
                flat = "p t b -> p (t b)"
                pe.matmul(ps_pre[c % 2][:], b_t[:], inp[:, c * CT:(c + 1) * CT, :].rearrange(flat),
                          start=True, stop=False, skip_group_check=True)
                last = pe.matmul(ps_pre[c % 2][:], a_pos[:], c2[:, c * CT:(c + 1) * CT, :].rearrange(flat),
                                 start=False, stop=False, skip_group_check=True)
                if c == 0:
                    last.then_inc(pre_ready, 1)

            def step(t):
                if t % CT == 0:
                    chunk_base(t // CT)
                if t == 0:
                    return
                pe.wait_ge(w_ready, t)
                col = (t % CT) * NB
                pe.matmul(ps_pre[t // CT % 2][:, col:col + NB], a_neg[:], w2n[:, t - 1, :], start=False, stop=True,
                          skip_group_check=True).then_inc(pre_ready, 1)

            pe.wait_ge(setup_copied, 3)
            prep_t(0)
            prep_inp(0)
            prep_gate(0)
            pe.wait_ge(bias_derived, 1)
            for c in range(NC // 2):
                for s in range(CT):
                    step(c * CT + s)
                    n = 2 * c + 1 + s // 4
                    if s % 4 == 0:
                        ctx_trans(2 * c + s // 4)
                    elif n < NC:
                        (prep_t, prep_inp, prep_gate)[s % 4 - 1](n)

            def l1(i, k):
                n = NK * i + k
                if k == 0:
                    pe.wait_ge(x3_t_ready, i + 1)
                if k == NHC:
                    pe.wait_ge(e0_t_ready, i + 1)
                if n >= 2:
                    pe.wait_ge(hid_ready, n - 1)
                e = k // NHC
                col = (k % NHC) * P
                pe.matmul(ps_l1[k % 2][:], w1_sb[:, e, col:col + P], x3_t[:, i % 2, e, :],
                          start=True, stop=True).then_inc(l1_done, 1)

            def l2(i, k):
                n = NK * i + k
                pe.wait_ge(hid_ready, n + 1)
                if k == 0 and i >= 1:
                    pe.wait_ge(y_t_ready, i)
                pe.matmul(ps_l2[:], w2_sb[:, k, :], hid[:, n % 3, :], start=(k == 0), stop=(k == NK - 1)).then_inc(l2_done, 1)

            pe.wait_ge(f_loaded, 16 * 5)
            for i in range(NG + 1):
                b0, h0 = first_batch(i), SH * half(i)
                for k in range(NK):
                    if i >= 1:
                        l1(i - 1, k)
                        if k >= 1:
                            l2(i - 1, k - 1)
                    if i < NG // 2 and k in STEP_SLOTS:
                        step((NC // 2 + i) * CT + STEP_SLOTS.index(k))
                    if i == NG:
                        continue
                    if k == SLOT_OP:
                        pe.wait_ge(s_ready, i + 1)
                        if i == 0:
                            pe.wait_ge(ctx_t_ready, 8)
                        else:
                            pe.wait_ge(e1_t_ready, i)
                        for n in range(NTL):
                            last = pe.matmul(ps_mix[:, n * P:(n + 1) * P],
                                             s_t[:, BPT * n:BPT * (n + 1), :].rearrange("p b s -> p (b s)"),
                                             w_out_t[:], start=True, stop=True)
                        last.then_inc(op_done, 1)
                    if k == SLOT_QT:
                        pe.wait_ge(x1_ready, i + 1)
                        pe.wait_ge(q_ready, i + 1)
                        transposes(ps_mix, q_nat).then_inc(q_t_done, 1)
                    if k == SLOT_GATES:
                        pe.wait_ge(q_t_ready, i + 1)
                        pe.wait_ge(ctx_g_ready, i + 1)
                        for n in range(NTL):
                            dst = ps_mix[:, 8 * n:8 * n + 8]
                            pe.matmul(dst, q_t[:, BPT * n:BPT * (n + 1), :].rearrange("p b s -> p (b s)"), gw_t[:, 0, :],
                                      start=True, stop=False)
                            last = pe.matmul(dst, ctx_g[:, BPT * n:BPT * (n + 1), :].rearrange("p b s -> p (b s)"), gw_kv[:],
                                             start=False, stop=True)
                        last.then_inc(gates_done, 1)
                    if k == SLOT_ROWS:
                        pe.wait_ge(log_f_ready, i + 1)
                        pe.transpose(ps_mix[0:R, 0:P], log_f[:].rearrange("p k h -> p (k h)"), ident[:])
                        pe.transpose(ps_mix[0:R, P:2 * P], g_i[:].rearrange("p k h -> p (k h)"), ident[:]).then_inc(rows_done, 1)
                    if k == SLOT_AT:
                        pe.wait_ge(scans_ready, i + 1)
                        for b in range(BPT):
                            r0 = S * (b % 2) + h0
                            pe.matmul(ps_mix[r0:r0 + SH, 256 + R * (b // 2):256 + R * (b // 2 + 1)],
                                      a_rows[:, i % 2, b, 1:SH + 1], ident[0:R, 0:R], start=True, stop=True)
                        pe.transpose(ps_mix[:, 320:320 + R], nmc_rows[:, i % 2].rearrange("r b s -> r (b s)"),
                                     ident[0:R, 0:R]).then_inc(a_done, 1)
                    if k == SLOT_QK:
                        pe.wait_ge(q_heads_ready, i + 1)
                        if i >= 1:
                            pe.wait_ge(h_n_ready, i)
                        for b in range(GB):
                            n, r = b // BPT, b % BPT
                            j = r % 2
                            last = pe.matmul(ps_att[S * j:S * j + S, r // 2, n * P:(n + 1) * P], ctx_t[:, b0 + b, :],
                                             q_heads[:, b].rearrange("p h s -> p (h s)"), start=True, stop=True)
                        last.then_inc(qk_done, 1)
                    if k == SLOT_PV:
                        pe.wait_ge(c_ready, i + 1)
                        if i == 0:
                            pe.wait_ge(v_ready, 8)
                        for n in range(NTL):
                            for h in range(NH):
                                for b in range(2):
                                    col = ((n % 2) * NH + h) * (DH + 1)
                                    last = pe.matmul(ps_att[S * b:S * b + S, n // 2, col:col + DH + 1],
                                                     c_diag[:, R * b + NH * n + h].rearrange("p j s -> p (j s)"),
                                                     v_ones[:, b0 // 2 + 2 * n + b, h, :], start=True, stop=True)
                        last.then_inc(pv_done, 1)
                if i >= 1:
                    l2(i - 1, NK - 1)
                    pe.wait_ge(y_t_ready, i)
                    if i < NG:
                        pe.wait_ge(floor_ready, i + 1)
                    else:
                        pe.wait_ge(e1_t_ready, NG)
                    transposes(ps_mix, y_t[:].rearrange("p (k m) -> p k m", k=NTL)).then_inc(y_done, 1)
                if i < NG:
                    pe.wait_ge(x3_ready, i + 1)
                    if i >= 1:
                        pe.wait_ge(o_ready, i)
                    else:
                        pe.wait_ge(floor_ready, 1)
                    transposes(ps_mix, x3).then_inc(x3_t_done, 1)
                    pe.wait_ge(x3_e1_ready, i + 1)
                    pe.wait_ge(x3_t_ready, i + 1)
                    transposes(ps_mix, x3_e1).then_inc(e1_t_done, 1)

        @block.vector
        def _(dve):
            own = [0]

            def then(ins):
                own[0] += 1
                ins.then_inc(dve_own, 1)

            def settle():
                dve.wait_ge(dve_own, own[0])

            def statistics(src, bn, mv, signal):
                for k in range(NTL):
                    then(dve.bn_stats(bn[:, k, :], src[:, k, :]))
                settle()
                for k in range(NTL):
                    last = dve.bn_aggr(mv[:, k, :], bn[:, k, :])
                last.then_inc(signal, 1)

            def normalise(dst, src, mv, rs, signal):
                for k in range(NTL):
                    last = dve.tensor_scalar(dst[:, k, :], src[:, k, :], mv[:, k, 0:1], rs[:, k:k + 1],
                                             ALU.subtract, ALU.mult)
                last.then_inc(signal, 1)

            def prep_stats(c):
                dve.wait_ge(x_tb_loaded[c % 2], 32 * (c // 2 + 1))
                if c >= 1:
                    dve.wait_ge(xn_ready, c)
                statistics(x_tb[:, c % 2], bn_tb, mv_tb, p_var)

            def prep_norm(c):
                dve.wait_ge(p_rstd, c + 1)
                dve.wait_ge(p_var, c + 1)
                normalise(x_tb[:, c % 2], x_tb[:, c % 2], mv_tb, rstd_tb, xn_ready)

            def prep_c2(c):
                dve.wait_ge(tg_ready, c + 1)
                dve.wait_ge(inp_ready, c + 1)
                flat = "p t b -> p (t b)"
                dve.scalar_tensor_tensor(c2[:, c * CT + 1:(c + 1) * CT + 1, :].rearrange(flat),
                                         neg_tg[:, c * CT:(c + 1) * CT, :].rearrange(flat), 1.0,
                                         inp[:, c * CT:(c + 1) * CT, :].rearrange(flat), ALU.add, ALU.mult).then_inc(c2_ready, 1)

            def values(q, part):
                src = ctx_nat[:, q % 4].rearrange("p n (h d) -> p (n h) d", h=NH)
                if part == 0:
                    dve.wait_ge(ctx_loaded[q], 16)
                    then(dve.reduce_sum(v_mean[:], src, AX_X))
                    settle()
                else:
                    if q == 0:
                        dve.wait_ge(pool_zero, 6)
                    dst = v_ones[:, 4 * q:4 * q + 4, :, 0:DH].rearrange("p n h d -> p (n h) d")
                    dve.scalar_tensor_tensor(dst, v_mean[:].unsqueeze(2).to_broadcast([P, 16, DH]), -1.0 / DH, src,
                                             ALU.mult, ALU.add).then_inc(v_ready, 1)
                    dve.wait_ge(v_ready, q + 1)

            def step(t):
                dve.wait_ge(th_ready, t + 1)
                dve.scalar_tensor_tensor(w2n[:, t, :], neg_tg[:, t, :], 1.0, th[:, t % 2, :],
                                         ALU.subtract, ALU.mult).then_inc(w_ready, 1)

            prep_stats(0)
            prep_norm(0)
            prep_c2(0)
            dve.wait_ge(setup_copied, 10)
            then(dve.tensor_tensor(gw_kv[:], gw_t[:, 1, :], gw_t[:, 2, :], ALU.add))
            prep_stats(1)
            prep_norm(1)
            for c in range(NC // 2):
                for s in range(CT):
                    step(c * CT + s)
                    n = 2 * c + 1 + s // 4
                    if s % 4 == 0:
                        values(2 * c + s // 4, 0)
                    if s % 4 == 1:
                        values(2 * c + s // 4, 1)
                    if n + 1 < NC and s % 4 == 2:
                        prep_stats(n + 1)
                    if s % 4 == 3:
                        if n < NC:
                            prep_c2(n)
                        if n + 1 < NC:
                            prep_norm(n + 1)

            for i in range(NG + 1):
                d = i % 2
                b0, h0 = first_batch(i), SH * half(i)
                for k in range(NK):
                    if i < NG // 2 and k in STEP_SLOTS:
                        step((NC // 2 + i) * CT + STEP_SLOTS.index(k))
                    if i == NG:
                        continue
                    if k == SLOT_OP:
                        if i == 0:
                            dve.wait_ge(ctx_t_ready, 8)
                        else:
                            dve.wait_ge(gates_done, i)
                        dve.tensor_copy(ctx_g[:], ctx_t[:, b0:b0 + GB, h0:h0 + SH]).then_inc(ctx_g_ready, 1)
                        dve.wait_ge(op_done, i + 1)
                        dve.wait_ge(xb_ready, i + 1)
                        dve.tensor_tensor(x1[:, d], ps_mix[:].rearrange("p (k m) -> p k m", k=NTL), x_g[:, d],
                                          ALU.add).then_inc(x1_ready, 1)
                        dve.wait_ge(x1_ready, i + 1)
                        if i >= 1:
                            dve.wait_ge(ln2_rstd, i)
                        statistics(x1[:, d], bn_g, mv_g, ln1_var)
                    if k == SLOT_OP + 1:
                        dve.wait_ge(ln1_rstd, i + 1)
                        dve.wait_ge(ln1_var, i + 1)
                        if i >= 1:
                            dve.wait_ge(q_t_done, i)
                        normalise(q_nat, x1[:, d], mv_g, rstd_g, q_ready)
                    if k == SLOT_QT:
                        dve.wait_ge(q_t_ready, i + 1)
                        if i == 0:
                            dve.wait_ge(pool_zero, 6)
                        else:
                            dve.wait_ge(qk_done, i)
                        for h in range(NH):
                            r = slice(DH * h, DH * h + DH)
                            last = dve.tensor_copy(q_heads[r, :, h, :], q_t[r])
                        last.then_inc(q_heads_ready, 1)
                    if k == SLOT_GATES:
                        dve.wait_ge(gates_done, i + 1)
                        if i >= 1:
                            dve.wait_ge(rows_done, i)
                        pre = ps_mix[:, 0:8 * NTL].rearrange("p (k g) -> p k g", g=8)
                        then(dve.tensor_tensor(g_i[:], pre[:, :, NH:], gate_bias_rows[:, NH:].unsqueeze(1).to_broadcast([P, NTL, NH]), ALU.add))
                        dve.tensor_tensor(g_f[:], pre[:, :, 0:NH], gate_bias_rows[:, 0:NH].unsqueeze(1).to_broadcast([P, NTL, NH]),
                                          ALU.add).then_inc(gates_ready, 1)
                    if k == SLOT_GATES + 1:
                        dve.wait_ge(ln_f_ready, i + 1)
                        dve.wait_ge(gates_ready, i + 1)
                        settle()
                        dve.scalar_tensor_tensor(log_f[:].rearrange("p k h -> p (k h)"), g_f[:].rearrange("p k h -> p (k h)"), 0.0,
                                                 ln_f[:].rearrange("p k h -> p (k h)"), ALU.min, ALU.subtract).then_inc(log_f_ready, 1)
                    if k == SLOT_ROWS:
                        dve.wait_ge(rows_done, i + 1)
                        if i >= 2:
                            dve.wait_ge(a_done, i - 1)
                            dve.wait_ge(nm_stored, 16 * (i - 1))
                        if i == 0:
                            dve.wait_ge(pool_zero, 6)
                        g = i % NBG
                        lf_ps = ps_mix[0:R, 0:P].rearrange("r (b s) -> r b s", b=BPT)
                        ig_ps = ps_mix[0:R, P:2 * P].rearrange("r (b s) -> r b s", b=BPT)
                        settle()
                        then(dve.tensor_copy(lf_rows[:, :, 0:1], cs_carry[:, g].unsqueeze(2)))
                        then(dve.tensor_copy(lf_rows[:, :, 1:], lf_ps))
                        then(dve.tensor_copy(a_rows[:, d, :, 0:1], m_carry[:, g].unsqueeze(2)))
                        settle()
                        flat = "r b s -> r (b s)"
                        then(dve.tensor_tensor_scan(cs_rows[:].rearrange(flat), seg_keep[:].rearrange(flat), lf_rows[:].rearrange(flat),
                                                    0.0, ALU.mult, ALU.add))
                        settle()
                        then(dve.tensor_tensor(a_rows[:, d, :, 1:], ig_ps, cs_rows[:, :, 0:SH], ALU.subtract))
                        settle()
                        then(dve.tensor_tensor_scan(m_rows[:].rearrange(flat), seg_drop[:].rearrange(flat), a_rows[:, d].rearrange(flat),
                                                    0.0, ALU.add, ALU.max))
                        settle()
                        dve.tensor_scalar(nm_rows[:, d], m_rows[:, :, 1:], -1.0, None, ALU.mult).then_inc(nm_ready, 1)
                        dve.wait_ge(nm_ready, i + 1)
                        then(dve.tensor_copy(cs_carry[:, g].unsqueeze(2), cs_rows[:, :, SH:]))
                        then(dve.tensor_copy(m_carry[:, g].unsqueeze(2), m_rows[:, :, SH:]))
                        dve.tensor_tensor(nmc_rows[:, d], nm_rows[:, d], cs_rows[:, :, 1:], ALU.subtract).then_inc(scans_ready, 1)
                    if k == SLOT_AT:
                        dve.wait_ge(a_cols_ready, 2 * (i + 1))
                        dve.wait_ge(arg_m_ready, i + 1)
                        dve.tensor_tensor(decay[:], decay[:], a_cols[:, i % NBG].unsqueeze(2).to_broadcast([P, 2 * R, SH]),
                                          ALU.add).then_inc(arg_ready, 1)
                    if k == SLOT_QK + 1:
                        dve.wait_ge(qk_done, i + 1)
                        dve.wait_ge(decay_ready, i + 1)
                        if i >= 1:
                            dve.wait_ge(pv_done, i)
                        for j in range(2):
                            r = slice(S * j, S * j + S)
                            last = dve.scalar_tensor_tensor(c_diag[r, :, j, :], ps_att[r].rearrange("p a (c s) -> p (a c) s", s=SH),
                                                            DH ** -0.5, decay[r], ALU.mult, ALU.mult)
                        last.then_inc(c_ready, 1)
                    if k == SLOT_PV:
                        dve.wait_ge(pv_done, i + 1)
                        dve.wait_ge(floor_ready, i + 1)
                        if i >= 1:
                            dve.wait_ge(h_sq_ready, i)
                        hp = ps_att[:, :, 0:2 * NH * (DH + 1)].rearrange("p a (g c) -> p a g c", c=DH + 1)
                        total = hp[:, :, :, DH]
                        two = "p (a g) -> p a g"
                        nv = [norm[:, n].rearrange(two, a=2) for n in range(4)]
                        settle()
                        then(dve.tensor_tensor(nv[0], total, floor_exp[:].rearrange(two, a=2), ALU.max))
                        settle()
                        then(dve.scalar_tensor_tensor(nv[1], total, -1.0, nv[0], ALU.mult, ALU.max))
                        settle()
                        then(dve.tensor_scalar(norm[:, 2], norm[:, 1], N_EPS, None, ALU.add))
                        settle()
                        then(dve.reciprocal(norm[:, 3], norm[:, 2]))
                        settle()
                        dve.tensor_tensor(h_n[:].rearrange("p (a g) d -> p a g d", a=2), hp[:, :, :, 0:DH],
                                          nv[3].unsqueeze(3).to_broadcast([P, 2, 2 * NH, DH]), ALU.mult).then_inc(h_n_ready, 1)
                        dve.wait_ge(h_sq_ready, i + 1)
                        dve.reduce_sum(h_var[:], h_y[:], AX_X).then_inc(h_var_ready, 1)
                if i < NG:
                    dve.wait_ge(h_rstd_ready, i + 1)
                    dve.wait_ge(h_var_ready, i + 1)
                    dve.tensor_tensor(h_y[:], h_n[:], h_rstd[:].unsqueeze(2).to_broadcast([P, R, DH]), ALU.mult).then_inc(h_y_ready, 1)
                    dve.wait_ge(h_o_ready, i + 1)
                    if i >= 2:
                        dve.wait_ge(stored, 16 * BPT * (i - 1))
                    dve.tensor_tensor(x2[:, d], x1[:, d], h_o[:], ALU.add).then_inc(x2_ready, 1)
                    dve.wait_ge(x2_ready, i + 1)
                    statistics(x2[:, d], bn_g, mv_g, ln2_var)
                if i >= 1:
                    dve.wait_ge(y_done, i)
                    dve.tensor_tensor(x2[:, 1 - d], ps_mix[:].rearrange("p (k m) -> p k m", k=NTL), x2[:, 1 - d],
                                      ALU.add).then_inc(o_ready, 1)
                if i < NG:
                    dve.wait_ge(ln2_rstd, i + 1)
                    dve.wait_ge(ln2_var, i + 1)
                    if i >= 1:
                        dve.wait_ge(x3_t_done, i)
                        dve.wait_ge(e1_t_done, i)
                    normalise(x3, x2[:, d], mv_g, rstd_g, x3_ready)
                    dve.wait_ge(x3_ready, i + 1)
                    if i == 0:
                        dve.wait_ge(rows_b_ready, 1)
                    for k in range(NTL):
                        then(dve.tensor_tensor_reduce(prod3[:], x3[:, k, :], route_diff[:], 1.0, 0.0, ALU.mult, ALU.add,
                                                      route[:, k:k + 1]))
                        settle()
                    then(dve.tensor_scalar(pick[:], route[:], 0.0, None, ALU.is_gt))
                    settle()
                    dve.tensor_tensor(x3_e1[:], x3[:], pick[:].unsqueeze(2).to_broadcast([P, NTL, D]), ALU.mult).then_inc(x3_e1_ready, 1)
                    dve.wait_ge(e1_t_ready, i + 1)
                    dve.wait_ge(x3_t_ready, i + 1)
                    dve.tensor_tensor(x3_t[:, d, 1, :], x3_t[:, d, 0, :], x3_t[:, d, 2, :], ALU.subtract).then_inc(e0_t_ready, 1)


_INS = ['x', 'ctx_1024', 'L0_attn_A', 'L0_attn_B', 'L0_attn_W_in', 'L0_attn_b_in', 'L0_attn_W_gate', 'L0_attn_b_gate',
        'L0_attn_W_out', 'L0_attn_b_out', 'L0_xattn_igate_w', 'L0_xattn_igate_b', 'L0_xattn_fgate_w', 'L0_xattn_fgate_b',
        'L0_xattn_out_w', 'L0_ffn_gate_w', 'L0_ffn_w1', 'L0_ffn_b1', 'L0_ffn_w2', 'L0_ffn_b2', 'L0_ffn_sw1', 'L0_ffn_sb1',
        'L0_ffn_sw2', 'L0_ffn_sb2']


def kernel(**inputs):
    import numpy as np
    import concourse.bacc as bacc
    from concourse.bass_utils import run_bass_kernel_spmd

    nc = bacc.Bacc("TRN2", target_bir_lowering=False, num_devices=1)
    arrays, args = {}, []
    for name in _INS:
        a = np.ascontiguousarray(inputs[name])
        arrays[f"in_{name}"] = a
        args.append(nc.dram_tensor(f"in_{name}", a.shape, mybir.dt.from_np(a.dtype), kind="ExternalInput").ap())
    out = nc.dram_tensor("out_x", (NB, S, D), F32, kind="ExternalOutput").ap()
    decoder_layer(nc, *args, out)
    r = run_bass_kernel_spmd(nc, [arrays], core_ids=[0])
    return r.results[0]["out_x"]
```

```python
from contextlib import ExitStack

import concourse.bass as bass
from concourse import mybir

ALU = mybir.AluOpType
ACT = mybir.ActivationFunctionType
F32 = mybir.dt.float32
AX_X = mybir.AxisListType.X

P = 128
NB, S, D = 64, 64, 128
NH, DH = 4, 32
NE, HID = 3, 512
NHC = HID // P
NK = NE * NHC
CT = 8
NC = S // CT
TOK = CT * NB
SH = S // 2
GB = TOK // SH
NG = NB * S // TOK
NBG = NB // GB
NTL = TOK // P
BPT = P // SH
LN_EPS, N_EPS = 1e-5, 1e-8
NEG = -1e30
OP, QT, GATES, ROWS, ACOL, QK, PV, X3T, E1T, FFN, YT = 0, 3, 4, 7, 9, 11, 14, 22, 23, 24, 37
NIT = NG + (YT + 1 + NK - 1) // NK - 1
STEP_SLOTS = (0, 1, 3, 4, 6, 7, 9, 10)
BASE_SLOTS = (7, 8)
NP1 = NC // 2
PREP_AT = {(0, 0): 5, (0, 6): 6, (1, 0): 7}
CTX_AT = {(0, 1): 4, (0, 7): 5, (1, 1): 6, (1, 7): 7}
STATS_AT = {(0, 2): 6, (0, 8): 7}


def decoder_layer(nc, x, ctx_in, w_a, w_b, w_in, b_in, w_gate, b_gate, w_out, b_out,
                  ig_w, ig_b, fg_w, fg_b, out_w, gate_w, w1, b1, w2, b2, sw1, sb1, sw2, sb2, out):
    row_scratch = nc.dram_tensor("row_scratch", (2, BPT, NTL * NH, SH), F32).ap()

    with ExitStack() as stack:
        def sb(name, shape, dt=F32):
            return stack.enter_context(nc.sbuf_tensor(name, shape, dt))

        def psum(name, shape):
            return stack.enter_context(nc.psum_tensor(name, shape, F32))

        def sem(name):
            return stack.enter_context(nc.semaphore(name))

        ps_pre = [psum(f"ps_pre{n}", [P, TOK]) for n in range(2)]
        ps_att = psum("ps_att", [P, 2, 512])
        ps_l1 = [psum(f"ps_l1_{n}", [P, TOK]) for n in range(2)]
        ps_l2 = psum("ps_l2", [P, TOK])
        ps_mix = psum("ps_mix", [P, TOK])

        ident = sb("ident", [P, P])
        causal = sb("causal", [P, S])
        seg_keep = sb("seg_keep", [NTL * NH, BPT, SH + 1])
        seg_drop = sb("seg_drop", [NTL * NH, BPT, SH + 1])
        minus_half = sb("minus_half", [P, 16])
        w_nat = sb("w_nat", [P, 5, P])
        io_rows = sb("io_rows", [2, P])
        io_cols = sb("io_cols", [P, 2])
        gw_nat = sb("gw_nat", [2 * NH, 3 * D])
        bias_rows = sb("bias_rows", [15, P])
        bias_cols = sb("bias_cols", [P, 15])
        half_neg_bgate = sb("half_neg_bgate", [P, 1])
        b2_sum = sb("b2_sum", [P, 1])
        b2_part = sb("b2_part", [P, 1])
        a_pos = sb("a_pos", [P, P])
        a_neg = sb("a_neg", [P, P])
        b_t = sb("b_t", [P, P])
        w_in_t = sb("w_in_t", [P, P])
        w_gate_t = sb("w_gate_t", [P, P])
        w_out_t = sb("w_out_t", [P, P])
        gw_t = sb("gw_t", [P, 3, 2 * NH])
        gw_kv = sb("gw_kv", [P, 2 * NH])
        b_out_rows = sb("b_out_rows", [P, D])
        gate_bias_rows = sb("gate_bias_rows", [P, 2 * NH])
        ow_rows = sb("ow_rows", [P, D])
        ow1_rows = sb("ow1_rows", [P, D])
        route_rows = sb("route_rows", [P, 2, D])
        route_diff = sb("route_diff", [P, D])
        w1_sb = sb("w1_sb", [P, NE, HID])
        w2_sb = sb("w2_sb", [P, NK, D])
        ctx_nat = sb("ctx_nat", [P, 4, NTL, D])
        ctx_t = sb("ctx_t", [P, NB, S])
        v_sum = sb("v_sum", [P, 8, NTL * NH])
        v_mean = sb("v_mean", [P, 8, NTL * NH])
        v_ones = sb("v_ones", [P, NB * S // P, NH, DH + 1])
        x_tb = sb("x_tb", [P, 2, NTL, D])
        bn_tb = sb("bn_tb", [P, NTL, 6])
        mv_tb = sb("mv_tb", [P, NTL, 2])
        var_tb = sb("var_tb", [P, NTL])
        rstd_tb = sb("rstd_tb", [P, NTL])
        xn_t = sb("xn_t", [P, 2, TOK])
        inp = sb("inp", [P, S, NB])
        neg_tg = sb("neg_tg", [P, S, NB])
        w2n = neg_tg
        c2 = sb("c2", [P, S + 1, NB])
        th = sb("th", [P, 2, NB])
        x_g = sb("x_g", [P, 2, NTL, D])
        s_t = sb("s_t", [P, GB, SH])
        x1 = sb("x1", [P, 2, NTL, D])
        bn_g = sb("bn_g", [P, NTL, 6])
        mv_g = sb("mv_g", [P, NTL, 2])
        var_g = sb("var_g", [P, NTL])
        rstd_g = sb("rstd_g", [P, NTL])
        q_nat = sb("q_nat", [P, NTL, D])
        q_t = sb("q_t", [P, GB, SH])
        ctx_g = sb("ctx_g", [P, GB, SH])
        q_heads = sb("q_heads", [P, GB, NH, SH])
        g_f = sb("g_f", [P, NTL, NH])
        g_i = sb("g_i", [P, NTL, NH])
        abs_f = sb("abs_f", [P, NTL, NH])
        exp_f = sb("exp_f", [P, NTL, NH])
        ln_f = sb("ln_f", [P, NTL, NH])
        log_f = sb("log_f", [P, NTL, NH])
        R = NTL * NH
        lf_rows = sb("lf_rows", [R, BPT, SH + 1])
        cs_rows = sb("cs_rows", [R, BPT, SH + 1])
        a_rows = sb("a_rows", [R, 2, BPT, SH + 1])
        m_rows = sb("m_rows", [R, BPT, SH + 1])
        nm_rows = sb("nm_rows", [R, 2, BPT, SH])
        nmc_rows = sb("nmc_rows", [R, 2, BPT, SH])
        cs_carry = sb("cs_carry", [R, NBG, BPT])
        m_carry = sb("m_carry", [R, NBG, BPT])
        a_cols = sb("a_cols", [P, NBG, 2 * R])
        floor_exp = sb("floor_exp", [P, R])
        arg = sb("arg", [P, 2, 2 * R, SH])
        decay = sb("decay", [P, 2 * R, SH])
        c_diag = sb("c_diag", [P, 2 * R, 2, SH])
        norm = sb("norm", [P, 4, R])
        h_n = sb("h_n", [P, R, DH])
        h_var = sb("h_var", [P, R])
        h_ve = sb("h_ve", [P, R])
        h_rstd = sb("h_rstd", [P, R])
        h_y = sb("h_y", [P, R, DH])
        h_o = sb("h_o", [P, NTL, D])
        x2 = sb("x2", [P, 2, NTL, D])
        x3 = sb("x3", [P, NTL, D])
        route = sb("route", [P, NTL])
        pick = sb("pick", [P, NTL])
        x3_e1 = sb("x3_e1", [P, NTL, D])
        x3_t = sb("x3_t", [P, NE, TOK])
        hid = sb("hid", [P, 3, TOK])
        y_t = sb("y_t", [P, TOK])

        io_loaded, ab_loaded, w_loaded, f_loaded = sem("io_loaded"), sem("ab_loaded"), sem("w_loaded"), sem("f_loaded")
        x_tb_loaded = [sem(f"x_tb_loaded{n}") for n in range(2)]
        ctx_loaded = [sem(f"ctx_loaded{n}") for n in range(8)]
        x_g_loaded = [sem(f"x_g_loaded{n}") for n in range(2)]
        consts_ready, pool_zero, rows_b_ready = sem("consts_ready"), sem("pool_zero"), sem("rows_b_ready")
        io_turned, io_copied, ab_turned, ab_copied = sem("io_turned"), sem("io_copied"), sem("ab_turned"), sem("ab_copied")
        rest_turned, rest_copied, b2_ready, gw_kv_ready = (
            sem("rest_turned"), sem("rest_copied"), sem("b2_ready"), sem("gw_kv_ready"))
        p_var, p_rstd, xn_ready, xn_t_done, xn_t_ready = (
            sem("p_var"), sem("p_rstd"), sem("xn_ready"), sem("xn_t_done"), sem("xn_t_ready"))
        inp_done, inp_ready, pgate_done, tg_ready, c2_ready = (
            sem("inp_done"), sem("inp_ready"), sem("pgate_done"), sem("tg_ready"), sem("c2_ready"))
        ctx_t_done, ctx_t_ready, v_mean_ready, v_ready = (
            sem("ctx_t_done"), sem("ctx_t_ready"), sem("v_mean_ready"), sem("v_ready"))
        pre_ready, th_ready, w_ready = sem("pre_ready"), sem("th_ready"), sem("w_ready")
        xb_ready, s_ready, op_done, x1_ready = sem("xb_ready"), sem("s_ready"), sem("op_done"), sem("x1_ready")
        ln1_var, ln1_rstd, q_ready, q_t_done, q_t_ready, q_heads_ready = (
            sem("ln1_var"), sem("ln1_rstd"), sem("q_ready"), sem("q_t_done"), sem("q_t_ready"), sem("q_heads_ready"))
        ctx_g_ready, gates_done, gates_ready, ln_f_ready, log_f_ready, rows_done = (
            sem("ctx_g_ready"), sem("gates_done"), sem("gates_ready"), sem("ln_f_ready"), sem("log_f_ready"), sem("rows_done"))
        nm_ready, scans_ready, a_done, floor_ready, a_cols_ready = (
            sem("nm_ready"), sem("scans_ready"), sem("a_done"), sem("floor_ready"), sem("a_cols_ready"))
        nm_stored, arg_loaded = sem("nm_stored"), sem("arg_loaded")
        arg_m_ready, arg_ready, decay_ready = sem("arg_m_ready"), sem("arg_ready"), sem("decay_ready")
        qk_done, c_ready, pv_done, h_n_ready, h_sq_ready = (
            sem("qk_done"), sem("c_ready"), sem("pv_done"), sem("h_n_ready"), sem("h_sq_ready"))
        h_var_ready, h_rstd_ready, h_y_ready, h_o_ready, x2_ready = (
            sem("h_var_ready"), sem("h_rstd_ready"), sem("h_y_ready"), sem("h_o_ready"), sem("x2_ready"))
        ln2_var, ln2_rstd, x3_ready, x3_e1_ready = sem("ln2_var"), sem("ln2_rstd"), sem("x3_ready"), sem("x3_e1_ready")
        x3_t_done, x3_t_ready, e1_t_done, e1_t_ready, e0_t_ready = (
            sem("x3_t_done"), sem("x3_t_ready"), sem("e1_t_done"), sem("e1_t_ready"), sem("e0_t_ready"))
        l1_done, hid_ready, l2_done, y_t_ready, y_done, o_ready = (
            sem("l1_done"), sem("hid_ready"), sem("l2_done"), sem("y_t_ready"), sem("y_done"), sem("o_ready"))
        stored = sem("stored")
        dve_own, pool_own, act_own = sem("dve_own"), sem("pool_own"), sem("act_own")

        def first_batch(i):
            return GB * (i % NBG)

        def half(i):
            return i // NBG

        def group_at(i, k, pos):
            g = i - pos // NK
            return g if k == pos % NK and 0 <= g < NG else None

        def step_at(i, k):
            return (NP1 + i) * CT + STEP_SLOTS.index(k) if i < NC - NP1 and k in STEP_SLOTS else None

        block = stack.enter_context(nc.Block())

        @block.sync
        def _(sp):
            def load_chunk(c):
                if c >= 2:
                    sp.wait_ge(xn_t_done, c - 1)
                src = x[:, c * CT:(c + 1) * CT, :].rearrange("b (k t) d -> t b k d", t=2)
                for t in range(2):
                    sp.dma_start(x_tb[64 * t:64 * t + 64, c % 2], src[t]).then_inc(x_tb_loaded[c % 2], 16)

            def load_ctx(q):
                if q >= 4:
                    sp.wait_ge(v_ready, q - 3)
                    sp.wait_ge(ctx_t_done, q - 3)
                src = ctx_in.rearrange("(n j) t d -> (j t) n d", j=2)
                sp.dma_start(ctx_nat[:, q % 4], src[:, 4 * q:4 * q + 4, :]).then_inc(ctx_loaded[q], 16)

            def load_group(i):
                if i >= 2:
                    sp.wait_ge(x1_ready, i - 1)
                b0, s0 = first_batch(i), SH * half(i)
                for r in range(BPT):
                    src = x[b0 + r:b0 + GB:BPT, s0:s0 + SH, :].rearrange("k s d -> s k d")
                    sp.dma_start(x_g[SH * r:SH * r + SH, i % 2], src).then_inc(x_g_loaded[i % 2], 16)

            load_chunk(0)
            sp.dma_start(w_nat[:, 0, :], w_in).then_inc(io_loaded, 16)
            sp.dma_start(w_nat[:, 1, :], w_gate).then_inc(io_loaded, 16)
            sp.dma_start(io_rows[0:1, :], b_in.unsqueeze(0)).then_inc(io_loaded, 16)
            sp.dma_start(io_rows[1:2, :], b_gate.unsqueeze(0)).then_inc(io_loaded, 16)
            sp.dma_start(w_nat[:, 2, :], w_b).then_inc(ab_loaded, 16)
            sp.dma_start(w_nat[:, 3, :], w_a).then_inc(ab_loaded, 16)
            load_chunk(1)
            load_ctx(0)
            load_ctx(1)
            load_chunk(2)
            load_group(0)
            load_ctx(2)
            sp.dma_start(w_nat[:, 4, :], w_out).then_inc(w_loaded, 16)
            sp.dma_start(gw_nat[0:NH, :], fg_w).then_inc(w_loaded, 16)
            sp.dma_start(gw_nat[NH:2 * NH, :], ig_w).then_inc(w_loaded, 16)
            sp.dma_start(bias_rows[0:NHC, :], sb1.rearrange("(c p) -> c p", p=P)).then_inc(w_loaded, 16)
            sp.dma_start(bias_rows[NHC:NK, :], b1.rearrange("e (c p) -> (e c) p", p=P)).then_inc(w_loaded, 16)
            sp.dma_start(bias_rows[NK:NK + 2, :], b2).then_inc(w_loaded, 16)
            sp.dma_start(bias_rows[NK + 2:NK + 3, :], sb2.unsqueeze(0)).then_inc(w_loaded, 16)
            load_ctx(3)
            load_chunk(3)
            sp.dma_start(b_out_rows[:], b_out.partition_broadcast(P)).then_inc(f_loaded, 16)
            sp.dma_start(gate_bias_rows[:, 0:NH], fg_b.partition_broadcast(P)).then_inc(f_loaded, 16)
            sp.dma_start(gate_bias_rows[:, NH:], ig_b.partition_broadcast(P)).then_inc(f_loaded, 16)
            sp.dma_start(ow_rows[:], out_w.partition_broadcast(P)).then_inc(f_loaded, 16)
            sp.dma_start(route_rows[:], gate_w.partition_broadcast(P)).then_inc(f_loaded, 16)
            sp.dma_start(w1_sb[:, 0, :], sw1).then_inc(f_loaded, 16)
            sp.dma_start(w1_sb[:, 1:3, :], w1.rearrange("e d h -> d e h")).then_inc(f_loaded, 16)
            sp.dma_start(w2_sb[:, 0:NHC, :], sw2.rearrange("(c p) d -> p c d", p=P)).then_inc(f_loaded, 16)
            sp.dma_start(w2_sb[:, NHC:, :], w2.rearrange("e (c p) d -> p (e c) d", p=P)).then_inc(f_loaded, 16)
            load_chunk(4)
            load_ctx(4)
            load_chunk(5)
            load_ctx(5)
            load_group(1)
            load_chunk(6)
            load_ctx(6)
            load_chunk(7)
            load_ctx(7)

            for i in range(NIT):
                g = i - YT // NK
                if g >= 0:
                    sp.wait_ge(o_ready, g + 1)
                    b0, s0 = first_batch(g), SH * half(g)
                    for r in range(BPT):
                        dst = out[b0 + r:b0 + GB:BPT, s0:s0 + SH, :].rearrange("k s d -> s k d")
                        sp.dma_start(dst, x2[SH * r:SH * r + SH, g % 2]).then_inc(stored, 16)
                if i < NG:
                    sp.wait_ge(nm_ready, i + 1)
                    sp.dma_start(row_scratch[i % 2].rearrange("b r s -> r b s"), nm_rows[:, i % 2]).then_inc(nm_stored, 16)
                    sp.wait_ge(nm_stored, 16 * (i + 1))
                    if i >= 2:
                        sp.wait_ge(arg_m_ready, i - 1)
                    for j in range(2):
                        src = row_scratch[i % 2, j::2].rearrange("b r s -> b (r s)").partition_broadcast(S)
                        dst = arg[S * j:S * j + S, i % 2].rearrange("p (b r) s -> p b (r s)", b=2)
                        sp.dma_start(dst, src).then_inc(arg_loaded, 16)
                    if i + 2 < NG:
                        load_group(i + 2)
            sp.wait_ge(stored, 16 * BPT * NG)
            sp.wait_ge(nm_stored, 16 * NG)

        @block.gpsimd
        def _(pool):
            own = [0]

            def then(ins):
                own[0] += 1
                ins.then_inc(pool_own, 1)

            def settle():
                pool.wait_ge(pool_own, own[0])

            def rstd(var_in, ve, dst, seen, n, width, scale, signal):
                pool.wait_ge(seen, n)
                then(pool.tensor_scalar(ve, var_in, scale, LN_EPS, ALU.mult, ALU.add))
                settle()
                pool.tensor_tensor(dst, ve, minus_half[:, 0:width], ALU.pow).then_inc(signal, 1)

            def rstd_chunk(c):
                rstd(mv_tb[:, :, 1], var_tb[:], rstd_tb[:], p_var, c + 1, NTL, 1.0, p_rstd)

            def values(q):
                pool.wait_ge(v_mean_ready, q + 1)
                pool.tensor_tensor(v_ones[:, 4 * q:4 * q + 4, :, 0:DH].rearrange("p n h d -> p (n h) d"),
                                   ctx_nat[:, q % 4].rearrange("p n (h d) -> p (n h) d", h=NH),
                                   v_mean[:, q].unsqueeze(2).to_broadcast([P, NTL * NH, DH]), ALU.subtract).then_inc(v_ready, 1)

            def residual_base(i):
                d = i % 2
                pool.wait_ge(x_g_loaded[d], 16 * BPT * (i // 2 + 1))
                pool.tensor_tensor(x_g[:, d], x_g[:, d], b_out_rows[:].unsqueeze(1).to_broadcast([P, NTL, D]),
                                   ALU.add).then_inc(xb_ready, 1)

            def states(i):
                b0, t0 = first_batch(i), SH * half(i)
                pool.wait_ge(w_ready, t0 + SH)
                pool.wait_ge(c2_ready, (t0 + SH) // CT)
                if i >= 1:
                    pool.wait_ge(op_done, i)
                pool.tensor_tensor(s_t[:], c2[:, t0 + 1:t0 + SH + 1, b0:b0 + GB].rearrange("p t b -> p b t"),
                                   w2n[:, t0:t0 + SH, b0:b0 + GB].rearrange("p t b -> p b t"),
                                   ALU.subtract).then_inc(s_ready, 1)

            then(pool.memset(ident[:], 0.0))
            then(pool.memset(causal[:], 0.0))
            then(pool.memset(seg_keep[:], 1.0))
            then(pool.memset(seg_drop[:], 0.0))
            then(pool.memset(minus_half[:], -0.5))
            settle()
            then(pool.affine_select(out=ident[:], in_=ident[:], compare_op=ALU.not_equal, fill=1.0, base=0,
                                    pattern=[[-1, P]], channel_multiplier=1))
            settle()
            pool.memset(c2[:, 0, :], 0.0).then_inc(consts_ready, 1)
            rstd_chunk(0)
            for j in range(2):
                part = causal[S * j:S * j + S, :]
                settle()
                then(pool.affine_select(out=part, in_=part, compare_op=ALU.is_ge, fill=NEG, base=0,
                                        pattern=[[1, S]], channel_multiplier=-1))
            settle()
            then(pool.memset(seg_keep[:, :, 0:1], 0.0))
            then(pool.memset(seg_drop[:, :, 0:1], NEG))
            settle()
            rstd_chunk(1)
            for t, v in ((q_heads, 0.0), (c_diag, 0.0), (a_cols, 0.0), (cs_carry, 0.0), (m_carry, NEG)):
                pool.memset(t[:], v).then_inc(pool_zero, 1)
            pool.memset(v_ones[:, :, :, DH:DH + 1], 1.0).then_inc(pool_zero, 1)
            pool.wait_ge(pool_zero, 6)
            for c in range(NP1):
                values(c)
                rstd_chunk(c + 2)
            pool.wait_ge(f_loaded, 16 * 9)
            then(pool.tensor_scalar(ow1_rows[:], ow_rows[:], 1.0, None, ALU.add))
            pool.tensor_tensor(route_diff[:], route_rows[:, 1, :], route_rows[:, 0, :], ALU.subtract).then_inc(rows_b_ready, 1)
            pool.wait_ge(rows_b_ready, 1)
            settle()
            residual_base(0)
            states(0)

            for i in range(NIT):
                for k in range(NK):
                    if (i, k) in STATS_AT:
                        rstd_chunk(STATS_AT[i, k])
                    if (i, k) in CTX_AT:
                        values(CTX_AT[i, k])
                    if (g := group_at(i, k, OP + 1)) is not None:
                        rstd(mv_g[:, :, 1], var_g[:], rstd_g[:], ln1_var, g + 1, NTL, 1.0, ln1_rstd)
                    if (g := group_at(i, k, PV + 1)) is not None:
                        rstd(h_var[:], h_ve[:], h_rstd[:], h_var_ready, g + 1, R, 1.0 / DH, h_rstd_ready)
                    if (g := group_at(i, k, PV + 3)) is not None:
                        pool.wait_ge(h_y_ready, g + 1)
                        pool.tensor_tensor(h_o[:], h_y[:].rearrange("p (k h) d -> p k (h d)", k=NTL),
                                           ow1_rows[:].unsqueeze(1).to_broadcast([P, NTL, D]), ALU.mult).then_inc(h_o_ready, 1)
                    if (g := group_at(i, k, X3T - 3)) is not None:
                        rstd(mv_g[:, :, 1], var_g[:], rstd_g[:], ln2_var, g + 1, NTL, 1.0, ln2_rstd)
                    if (g := group_at(i, k, ACOL)) is not None:
                        pool.wait_ge(arg_loaded, 32 * (g + 1))
                        if g >= 1:
                            pool.wait_ge(c_ready, g)
                        h0 = SH * half(g)
                        pool.tensor_tensor(decay[:], arg[:, g % 2],
                                           causal[:, h0:h0 + SH].unsqueeze(1).to_broadcast([P, 2 * R, SH]),
                                           ALU.add).then_inc(arg_m_ready, 1)
                    if k == NK - 2 and i + 1 < NG:
                        residual_base(i + 1)
                        states(i + 1)

        @block.scalar
        def _(act):
            own = [0]

            def then(ins):
                own[0] += 1
                ins.then_inc(act_own, 1)

            def settle():
                act.wait_ge(act_own, own[0])

            def prep_t(c):
                act.wait_ge(xn_t_done, c + 1)
                act.activation(xn_t[:, c % 2, :], ps_l1[0][:], ACT.Copy).then_inc(xn_t_ready, 1)

            def prep_inp(c):
                act.wait_ge(inp_done, c + 1)
                act.activation(inp[:, c * CT:(c + 1) * CT, :].rearrange("p t b -> p (t b)"), ps_l1[1][:], ACT.Identity,
                               bias=io_cols[:, 0:1]).then_inc(inp_ready, 1)

            def prep_gate(c):
                act.wait_ge(pgate_done, c + 1)
                act.activation(neg_tg[:, c * CT:(c + 1) * CT, :].rearrange("p t b -> p (t b)"), ps_l2[:], ACT.Tanh,
                               bias=half_neg_bgate[:], scale=-0.5).then_inc(tg_ready, 1)

            def ctx_evac(q):
                act.wait_ge(ctx_t_done, q + 1)
                act.activation(ctx_t[:, 8 * q:8 * q + 8, :].rearrange("p b t -> p (b t)"), ps_l1[0][:],
                               ACT.Copy).then_inc(ctx_t_ready, 1)

            def step(t):
                act.wait_ge(pre_ready, t + 1)
                col = (t % CT) * NB
                act.activation(th[:, t % 2, :], ps_pre[t // CT % 2][:, col:col + NB], ACT.Tanh).then_inc(th_ready, 1)

            act.wait_ge(io_turned, 1)
            act.activation(io_cols[:], ps_att[:, 0, 2 * P:2 * P + 2], ACT.Copy).then_inc(io_copied, 1)
            act.activation(w_in_t[:], ps_att[:, 0, 0:P], ACT.Copy).then_inc(io_copied, 1)
            act.activation(w_gate_t[:], ps_att[:, 0, P:2 * P], ACT.Copy).then_inc(io_copied, 1)
            act.wait_ge(io_copied, 1)
            act.activation(half_neg_bgate[:], io_cols[:, 1:2], ACT.Copy, scale=-0.5).then_inc(io_copied, 1)
            act.wait_ge(io_copied, 4)
            prep_t(0)
            act.wait_ge(ab_turned, 1)
            act.activation(b_t[:], ps_att[:, 1, 0:P], ACT.Copy).then_inc(ab_copied, 1)
            act.activation(a_pos[:], ps_att[:, 1, P:2 * P], ACT.Copy, scale=0.5).then_inc(ab_copied, 1)
            act.activation(a_neg[:], ps_att[:, 1, P:2 * P], ACT.Copy, scale=-0.5).then_inc(ab_copied, 1)
            prep_inp(0)
            prep_gate(0)
            for c in range(NP1):
                for s in range(CT):
                    step(c * CT + s)
                    if s == 0:
                        prep_t(c + 1)
                    if s == 2:
                        prep_inp(c + 1)
                    if s == 4:
                        prep_gate(c + 1)
                    if s == 6:
                        ctx_evac(c)
                    if c == 2 and s == 1:
                        act.wait_ge(rest_turned, 1)
                        act.activation(bias_cols[:], ps_att[:, 0, 3 * P:3 * P + 15], ACT.Copy).then_inc(rest_copied, 1)
                        act.activation(w_out_t[:], ps_att[:, 1, 2 * P:3 * P], ACT.Copy, scale=0.5).then_inc(rest_copied, 1)
                        act.activation(gw_t[:], ps_att[:, 1, 3 * P:3 * P + 24].rearrange("p (n g) -> p n g", n=3),
                                       ACT.Copy).then_inc(rest_copied, 1)
                    if c == 2 and s == 3:
                        act.wait_ge(rest_copied, 3)
                        then(act.activation(b2_part[:], bias_cols[:, NK:NK + 1], ACT.Identity, bias=bias_cols[:, NK + 1:NK + 2]))
                        settle()
                        act.activation(b2_sum[:], b2_part[:], ACT.Identity, bias=bias_cols[:, NK + 2:NK + 3]).then_inc(b2_ready, 1)

            for i in range(NIT):
                f = i - FFN // NK
                if i == NC - NP1:
                    act.preload_act_table_set("natural_log_exp_and_others")
                for k in range(NK):
                    if 0 <= f < NG:
                        n = NK * f + k
                        act.wait_ge(l1_done, n + 1)
                        if n >= 3:
                            act.wait_ge(l2_done, n - 2)
                        if n == 0:
                            act.wait_ge(b2_ready, 1)
                        act.activation(hid[:, n % 3, :], ps_l1[k % 2][:], ACT.Relu,
                                       bias=bias_cols[:, k:k + 1]).then_inc(hid_ready, 1)
                    if (t := step_at(i, k)) is not None:
                        step(t)
                    if (i, k) in PREP_AT:
                        prep_t(PREP_AT[i, k])
                    if (i, k) in CTX_AT:
                        ctx_evac(CTX_AT[i, k])
                    if (i, k - 2) in PREP_AT:
                        prep_inp(PREP_AT[i, k - 2])
                    if (i, k - 4) in PREP_AT:
                        prep_gate(PREP_AT[i, k - 4])
                    if k == 0 and 1 <= f + 0 <= NG:
                        act.wait_ge(l2_done, NK * f)
                        if f >= 2:
                            act.wait_ge(y_done, f - 1)
                        act.activation(y_t[:], ps_l2[:], ACT.Identity, bias=b2_sum[:]).then_inc(y_t_ready, 1)
                    if (g := group_at(i, k, QT)) is not None:
                        act.wait_ge(q_t_done, g + 1)
                        if g >= 1:
                            act.wait_ge(gates_done, g)
                            act.wait_ge(q_heads_ready, g)
                        act.activation(q_t[:].rearrange("p b s -> p (b s)"), ps_mix[:], ACT.Copy).then_inc(q_t_ready, 1)
                    if (g := group_at(i, k, GATES + 1)) is not None:
                        act.wait_ge(gates_ready, g + 1)
                        then(act.activation(abs_f[:], g_f[:], ACT.Abs))
                        settle()
                        then(act.activation(exp_f[:], abs_f[:], ACT.Exp, scale=-1.0))
                        settle()
                        act.activation(ln_f[:], exp_f[:], ACT.Ln, bias=1.0).then_inc(ln_f_ready, 1)
                    if (g := group_at(i, k, ACOL)) is not None:
                        act.wait_ge(a_done, g + 1)
                        for j in range(2):
                            r0 = S * j + SH * half(g)
                            act.activation(a_cols[r0:r0 + SH, g % NBG, :], ps_mix[r0:r0 + SH, 256:256 + 2 * R],
                                           ACT.Copy).then_inc(a_cols_ready, 1)
                        act.activation(floor_exp[:], ps_mix[:, 320:320 + R], ACT.Exp).then_inc(floor_ready, 1)
                    if (g := group_at(i, k, QK)) is not None:
                        act.wait_ge(arg_ready, g + 1)
                        act.activation(decay[:], decay[:], ACT.Exp).then_inc(decay_ready, 1)
                    if (g := group_at(i, k, PV + 1)) is not None:
                        act.wait_ge(h_n_ready, g + 1)
                        if g >= 1:
                            act.wait_ge(h_o_ready, g)
                        act.activation(h_y[:], h_n[:], ACT.Square).then_inc(h_sq_ready, 1)
                    if (g := group_at(i, k, X3T)) is not None:
                        act.wait_ge(x3_t_done, g + 1)
                        if g >= 1:
                            act.wait_ge(l1_done, NK * (g - 1) + NHC)
                        act.activation(x3_t[:, 0, :], ps_mix[:], ACT.Copy).then_inc(x3_t_ready, 1)
                    if (g := group_at(i, k, E1T)) is not None:
                        act.wait_ge(e1_t_done, g + 1)
                        if g >= 1:
                            act.wait_ge(l1_done, NK * g)
                        act.activation(x3_t[:, 2, :], ps_mix[:], ACT.Copy).then_inc(e1_t_ready, 1)

        @block.tensor
        def _(pe):
            flat = "p t b -> p (t b)"

            def transposes(dst, src, n=NTL):
                for k in range(n):
                    last = pe.transpose(dst[:, k * P:(k + 1) * P], src[:, k, :], ident[:])
                return last

            turned = [0, 0]

            def bank_free():
                if turned[0]:
                    pe.wait_ge(xn_t_ready, turned[0])
                if turned[1]:
                    pe.wait_ge(ctx_t_ready, turned[1])

            def prep_t(c):
                pe.wait_ge(xn_ready, c + 1)
                bank_free()
                transposes(ps_l1[0], x_tb[:, c % 2]).then_inc(xn_t_done, 1)
                turned[0] += 1

            def ctx_trans(q):
                pe.wait_ge(ctx_loaded[q], 16)
                bank_free()
                transposes(ps_l1[0], ctx_nat[:, q % 4]).then_inc(ctx_t_done, 1)
                turned[1] += 1

            def halves(h):
                return [slice(n * TOK // 2, (n + 1) * TOK // 2) for n in ((0, 1) if h is None else (h,))]

            def prep_inp(c, h=None):
                pe.wait_ge(xn_t_ready, c + 1)
                if c >= 1:
                    pe.wait_ge(inp_ready, c)
                for r in halves(h):
                    last = pe.matmul(ps_l1[1][:, r], w_in_t[:], xn_t[:, c % 2, r], start=True, stop=True)
                if h != 0:
                    last.then_inc(inp_done, 1)

            def prep_gate(c, h=None):
                pe.wait_ge(inp_ready, c + 1)
                if c >= 1:
                    pe.wait_ge(tg_ready, c)
                for r in halves(h):
                    last = pe.matmul(ps_l2[:, r], w_gate_t[:], inp[:, c * CT:(c + 1) * CT, :].rearrange(flat)[:, r],
                                     start=True, stop=True)
                if h != 0:
                    last.then_inc(pgate_done, 1)

            def base_b(c, h=None):
                pe.wait_ge(inp_ready, c + 1)
                if c >= 2:
                    pe.wait_ge(th_ready, CT * (c - 1))
                for r in halves(h):
                    pe.matmul(ps_pre[c % 2][:, r], b_t[:], inp[:, c * CT:(c + 1) * CT, :].rearrange(flat)[:, r],
                              start=(r.start == 0), stop=False, skip_group_check=True)

            def base_a(c, h=None):
                pe.wait_ge(c2_ready, c + 1)
                for r in halves(h):
                    last = pe.matmul(ps_pre[c % 2][:, r], a_pos[:], c2[:, c * CT:(c + 1) * CT, :].rearrange(flat)[:, r],
                                     start=False, stop=False, skip_group_check=True)
                if c == 0:
                    last.then_inc(pre_ready, 1)

            def step(t):
                if t == 0:
                    return
                pe.wait_ge(w_ready, t)
                col = (t % CT) * NB
                pe.matmul(ps_pre[t // CT % 2][:, col:col + NB], a_neg[:], w2n[:, t - 1, :], start=False, stop=True,
                          skip_group_check=True).then_inc(pre_ready, 1)

            pe.wait_ge(consts_ready, 1)
            pe.wait_ge(io_loaded, 16 * 4)
            pe.transpose(ps_att[:, 0, 2 * P:2 * P + 2], io_rows[:], ident[0:2, 0:2])
            transposes(ps_att[:, 0, :], w_nat, 2).then_inc(io_turned, 1)
            prep_t(0)
            pe.wait_ge(ab_loaded, 16 * 2)
            transposes(ps_att[:, 1, :], w_nat[:, 2:4, :], 2).then_inc(ab_turned, 1)
            pe.wait_ge(io_copied, 4)
            prep_inp(0)
            prep_gate(0)
            pe.wait_ge(ab_copied, 3)
            base_b(0)
            base_a(0)
            for c in range(NP1):
                for s in range(CT):
                    step(c * CT + s)
                    if s == 0:
                        prep_t(c + 1)
                    if s in (1, 2):
                        prep_inp(c + 1, s - 1)
                    if s in (3, 4):
                        prep_gate(c + 1, s - 3)
                    if s in (5, 6):
                        base_b(c + 1, s - 5)
                    if s == 6:
                        ctx_trans(c)
                    if s == 7:
                        base_a(c + 1)
                    if c == 2 and s == 0:
                        pe.wait_ge(w_loaded, 16 * 7)
                        pe.transpose(ps_att[:, 0, 3 * P:3 * P + 15], bias_rows[:], ident[0:15, 0:15])
                        pe.transpose(ps_att[:, 1, 2 * P:3 * P], w_nat[:, 4, :], ident[:])
                        for n in range(3):
                            last = pe.transpose(ps_att[:, 1, 3 * P + 8 * n:3 * P + 8 * n + 8], gw_nat[:, n * P:(n + 1) * P],
                                                ident[0:8, 0:8])
                        last.then_inc(rest_turned, 1)

            def l1(g, k):
                n = NK * g + k
                if k == 0:
                    pe.wait_ge(x3_t_ready, g + 1)
                if k == NHC:
                    pe.wait_ge(e0_t_ready, g + 1)
                if k == 2 * NHC:
                    pe.wait_ge(e1_t_ready, g + 1)
                if n >= 2:
                    pe.wait_ge(hid_ready, n - 1)
                e = k // NHC
                col = (k % NHC) * P
                pe.matmul(ps_l1[k % 2][:], w1_sb[:, e, col:col + P], x3_t[:, e, :],
                          start=True, stop=True).then_inc(l1_done, 1)

            def l2(g, k):
                n = NK * g + k
                pe.wait_ge(hid_ready, n + 1)
                if k == 0 and g >= 1:
                    pe.wait_ge(y_t_ready, g)
                pe.matmul(ps_l2[:], w2_sb[:, k, :], hid[:, n % 3, :], start=(k == 0), stop=(k == NK - 1)).then_inc(l2_done, 1)

            pe.wait_ge(f_loaded, 16 * 9)
            pe.wait_ge(rest_copied, 3)
            for i in range(NIT):
                f = i - FFN // NK
                for k in range(NK):
                    if k == 0 and 1 <= f <= NG:
                        l2(f - 1, NK - 1)
                    if 0 <= f < NG:
                        if f == 0 and k == 0:
                            pe.wait_ge(tg_ready, NC)
                            pe.wait_ge(ctx_t_ready, 8)
                        l1(f, k)
                        if k >= 1:
                            l2(f, k - 1)
                    if (t := step_at(i, k)) is not None:
                        step(t)
                    if (i, k) in PREP_AT:
                        prep_t(PREP_AT[i, k])
                    if (i, k) in CTX_AT:
                        ctx_trans(CTX_AT[i, k])
                    if (i, k - 2) in PREP_AT:
                        prep_inp(PREP_AT[i, k - 2])
                    if (i, k - 4) in PREP_AT:
                        prep_gate(PREP_AT[i, k - 4])
                    if NP1 + i + 1 < NC and k == BASE_SLOTS[0]:
                        base_b(NP1 + i + 1)
                    if NP1 + i + 1 < NC and k == BASE_SLOTS[1]:
                        base_a(NP1 + i + 1)
                    if (g := group_at(i, k, OP)) is not None:
                        pe.wait_ge(s_ready, g + 1)
                        if g == 1:
                            pe.wait_ge(floor_ready, 1)
                        if g >= 2:
                            pe.wait_ge(e1_t_ready, g - 1)
                        for n in range(NTL):
                            last = pe.matmul(ps_mix[:, n * P:(n + 1) * P],
                                             s_t[:, BPT * n:BPT * (n + 1), :].rearrange("p b s -> p (b s)"),
                                             w_out_t[:], start=True, stop=True)
                        last.then_inc(op_done, 1)
                    if (g := group_at(i, k, YT)) is not None:
                        pe.wait_ge(y_t_ready, g + 1)
                        if i < NG:
                            pe.wait_ge(x1_ready, i + 1)
                        elif i <= NG + 1:
                            pe.wait_ge(e1_t_ready, i - 1)
                        else:
                            pe.wait_ge(o_ready, g)
                        transposes(ps_mix, y_t[:].rearrange("p (k m) -> p k m", k=NTL)).then_inc(y_done, 1)
                    if (g := group_at(i, k, QT)) is not None:
                        pe.wait_ge(x1_ready, g + 1)
                        if i >= YT // NK:
                            pe.wait_ge(o_ready, i - YT // NK + 1)
                        pe.wait_ge(q_ready, g + 1)
                        transposes(ps_mix, q_nat).then_inc(q_t_done, 1)
                    if (g := group_at(i, k, GATES)) is not None:
                        pe.wait_ge(q_t_ready, g + 1)
                        pe.wait_ge(ctx_g_ready, g + 1)
                        if g == 0:
                            pe.wait_ge(gw_kv_ready, 1)
                        for n in range(NTL):
                            dst = ps_mix[:, 8 * n:8 * n + 8]
                            pe.matmul(dst, q_t[:, BPT * n:BPT * (n + 1), :].rearrange("p b s -> p (b s)"), gw_t[:, 0, :],
                                      start=True, stop=False)
                            last = pe.matmul(dst, ctx_g[:, BPT * n:BPT * (n + 1), :].rearrange("p b s -> p (b s)"), gw_kv[:],
                                             start=False, stop=True)
                        last.then_inc(gates_done, 1)
                    if (g := group_at(i, k, ROWS)) is not None:
                        pe.wait_ge(log_f_ready, g + 1)
                        pe.transpose(ps_mix[0:R, 0:P], log_f[:].rearrange("p k h -> p (k h)"), ident[:])
                        pe.transpose(ps_mix[0:R, P:2 * P], g_i[:].rearrange("p k h -> p (k h)"), ident[:]).then_inc(rows_done, 1)
                    if (g := group_at(i, k, ACOL)) is not None:
                        h0 = SH * half(g)
                        pe.wait_ge(scans_ready, g + 1)
                        for b in range(BPT):
                            r0 = S * (b % 2) + h0
                            pe.matmul(ps_mix[r0:r0 + SH, 256 + R * (b // 2):256 + R * (b // 2 + 1)],
                                      a_rows[:, g % 2, b, 1:SH + 1], ident[0:R, 0:R], start=True, stop=True)
                        pe.transpose(ps_mix[:, 320:320 + R], nmc_rows[:, g % 2].rearrange("r b s -> r (b s)"),
                                     ident[0:R, 0:R]).then_inc(a_done, 1)
                    if (g := group_at(i, k, QK)) is not None:
                        b0 = first_batch(g)
                        pe.wait_ge(q_heads_ready, g + 1)
                        if g < NBG:
                            pe.wait_ge(ctx_t_ready, 2 * g + 2)
                        if g >= 1:
                            pe.wait_ge(h_n_ready, g)
                        for b in range(GB):
                            n, r = b // BPT, b % BPT
                            j = r % 2
                            last = pe.matmul(ps_att[S * j:S * j + S, r // 2, n * P:(n + 1) * P], ctx_t[:, b0 + b, :],
                                             q_heads[:, b].rearrange("p h s -> p (h s)"), start=True, stop=True)
                        last.then_inc(qk_done, 1)
                    if (g := group_at(i, k, PV)) is not None:
                        b0 = first_batch(g)
                        pe.wait_ge(c_ready, g + 1)
                        if g < NBG:
                            pe.wait_ge(v_ready, 2 * g + 2)
                        for n in range(NTL):
                            for h in range(NH):
                                for b in range(2):
                                    col = ((n % 2) * NH + h) * (DH + 1)
                                    last = pe.matmul(ps_att[S * b:S * b + S, n // 2, col:col + DH + 1],
                                                     c_diag[:, R * b + NH * n + h].rearrange("p j s -> p (j s)"),
                                                     v_ones[:, b0 // 2 + 2 * n + b, h, :], start=True, stop=True)
                        last.then_inc(pv_done, 1)
                    if (g := group_at(i, k, X3T)) is not None:
                        pe.wait_ge(x3_ready, g + 1)
                        if i < NG:
                            pe.wait_ge(floor_ready, i + 1)
                        else:
                            pe.wait_ge(o_ready, i - YT // NK + 1)
                        transposes(ps_mix, x3).then_inc(x3_t_done, 1)
                    if (g := group_at(i, k, E1T)) is not None:
                        pe.wait_ge(x3_e1_ready, g + 1)
                        pe.wait_ge(x3_t_ready, g + 1)
                        transposes(ps_mix, x3_e1).then_inc(e1_t_done, 1)

        @block.vector
        def _(dve):
            flat = "p t b -> p (t b)"
            own = [0]

            def then(ins):
                own[0] += 1
                ins.then_inc(dve_own, 1)

            def settle():
                dve.wait_ge(dve_own, own[0])

            def statistics(src, bn, mv, signal):
                for k in range(NTL):
                    last = dve.bn_stats(bn[:, k, :], src[:, k, :])
                then(last)
                settle()
                for k in range(NTL):
                    last = dve.bn_aggr(mv[:, k, :], bn[:, k, :])
                last.then_inc(signal, 1)

            def normalise(dst, src, mv, rs, signal):
                for k in range(NTL):
                    last = dve.tensor_scalar(dst[:, k, :], src[:, k, :], mv[:, k, 0:1], rs[:, k:k + 1],
                                             ALU.subtract, ALU.mult)
                last.then_inc(signal, 1)

            def prep_stats(c):
                dve.wait_ge(x_tb_loaded[c % 2], 32 * (c // 2 + 1))
                statistics(x_tb[:, c % 2], bn_tb, mv_tb, p_var)

            def prep_norm(c):
                dve.wait_ge(p_rstd, c + 1)
                dve.wait_ge(p_var, c + 1)
                normalise(x_tb[:, c % 2], x_tb[:, c % 2], mv_tb, rstd_tb, xn_ready)

            def prep_c2(c):
                dve.wait_ge(tg_ready, c + 1)
                dve.wait_ge(inp_ready, c + 1)
                dve.scalar_tensor_tensor(c2[:, c * CT + 1:(c + 1) * CT + 1, :].rearrange(flat),
                                         neg_tg[:, c * CT:(c + 1) * CT, :].rearrange(flat), 1.0,
                                         inp[:, c * CT:(c + 1) * CT, :].rearrange(flat), ALU.add, ALU.mult).then_inc(c2_ready, 1)

            def value_means(q):
                dve.wait_ge(ctx_loaded[q], 16)
                then(dve.reduce_sum(v_sum[:, q], ctx_nat[:, q % 4].rearrange("p n (h d) -> p (n h) d", h=NH), AX_X))
                settle()
                dve.tensor_scalar(v_mean[:, q], v_sum[:, q], 1.0 / DH, None, ALU.mult).then_inc(v_mean_ready, 1)

            def step(t):
                dve.wait_ge(th_ready, t + 1)
                dve.scalar_tensor_tensor(w2n[:, t, :], neg_tg[:, t, :], 1.0, th[:, t % 2, :],
                                         ALU.subtract, ALU.mult).then_inc(w_ready, 1)

            prep_stats(0)
            prep_norm(0)
            prep_stats(1)
            prep_norm(1)
            prep_c2(0)
            for c in range(NP1):
                for s in range(CT):
                    step(c * CT + s)
                    if s == 0:
                        value_means(c)
                    if s == 2:
                        prep_stats(c + 2)
                    if s == 4:
                        prep_c2(c + 1)
                    if s == 5:
                        prep_norm(c + 2)
                    if c == 2 and s == 6:
                        dve.wait_ge(rest_copied, 3)
                        dve.tensor_tensor(gw_kv[:], gw_t[:, 1, :], gw_t[:, 2, :], ALU.add).then_inc(gw_kv_ready, 1)

            for i in range(NIT):
                for k in range(NK):
                    if (t := step_at(i, k)) is not None:
                        step(t)
                    if (i, k) in CTX_AT:
                        value_means(CTX_AT[i, k])
                    if (i, k) in STATS_AT:
                        prep_stats(STATS_AT[i, k])
                    if (i, k - 2) in STATS_AT:
                        prep_norm(STATS_AT[i, k - 2])
                    if (i, k - 5) in PREP_AT:
                        prep_c2(PREP_AT[i, k - 5])
                    if (g := group_at(i, k, OP)) is not None:
                        b0, h0, d = first_batch(g), SH * half(g), g % 2
                        if g < NBG:
                            dve.wait_ge(ctx_t_ready, 2 * g + 2)
                        if g >= 1:
                            dve.wait_ge(gates_done, g)
                        dve.tensor_copy(ctx_g[:], ctx_t[:, b0:b0 + GB, h0:h0 + SH]).then_inc(ctx_g_ready, 1)
                        dve.wait_ge(op_done, g + 1)
                        dve.wait_ge(xb_ready, g + 1)
                        dve.tensor_tensor(x1[:, d], ps_mix[:].rearrange("p (k m) -> p k m", k=NTL), x_g[:, d],
                                          ALU.add).then_inc(x1_ready, 1)
                        dve.wait_ge(x1_ready, g + 1)
                        statistics(x1[:, d], bn_g, mv_g, ln1_var)
                    if (g := group_at(i, k, YT)) is not None:
                        dve.wait_ge(y_done, g + 1)
                        dve.tensor_tensor(x2[:, g % 2], ps_mix[:].rearrange("p (k m) -> p k m", k=NTL), x2[:, g % 2],
                                          ALU.add).then_inc(o_ready, 1)
                    if (g := group_at(i, k, QT - 1)) is not None:
                        dve.wait_ge(ln1_rstd, g + 1)
                        dve.wait_ge(ln1_var, g + 1)
                        if g >= 1:
                            dve.wait_ge(q_t_done, g)
                        normalise(q_nat, x1[:, g % 2], mv_g, rstd_g, q_ready)
                    if (g := group_at(i, k, QT)) is not None:
                        dve.wait_ge(q_t_ready, g + 1)
                        if g == 0:
                            dve.wait_ge(pool_zero, 6)
                        else:
                            dve.wait_ge(qk_done, g)
                        for h in range(NH):
                            r = slice(DH * h, DH * h + DH)
                            last = dve.tensor_copy(q_heads[r, :, h, :], q_t[r])
                        last.then_inc(q_heads_ready, 1)
                    if (g := group_at(i, k, GATES)) is not None:
                        dve.wait_ge(gates_done, g + 1)
                        if g >= 1:
                            dve.wait_ge(rows_done, g)
                        pre = ps_mix[:, 0:8 * NTL].rearrange("p (k g) -> p k g", g=8)
                        then(dve.tensor_tensor(g_i[:], pre[:, :, NH:], gate_bias_rows[:, NH:].unsqueeze(1).to_broadcast([P, NTL, NH]),
                                               ALU.add))
                        dve.tensor_tensor(g_f[:], pre[:, :, 0:NH], gate_bias_rows[:, 0:NH].unsqueeze(1).to_broadcast([P, NTL, NH]),
                                          ALU.add).then_inc(gates_ready, 1)
                    if (g := group_at(i, k, ROWS - 1)) is not None:
                        dve.wait_ge(ln_f_ready, g + 1)
                        dve.wait_ge(gates_ready, g + 1)
                        settle()
                        kh = "p k h -> p (k h)"
                        dve.scalar_tensor_tensor(log_f[:].rearrange(kh), g_f[:].rearrange(kh), 0.0, ln_f[:].rearrange(kh),
                                                 ALU.min, ALU.subtract).then_inc(log_f_ready, 1)
                    if (g := group_at(i, k, ROWS)) is not None:
                        d, b = g % 2, g % NBG
                        dve.wait_ge(rows_done, g + 1)
                        if g >= 2:
                            dve.wait_ge(a_done, g - 1)
                            dve.wait_ge(nm_stored, 16 * (g - 1))
                        lf_ps = ps_mix[0:R, 0:P].rearrange("r (b s) -> r b s", b=BPT)
                        ig_ps = ps_mix[0:R, P:2 * P].rearrange("r (b s) -> r b s", b=BPT)
                        rows = "r b s -> r (b s)"
                        settle()
                        then(dve.tensor_copy(lf_rows[:, :, 0:1], cs_carry[:, b].unsqueeze(2)))
                        then(dve.tensor_copy(lf_rows[:, :, 1:], lf_ps))
                        then(dve.tensor_copy(a_rows[:, d, :, 0:1], m_carry[:, b].unsqueeze(2)))
                        settle()
                        then(dve.tensor_tensor_scan(cs_rows[:].rearrange(rows), seg_keep[:].rearrange(rows), lf_rows[:].rearrange(rows),
                                                    0.0, ALU.mult, ALU.add))
                        settle()
                        then(dve.tensor_tensor(a_rows[:, d, :, 1:], ig_ps, cs_rows[:, :, 0:SH], ALU.subtract))
                        settle()
                        then(dve.tensor_tensor_scan(m_rows[:].rearrange(rows), seg_drop[:].rearrange(rows), a_rows[:, d].rearrange(rows),
                                                    0.0, ALU.add, ALU.max))
                        settle()
                        dve.tensor_scalar(nm_rows[:, d], m_rows[:, :, 1:], -1.0, None, ALU.mult).then_inc(nm_ready, 1)
                        dve.wait_ge(nm_ready, g + 1)
                        then(dve.tensor_copy(cs_carry[:, b].unsqueeze(2), cs_rows[:, :, SH:]))
                        then(dve.tensor_copy(m_carry[:, b].unsqueeze(2), m_rows[:, :, SH:]))
                        dve.tensor_tensor(nmc_rows[:, d], nm_rows[:, d], cs_rows[:, :, 1:], ALU.subtract).then_inc(scans_ready, 1)
                    if (g := group_at(i, k, QK - 1)) is not None:
                        dve.wait_ge(a_cols_ready, 2 * (g + 1))
                        dve.wait_ge(arg_m_ready, g + 1)
                        dve.tensor_tensor(decay[:], decay[:], a_cols[:, g % NBG].unsqueeze(2).to_broadcast([P, 2 * R, SH]),
                                          ALU.add).then_inc(arg_ready, 1)
                    if (g := group_at(i, k, QK + 1)) is not None:
                        dve.wait_ge(qk_done, g + 1)
                        dve.wait_ge(decay_ready, g + 1)
                        if g >= 1:
                            dve.wait_ge(pv_done, g)
                        for j in range(2):
                            r = slice(S * j, S * j + S)
                            last = dve.scalar_tensor_tensor(c_diag[r, :, j, :], ps_att[r].rearrange("p a (c s) -> p (a c) s", s=SH),
                                                            DH ** -0.5, decay[r], ALU.mult, ALU.mult)
                        last.then_inc(c_ready, 1)
                    if (g := group_at(i, k, PV)) is not None:
                        dve.wait_ge(pv_done, g + 1)
                        dve.wait_ge(floor_ready, g + 1)
                        hp = ps_att[:, :, 0:2 * NH * (DH + 1)].rearrange("p a (g c) -> p a g c", c=DH + 1)
                        total = hp[:, :, :, DH]
                        two = "p (a g) -> p a g"
                        nv = [norm[:, n].rearrange(two, a=2) for n in range(4)]
                        then(dve.tensor_tensor(nv[0], total, floor_exp[:].rearrange(two, a=2), ALU.max))
                        settle()
                        then(dve.scalar_tensor_tensor(nv[1], total, -1.0, nv[0], ALU.mult, ALU.max))
                        settle()
                        then(dve.tensor_scalar(norm[:, 2], norm[:, 1], N_EPS, None, ALU.add))
                        settle()
                        then(dve.reciprocal(norm[:, 3], norm[:, 2]))
                        settle()
                        dve.tensor_tensor(h_n[:].rearrange("p (a g) d -> p a g d", a=2), hp[:, :, :, 0:DH],
                                          nv[3].unsqueeze(3).to_broadcast([P, 2, 2 * NH, DH]), ALU.mult).then_inc(h_n_ready, 1)
                    if (g := group_at(i, k, PV + 1)) is not None:
                        dve.wait_ge(h_sq_ready, g + 1)
                        dve.reduce_sum(h_var[:], h_y[:], AX_X).then_inc(h_var_ready, 1)
                    if (g := group_at(i, k, PV + 3)) is not None:
                        dve.wait_ge(h_rstd_ready, g + 1)
                        dve.wait_ge(h_var_ready, g + 1)
                        dve.tensor_tensor(h_y[:], h_n[:], h_rstd[:].unsqueeze(2).to_broadcast([P, R, DH]), ALU.mult).then_inc(h_y_ready, 1)
                    if (g := group_at(i, k, X3T - 4)) is not None:
                        dve.wait_ge(h_o_ready, g + 1)
                        if g >= 2:
                            dve.wait_ge(stored, 16 * BPT * (g - 1))
                        dve.tensor_tensor(x2[:, g % 2], x1[:, g % 2], h_o[:], ALU.add).then_inc(x2_ready, 1)
                        dve.wait_ge(x2_ready, g + 1)
                        statistics(x2[:, g % 2], bn_g, mv_g, ln2_var)
                    if (g := group_at(i, k, X3T - 2)) is not None:
                        dve.wait_ge(ln2_rstd, g + 1)
                        dve.wait_ge(ln2_var, g + 1)
                        if g >= 1:
                            dve.wait_ge(x3_t_done, g)
                        normalise(x3, x2[:, g % 2], mv_g, rstd_g, x3_ready)
                    if (g := group_at(i, k, X3T - 1)) is not None:
                        dve.wait_ge(x3_ready, g + 1)
                        if g == 0:
                            dve.wait_ge(rows_b_ready, 1)
                        else:
                            dve.wait_ge(e1_t_done, g)
                        for n in range(NTL):
                            last = dve.tensor_tensor_reduce(x3_e1[:, n, :], x3[:, n, :], route_diff[:], 1.0, 0.0, ALU.mult, ALU.add,
                                                            route[:, n:n + 1])
                            then(last)
                        settle()
                        then(dve.tensor_scalar(pick[:], route[:], 0.0, None, ALU.is_gt))
                        settle()
                        dve.tensor_tensor(x3_e1[:], x3[:], pick[:].unsqueeze(2).to_broadcast([P, NTL, D]), ALU.mult).then_inc(x3_e1_ready, 1)
                    if (g := group_at(i, k, FFN)) is not None:
                        dve.wait_ge(e1_t_ready, g + 1)
                        if g >= 1:
                            dve.wait_ge(l1_done, NK * (g - 1) + 2 * NHC)
                        dve.tensor_tensor(x3_t[:, 1, :], x3_t[:, 0, :], x3_t[:, 2, :], ALU.subtract).then_inc(e0_t_ready, 1)


_INS = ['x', 'ctx_1024', 'L0_attn_A', 'L0_attn_B', 'L0_attn_W_in', 'L0_attn_b_in', 'L0_attn_W_gate', 'L0_attn_b_gate',
        'L0_attn_W_out', 'L0_attn_b_out', 'L0_xattn_igate_w', 'L0_xattn_igate_b', 'L0_xattn_fgate_w', 'L0_xattn_fgate_b',
        'L0_xattn_out_w', 'L0_ffn_gate_w', 'L0_ffn_w1', 'L0_ffn_b1', 'L0_ffn_w2', 'L0_ffn_b2', 'L0_ffn_sw1', 'L0_ffn_sb1',
        'L0_ffn_sw2', 'L0_ffn_sb2']


def kernel(**inputs):
    import numpy as np
    import concourse.bacc as bacc
    from concourse.bass_utils import run_bass_kernel_spmd

    nc = bacc.Bacc("TRN2", target_bir_lowering=False, num_devices=1)
    arrays, args = {}, []
    for name in _INS:
        a = np.ascontiguousarray(inputs[name])
        arrays[f"in_{name}"] = a
        args.append(nc.dram_tensor(f"in_{name}", a.shape, mybir.dt.from_np(a.dtype), kind="ExternalInput").ap())
    out = nc.dram_tensor("out_x", (NB, S, D), F32, kind="ExternalOutput").ap()
    decoder_layer(nc, *args, out)
    r = run_bass_kernel_spmd(nc, [arrays], core_ids=[0])
    return r.results[0]["out_x"]
```

```python
from contextlib import ExitStack

import concourse.bass as bass
from concourse import mybir

ALU = mybir.AluOpType
ACT = mybir.ActivationFunctionType
F32 = mybir.dt.float32
F32R = mybir.dt.float32r
AX_X = mybir.AxisListType.X

P = 128
NB, S, D = 64, 64, 128
NH, DH = 4, 32
NE, HID = 3, 512
NHC = HID // P
NK = NE * NHC
CT = 8
NC = S // CT
TOK = CT * NB
SH = S // 2
GB = TOK // SH
NG = NB * S // TOK
NBG = NB // GB
NTL = TOK // P
BPT = P // SH
LN_EPS, N_EPS = 1e-5, 1e-8
NEG = -1e30
NP1 = NC // 2
STEPS_AT = {
    0: (0,), 3: (1,), 4: (2,), 6: (3,), 8: (4,), 11: (5, 6), 13: (7,), 15: (8,), 19: (9,), 21: (10,), 22: (11, 12),
    24: (13,), 26: (14,), 30: (15,), 35: (16,), 36: (17,), 38: (18,), 40: (19,), 41: (20,), 43: (21,), 45: (22,),
    47: (23,), 50: (24, 25), 51: (26,), 53: (27,), 54: (28,), 58: (29,), 61: (30, 31), 65: (32, 33), 67: (34,),
    75: (35,), 77: (36,), 79: (37,), 82: (38,), 85: (39,), 88: (40,), 91: (41,), 94: (42,), 97: (43,), 102: (44,),
    104: (45,), 107: (46,), 111: (47,), 114: (48,), 115: (49,), 116: (50,), 118: (51,), 127: (52,), 129: (53,),
    130: (54,), 133: (55,), 134: (56,), 137: (57,), 142: (58,), 143: (59,), 145: (60,), 153: (61,), 157: (62,),
    158: (63,),
}
PREP_AT = {1: 0, 2: 16, 3: 32, 4: 50, 5: 68, 6: 84, 7: 95}
PREP = {
    "load_chunk": -42, "prep_stats0": -60, "prep_stats1": -48, "prep_aggr": -35, "prep_rstd": -49,
    "prep_norm0": -21, "prep_norm1": -15, "prep_turn": 0, "prep_xt": 1, "prep_inp0": 3, "prep_inp1": 4,
    "prep_inp_out": 5, "prep_gate0": 7, "prep_gate1": 8, "prep_gate_out": 8, "prep_c2": 10, "base_b0": 9,
    "base_b1": 11, "base_a": 14,
}
PREP_X = {
    2: {
        "prep_stats1": -9, "base_b1": 11, "base_b0": 8, "prep_stats0": -11, "prep_aggr": -8, "prep_rstd": -4,
        "prep_norm0": -5, "prep_norm1": -5, "base_a": 14, "prep_gate0": 6,
    },
    3: {
        "prep_stats0": -14, "prep_stats1": -14, "prep_aggr": -13, "prep_rstd": -13, "prep_norm0": -9,
        "prep_norm1": -8, "prep_inp1": 5, "prep_inp0": 4, "prep_xt": -1, "base_b0": 8, "base_b1": 11,
        "prep_turn": -2, "load_chunk": -50, "prep_inp_out": 4, "prep_gate_out": 9,
    },
    4: {
        "prep_inp0": 0, "prep_gate_out": 10, "prep_stats0": -14, "prep_stats1": -14, "prep_aggr": -13,
        "prep_rstd": -13, "prep_norm0": -10, "prep_norm1": -9, "base_b0": 8, "prep_turn": -2, "prep_xt": -2,
        "prep_gate0": 5, "prep_gate1": 7, "load_chunk": -40, "prep_c2": 9, "prep_inp1": 1, "prep_inp_out": 2,
        "base_b1": 12,
    },
    5: {
        "base_b0": 0, "base_b1": 7, "base_a": 11, "prep_c2": 5, "prep_stats0": -25, "prep_stats1": -21,
        "prep_aggr": -21, "prep_gate_out": 6, "prep_gate0": 5, "prep_rstd": -20, "prep_norm0": -12,
        "prep_norm1": -10, "load_chunk": -48, "prep_turn": -1, "prep_xt": -2, "prep_inp0": -1, "prep_inp1": 0,
        "prep_inp_out": 0, "prep_gate1": 6,
    },
    6: {
        "base_b0": 18, "base_b1": 18, "base_a": 19, "prep_gate0": 1, "prep_gate1": 3, "prep_gate_out": 1,
        "prep_c2": 3, "prep_stats0": -23, "prep_stats1": -21, "prep_aggr": -19, "prep_rstd": -20,
        "prep_norm0": -14, "prep_norm1": -12, "prep_xt": -5, "load_chunk": -46, "prep_turn": -6, "prep_inp0": -2,
        "prep_inp1": -2, "prep_inp_out": -2,
    },
    7: {
        "base_b0": 30, "base_b1": 33, "base_a": 38, "load_chunk": -44, "prep_inp0": 5, "prep_inp1": 5,
        "prep_inp_out": 6, "prep_stats0": -11, "prep_stats1": -11, "prep_aggr": -9, "prep_rstd": -9,
        "prep_gate0": 11, "prep_norm0": -5, "prep_norm1": -3, "prep_xt": 3, "prep_turn": 1, "prep_gate1": 14,
        "prep_gate_out": 13, "prep_c2": 15,
    },
}
CTX_AT = {0: 13, 1: 27, 2: 38, 3: 65, 4: 69, 5: 82, 6: 93, 7: 102}
MEANS_LAG, VALUES_LAG, CTX_LEAD = -12, -7, 45
W_AT = {0: 73, 1: 66, 2: 80}
W_LO_LAG = 11
CTX_GATES_AT = {0: 52, 4: 57, 5: 74, 1: 81, 2: 84, 6: 101, 7: 103, 3: 113}
CTX_GATES = {"ctx_copy": 0, "ctx_gates": 1, "ctx_gates_out": 2}
GROUP_AT = {0: 64, 1: 88, 2: 112, 3: 136, 4: 160, 5: 184, 6: 208, 7: 232}
GROUP = {
    "residual_base": -11, "states": -20, "out_product": 0, "x1": 1, "x1_stats0": 1, "x1_stats1": 1, "x1_aggr": 1,
    "ln1_rstd": 3, "q0": 4, "q1": 4, "q_turn": 6, "q_out": 8, "q_heads0": 9, "q_heads1": 10, "gates": 8,
    "gates_bias": 8, "softplus": 12, "log_sigmoid": 10, "rows": 12, "scans": 13, "bounce": 21, "a_cols": 18,
    "a_cols_out": 18, "mask": 18, "arg": 21, "qk": 22, "decay_exp": 23, "c_diag0": 24, "c_diag1": 24, "pv": 27,
    "h_n": 29, "h_square": 32, "h_var": 31, "h_rstd": 31, "h_y": 34, "h_out": 36, "x2": 37, "x2_stats0": 37,
    "x2_stats1": 39, "x2_aggr": 39, "ln2_rstd": 38, "x3_0": 40, "x3_1": 42, "route": 43, "x3_turn": 45,
    "x3_out": 46, "e1_turn": 51, "e1_out": 52, "e0": 52, "l1": 48, "relu": 49, "l2": 51, "y_out": 73, "y_turn": 74,
    "o": 74, "store": 79, "x3_rest": 46, "e1_rest": 53,
}
FILL = {
    0: {
        "states": -1, "residual_base": -2, "x2": 38, "x2_stats0": 38, "x2_stats1": 38, "x2_aggr": 39,
        "ln2_rstd": 41, "x3_0": 42, "x3_1": 42, "h_n": 28, "h_out": 36, "h_y": 34, "gates": 9, "gates_bias": 6,
        "x3_turn": 45, "e1_out": 53, "e1_rest": 53, "ln1_rstd": 0, "bounce": 13, "out_product": 1, "e0": 55,
        "decay_exp": 22, "x3_out": 45, "y_turn": 82, "o": 82, "store": 89, "q_turn": 8, "c_diag0": 23,
        "c_diag1": 23, "pv": 25, "h_square": 31, "h_var": 31, "h_rstd": 32, "mask": 19, "x1": 2, "x1_stats0": 2,
        "x1_stats1": 2, "x1_aggr": 2, "q0": 4, "q1": 4, "q_out": 7, "q_heads0": 8, "q_heads1": 9, "a_cols": 18,
        "a_cols_out": 19, "qk": 23, "arg": 22, "rows": 13, "scans": 14, "e1_turn": 53,
    },
    1: {
        "softplus": 12, "residual_base": -8, "pv": 29, "h_n": 29, "x3_turn": 44, "states": -15, "h_square": 32,
        "h_var": 29, "h_rstd": 36, "bounce": 17, "q_out": 7, "x3_0": 43, "x3_1": 43, "route": 45, "a_cols": 20,
        "c_diag0": 22, "c_diag1": 23, "x2": 38, "x2_stats0": 40, "x2_stats1": 40, "x2_aggr": 40, "mask": 19,
        "store": 86, "e0": 53, "scans": 12, "q0": 3, "q1": 3, "x3_rest": 47, "q_heads0": 9, "q_heads1": 9,
        "arg": 20, "decay_exp": 21, "e1_rest": 53, "x3_out": 43, "log_sigmoid": 10, "ln2_rstd": 36,
        "out_product": 1, "rows": 13, "gates_bias": 5,
    },
    2: {
        "qk": 22, "arg": 23, "decay_exp": 23, "c_diag0": 23, "c_diag1": 23, "q_heads0": 10, "q_heads1": 10,
        "route": 47, "a_cols_out": 18, "h_square": 32, "out_product": -1, "softplus": 9, "x1": 2, "x1_stats0": 2,
        "x1_stats1": 2, "x1_aggr": 2, "residual_base": -16, "states": -15, "x2": 40, "x2_stats0": 40,
        "x2_stats1": 40, "x2_aggr": 40, "ln2_rstd": 39, "x3_0": 41, "x3_1": 41, "h_out": 35, "mask": 19,
        "h_var": 31, "o": 76, "scans": 12,
    },
    3: {
        "bounce": 19, "e0": 56, "e1_out": 51, "route": 43, "x3_0": 42, "x3_1": 42, "x1": 1, "x1_stats0": 5,
        "x1_stats1": 5, "x1_aggr": 5, "q0": 5, "q1": 5, "store": 77, "q_turn": 6, "h_y": 36, "h_out": 35,
        "residual_base": -22, "states": -15, "out_product": 1, "qk": 23, "a_cols": 18, "ln1_rstd": 4, "q_out": 8,
        "q_heads0": 10, "q_heads1": 10, "h_square": 32, "ln2_rstd": 42, "x2": 40, "x2_stats0": 41, "x2_stats1": 41,
        "x2_aggr": 41, "rows": 13, "scans": 12,
    },
    4: {
        "states": -3, "residual_base": -2, "h_y": 34, "pv": 29, "h_n": 30, "x3_0": 43, "x3_1": 43, "route": 44,
        "h_var": 30, "e1_rest": 51, "h_out": 35, "bounce": 18, "a_cols": 17, "softplus": 11, "mask": 21,
        "x3_rest": 47, "h_square": 32, "h_rstd": 32, "q_turn": 4, "q_out": 4, "q_heads0": 6, "q_heads1": 6,
        "x2_stats0": 37, "x2_stats1": 37, "x2_aggr": 37, "e0": 52, "x1_stats1": 2, "x1_aggr": 2,
    },
    7: {
        "softplus": 9, "q_turn": 4, "h_rstd": 34, "h_square": 30, "e1_turn": 47, "e1_out": 48, "e1_rest": 47,
        "e0": 50, "a_cols": 19, "qk": 20, "y_out": 75, "y_turn": 79, "o": 75, "mask": 16, "x3_0": 43, "x3_1": 43,
        "route": 43, "ln1_rstd": 1, "states": -23, "decay_exp": 23, "rows": 10, "scans": 11, "bounce": 14,
        "h_y": 33, "h_out": 36, "store": 78, "q0": 3, "q1": 3, "q_out": 5, "q_heads0": 7, "q_heads1": 10, "x2": 38,
        "x2_stats0": 38, "x2_stats1": 40, "x2_aggr": 40, "ln2_rstd": 38,
    },
}
ROWS_B_SLOT, REST_SLOT, TABLE_SLOT = 60, 22, 160
SLOTS = GROUP_AT[NG - 1] + GROUP["store"] + 1


def decoder_layer(nc, x, ctx_in, w_a, w_b, w_in, b_in, w_gate, b_gate, w_out, b_out,
                  ig_w, ig_b, fg_w, fg_b, out_w, gate_w, w1, b1, w2, b2, sw1, sb1, sw2, sb2, out):
    row_scratch = nc.dram_tensor("row_scratch", (2, BPT, NTL * NH, SH), F32).ap()

    with ExitStack() as stack:
        def sb(name, shape, dt=F32):
            return stack.enter_context(nc.sbuf_tensor(name, shape, dt))

        def psum(name, shape):
            return stack.enter_context(nc.psum_tensor(name, shape, F32))

        def sem(name):
            return stack.enter_context(nc.semaphore(name))

        ps_pre = [psum(f"ps_pre{n}", [P, TOK]) for n in range(2)]
        ps_att = psum("ps_att", [P, 2, 512])
        ps_l1 = [psum(f"ps_l1_{n}", [P, TOK]) for n in range(2)]
        ps_l2 = psum("ps_l2", [P, TOK])
        ps_mix = psum("ps_mix", [P, TOK])

        ident = sb("ident", [P, P])
        causal = sb("causal", [P, S])
        seg_keep = sb("seg_keep", [NTL * NH, BPT, SH + 1])
        seg_drop = sb("seg_drop", [NTL * NH, BPT, SH + 1])
        minus_half = sb("minus_half", [P, 16])
        w_nat = sb("w_nat", [P, 5, P])
        io_rows = sb("io_rows", [2, P])
        io_cols = sb("io_cols", [P, 2])
        gw_nat = sb("gw_nat", [2 * NH, 3 * D])
        bias_rows = sb("bias_rows", [15, P])
        bias_cols = sb("bias_cols", [P, 15])
        half_neg_bgate = sb("half_neg_bgate", [P, 1])
        b2_sum = sb("b2_sum", [P, 1])
        b2_part = sb("b2_part", [P, 1])
        a_pos = sb("a_pos", [P, P])
        a_neg = sb("a_neg", [P, P])
        b_t = sb("b_t", [P, P])
        w_in_t = sb("w_in_t", [P, P])
        w_gate_t = sb("w_gate_t", [P, P])
        w_out_t = sb("w_out_t", [P, P])
        gw_t = sb("gw_t", [P, 3, 2 * NH])
        gw_kv = sb("gw_kv", [P, 2 * NH])
        b_out_rows = sb("b_out_rows", [P, D])
        gate_bias_rows = sb("gate_bias_rows", [P, 2 * NH])
        ow_rows = sb("ow_rows", [P, D])
        ow1_rows = sb("ow1_rows", [P, D])
        route_rows = sb("route_rows", [P, 2, D])
        route_diff = sb("route_diff", [P, D])
        w1_hi = sb("w1_hi", [P, NE, HID], F32R)
        w1_lo = sb("w1_lo", [P, NE, HID], F32R)
        w2_sb = sb("w2_sb", [P, NK, D])
        ctx_t = sb("ctx_t", [P, NB, S])
        v_sum = sb("v_sum", [P, 8, NTL * NH])
        v_mean = sb("v_mean", [P, 8, NTL * NH])
        v_ones = sb("v_ones", [P, NB * S // P, NH, DH + 1])
        bn_tb = sb("bn_tb", [P, NTL, 6])
        mv_tb = sb("mv_tb", [P, NTL, 2])
        var_tb = sb("var_tb", [P, NTL])
        rstd_tb = sb("rstd_tb", [P, NTL])
        inp = sb("inp", [P, S, NB])
        neg_tg = sb("neg_tg", [P, S, NB])
        w2n = neg_tg
        c2 = sb("c2", [P, S + 1, NB])
        th = sb("th", [P, 2, NB])
        x_g = sb("x_g", [P, 2, NTL, D])
        s_t = sb("s_t", [P, GB, SH])
        x1 = sb("x1", [P, 3, NTL, D])
        bn_g = [sb(f"bn_g{n}", [P, NTL, 6]) for n in range(2)]
        mv_g = [sb(f"mv_g{n}", [P, NTL, 2]) for n in range(2)]
        var_g = [sb(f"var_g{n}", [P, NTL]) for n in range(2)]
        rstd_g = [sb(f"rstd_g{n}", [P, NTL]) for n in range(2)]
        q_nat = sb("q_nat", [P, NTL, D])
        q_t = sb("q_t", [P, GB, SH])
        ctx_g = sb("ctx_g", [P, GB, SH])
        q_heads = sb("q_heads", [P, GB, NH, SH])
        ctx_gates = sb("ctx_gates", [P, NG, NTL, 2 * NH])
        g_f = sb("g_f", [P, NTL, NH])
        g_i = sb("g_i", [P, NTL, NH])
        abs_f = sb("abs_f", [P, NTL, NH])
        exp_f = sb("exp_f", [P, NTL, NH])
        ln_f = sb("ln_f", [P, NTL, NH])
        log_f = sb("log_f", [P, NTL, NH])
        R = NTL * NH
        lf_rows = sb("lf_rows", [R, BPT, SH + 1])
        cs_rows = sb("cs_rows", [R, BPT, SH + 1])
        a_rows = sb("a_rows", [R, 2, BPT, SH + 1])
        m_rows = sb("m_rows", [R, BPT, SH + 1])
        nm_rows = sb("nm_rows", [R, 2, BPT, SH])
        nmc_rows = sb("nmc_rows", [R, 2, BPT, SH])
        cs_carry = sb("cs_carry", [R, NBG, BPT])
        m_carry = sb("m_carry", [R, NBG, BPT])
        a_cols = sb("a_cols", [P, NBG, 2 * R])
        floor_exp = sb("floor_exp", [P, R])
        arg = sb("arg", [P, 2 * R, SH])
        decay = sb("decay", [P, 2 * R, SH])
        c_diag = sb("c_diag", [P, 2 * R, 2, SH])
        norm = sb("norm", [P, 4, R])
        h_n = sb("h_n", [P, R, DH])
        h_var = sb("h_var", [P, R])
        h_ve = sb("h_ve", [P, R])
        h_rstd = sb("h_rstd", [P, R])
        h_y = sb("h_y", [P, R, DH])
        x2 = sb("x2", [P, 3, NTL, D])
        x3 = sb("x3", [P, NTL, D])
        route = sb("route", [P, NTL])
        pick = sb("pick", [P, NTL])
        x3_e1 = sb("x3_e1", [P, NTL, D])
        with ExitStack() as early:
            w1_nat = early.enter_context(nc.sbuf_tensor("w1_nat", [P, NE, HID], F32))
            x_tb = early.enter_context(nc.sbuf_tensor("x_tb", [P, 2, NTL, D], F32))
            xn_t = early.enter_context(nc.sbuf_tensor("xn_t", [P, 2, TOK], F32))
            ctx_nat = early.enter_context(nc.sbuf_tensor("ctx_nat", [P, 4, NTL, D], F32))
        x3_hi = sb("x3_hi", [P, NE, TOK], F32R)
        x3_lo = sb("x3_lo", [P, NE, TOK], F32R)
        hid = sb("hid", [P, 3, TOK])
        y_t = sb("y_t", [P, TOK])

        io_loaded, ab_loaded, w_loaded, f_loaded = sem("io_loaded"), sem("ab_loaded"), sem("w_loaded"), sem("f_loaded")
        first_xn, first_turned, first_xt, first_product, first_inp, first_gate, first_tg, first_c2 = (
            sem("first_xn"), sem("first_turned"), sem("first_xt"), sem("first_product"), sem("first_inp"), sem("first_gate"),
            sem("first_tg"), sem("first_c2"))
        x_tb_loaded = [sem(f"x_tb_loaded{n}") for n in range(2)]
        ctx_loaded = [sem(f"ctx_loaded{n}") for n in range(8)]
        x_g_loaded = [sem(f"x_g_loaded{n}") for n in range(2)]
        consts_ready, pool_zero, rows_b_ready = sem("consts_ready"), sem("pool_zero"), sem("rows_b_ready")
        io_turned, io_copied, ab_turned, ab_copied = sem("io_turned"), sem("io_copied"), sem("ab_turned"), sem("ab_copied")
        rest_turned, rest_copied, b2_ready, gw_kv_ready = (
            sem("rest_turned"), sem("rest_copied"), sem("b2_ready"), sem("gw_kv_ready"))
        p_var, p_rstd, xn_ready, xn_t_done, xn_t_ready = (
            sem("p_var"), sem("p_rstd"), sem("xn_ready"), sem("xn_t_done"), sem("xn_t_ready"))
        inp_done, inp_ready, pgate_done, tg_ready, c2_ready = (
            sem("inp_done"), sem("inp_ready"), sem("pgate_done"), sem("tg_ready"), sem("c2_ready"))
        ctx_t_done, ctx_t_ready, v_mean_ready, v_ready = (
            sem("ctx_t_done"), sem("ctx_t_ready"), sem("v_mean_ready"), sem("v_ready"))
        pre_ready, th_ready, w_ready = sem("pre_ready"), sem("th_ready"), sem("w_ready")
        xb_ready, s_ready, op_done, x1_ready = sem("xb_ready"), sem("s_ready"), sem("op_done"), sem("x1_ready")
        ln1_var, ln1_rstd, q_ready, q_t_done, q_t_ready, q_heads_ready = (
            sem("ln1_var"), sem("ln1_rstd"), sem("q_ready"), sem("q_t_done"), sem("q_t_ready"), sem("q_heads_ready"))
        ctx_g_ready, gates_done, gates_ready, ln_f_ready, log_f_ready, rows_done = (
            sem("ctx_g_ready"), sem("gates_done"), sem("gates_ready"), sem("ln_f_ready"), sem("log_f_ready"), sem("rows_done"))
        nm_ready, scans_ready, a_done, floor_ready, a_cols_ready = (
            sem("nm_ready"), sem("scans_ready"), sem("a_done"), sem("floor_ready"), sem("a_cols_ready"))
        nm_stored, arg_loaded = sem("nm_stored"), sem("arg_loaded")
        a_masked, arg_ready, decay_ready = sem("a_masked"), sem("arg_ready"), sem("decay_ready")
        qk_done, c_ready, pv_done, h_n_ready, h_sq_ready = (
            sem("qk_done"), sem("c_ready"), sem("pv_done"), sem("h_n_ready"), sem("h_sq_ready"))
        h_var_ready, h_rstd_ready, h_y_ready, h_o_ready, x2_ready = (
            sem("h_var_ready"), sem("h_rstd_ready"), sem("h_y_ready"), sem("h_o_ready"), sem("x2_ready"))
        ln2_var, ln2_rstd, x3_ready, x3_e1_ready = sem("ln2_var"), sem("ln2_rstd"), sem("x3_ready"), sem("x3_e1_ready")
        x3_t_done, x3_t_ready, e1_t_done, e1_t_ready, e0_t_ready = (
            sem("x3_t_done"), sem("x3_t_ready"), sem("e1_t_done"), sem("e1_t_ready"), sem("e0_t_ready"))
        ctx_gates_done, ctx_gates_ready = sem("ctx_gates_done"), sem("ctx_gates_ready")
        w_hi_ready, w_lo_ready, x3_lo_ready, e1_lo_ready = (
            sem("w_hi_ready"), sem("w_lo_ready"), sem("x3_lo_ready"), sem("e1_lo_ready"))
        l1_done, hid_ready, l2_done, y_t_ready, y_done, o_ready = (
            sem("l1_done"), sem("hid_ready"), sem("l2_done"), sem("y_t_ready"), sem("y_done"), sem("o_ready"))
        stored = sem("stored")
        dve_own, pool_own, act_own = sem("dve_own"), sem("pool_own"), sem("act_own")

        def first_batch(i):
            return GB * (i % NBG)

        def half(i):
            return i // NBG

        def at(op, n):
            if op in PREP:
                return [c for c in PREP_AT if PREP_AT[c] + PREP_X.get(c, {}).get(op, PREP[op]) == n]
            if op in CTX_GATES:
                return [g for g in CTX_GATES_AT if CTX_GATES_AT[g] + CTX_GATES[op] == n]
            return [g for g in range(NG) if GROUP_AT[g] + FILL.get(g, {}).get(op, GROUP[op]) == n]

        def chunk_at(op, n):
            return [(g, k) for g in range(NG) for k in range(NK) if GROUP_AT[g] + GROUP[op] + 2 * k == n]

        def ctx_no(g):
            return list(CTX_GATES_AT).index(g)

        mix_ops = ("out_product", "y_turn", "e1_turn", "q_turn", "gates", "ctx_gates", "rows", "a_cols", "x3_turn")
        mix_uses = [(op, g) for n in range(SLOTS) for op in mix_ops for g in at(op, n)]
        mix_reader = {"out_product": x1_ready, "y_turn": o_ready, "e1_turn": e1_lo_ready, "q_turn": q_t_ready,
                      "gates": gates_ready, "ctx_gates": ctx_gates_ready, "rows": scans_ready, "a_cols": floor_ready,
                      "x3_turn": x3_lo_ready}

        def tile_done(ins, tiles, chunk, m):
            ins.then_inc(chunk if m == NTL - 1 else tiles, 1)

        def tile_wait(eng, tiles, chunk, m):
            if m == NTL - 1:
                eng.wait_ge(chunk, 1)
            else:
                eng.wait_ge(tiles, m + 1)

        SPT = CT // NTL
        first = lambda buf, m: buf[:, m * SPT:(m + 1) * SPT, :].rearrange("p t b -> p (t b)")
        cols = [slice(m * P, (m + 1) * P) for m in range(NTL)]
        first_t_banks = (ps_l1[0][:, 0:P], ps_mix[:, 0:P])
        first_inp_banks = (ps_l1[1][:, 0:P], ps_l2[:, 0:P])
        first_gate_banks = (ps_pre[1][:, 0:P], ps_att[:, 1, 0:P])
        block = stack.enter_context(nc.Block())

        @block.sync
        def _(sp):
            def load_chunk(c):
                if c >= 2:
                    sp.wait_ge(xn_t_done, c - 1)
                src = x[:, c * CT:(c + 1) * CT, :].rearrange("b (k t) d -> t b k d", t=2)
                for t in range(2):
                    sp.dma_start(x_tb[64 * t:64 * t + 64, c % 2], src[t]).then_inc(x_tb_loaded[c % 2], 16)

            def load_ctx(q):
                if q >= 4:
                    sp.wait_ge(v_ready, q - 3)
                    sp.wait_ge(ctx_t_done, q - 3)
                src = ctx_in.rearrange("(n j) t d -> (j t) n d", j=2)
                sp.dma_start(ctx_nat[:, q % 4], src[:, 4 * q:4 * q + 4, :]).then_inc(ctx_loaded[q], 16)

            def load_group(i):
                if i >= 2:
                    sp.wait_ge(x1_ready, i - 1)
                b0, s0 = first_batch(i), SH * half(i)
                for r in range(BPT):
                    src = x[b0 + r:b0 + GB:BPT, s0:s0 + SH, :].rearrange("k s d -> s k d")
                    sp.dma_start(x_g[SH * r:SH * r + SH, i % 2], src).then_inc(x_g_loaded[i % 2], 16)

            load_chunk(0)
            sp.dma_start(w_nat[:, 0, :], w_in).then_inc(io_loaded, 16)
            sp.dma_start(w_nat[:, 1, :], w_gate).then_inc(io_loaded, 16)
            sp.dma_start(io_rows[0:1, :], b_in.unsqueeze(0)).then_inc(io_loaded, 16)
            sp.dma_start(io_rows[1:2, :], b_gate.unsqueeze(0)).then_inc(io_loaded, 16)
            sp.dma_start(w_nat[:, 2, :], w_b).then_inc(ab_loaded, 16)
            sp.dma_start(w_nat[:, 3, :], w_a).then_inc(ab_loaded, 16)
            load_chunk(1)
            load_ctx(0)
            load_ctx(1)
            load_chunk(2)
            load_group(0)
            load_ctx(2)
            sp.dma_start(w_nat[:, 4, :], w_out).then_inc(w_loaded, 16)
            sp.dma_start(gw_nat[0:NH, :], fg_w).then_inc(w_loaded, 16)
            sp.dma_start(gw_nat[NH:2 * NH, :], ig_w).then_inc(w_loaded, 16)
            sp.dma_start(bias_rows[0:NHC, :], sb1.rearrange("(c p) -> c p", p=P)).then_inc(w_loaded, 16)
            sp.dma_start(bias_rows[NHC:NK, :], b1.rearrange("e (c p) -> (e c) p", p=P)).then_inc(w_loaded, 16)
            sp.dma_start(bias_rows[NK:NK + 2, :], b2).then_inc(w_loaded, 16)
            sp.dma_start(bias_rows[NK + 2:NK + 3, :], sb2.unsqueeze(0)).then_inc(w_loaded, 16)
            load_ctx(3)
            load_chunk(3)
            sp.dma_start(b_out_rows[:], b_out.partition_broadcast(P)).then_inc(f_loaded, 16)
            sp.dma_start(gate_bias_rows[:, 0:NH], fg_b.partition_broadcast(P)).then_inc(f_loaded, 16)
            sp.dma_start(gate_bias_rows[:, NH:], ig_b.partition_broadcast(P)).then_inc(f_loaded, 16)
            sp.dma_start(ow_rows[:], out_w.partition_broadcast(P)).then_inc(f_loaded, 16)
            sp.dma_start(route_rows[:], gate_w.partition_broadcast(P)).then_inc(f_loaded, 16)
            sp.dma_start(w1_nat[:, 0, :], sw1).then_inc(f_loaded, 16)
            sp.dma_start(w1_nat[:, 1:3, :], w1.rearrange("e d h -> d e h")).then_inc(f_loaded, 16)
            sp.dma_start(w2_sb[:, 0:NHC, :], sw2.rearrange("(c p) d -> p c d", p=P)).then_inc(f_loaded, 16)
            sp.dma_start(w2_sb[:, NHC:, :], w2.rearrange("e (c p) d -> p (e c) d", p=P)).then_inc(f_loaded, 16)
            load_group(1)

            for n in range(SLOTS):
                for c in at("load_chunk", n):
                    if c >= 4:
                        load_chunk(c)
                for q in CTX_AT:
                    if q >= 4 and CTX_AT[q] - CTX_LEAD == n:
                        load_ctx(q)
                for g in at("bounce", n):
                    sp.wait_ge(nm_ready, g + 1)
                    sp.dma_start(row_scratch[g % 2].rearrange("b r s -> r b s"), nm_rows[:, g % 2]).then_inc(nm_stored, 16)
                    sp.wait_ge(nm_stored, 16 * (g + 1))
                    if g >= 1:
                        sp.wait_ge(arg_ready, g)
                    for j in range(2):
                        src = row_scratch[g % 2, j::2].rearrange("b r s -> b (r s)").partition_broadcast(S)
                        dst = arg[S * j:S * j + S].rearrange("p (b r) s -> p b (r s)", b=2)
                        sp.dma_start(dst, src).then_inc(arg_loaded, 16)
                    if g + 2 < NG:
                        load_group(g + 2)
                for g in at("store", n):
                    sp.wait_ge(o_ready, g + 1)
                    b0, s0 = first_batch(g), SH * half(g)
                    for r in range(BPT):
                        dst = out[b0 + r:b0 + GB:BPT, s0:s0 + SH, :].rearrange("k s d -> s k d")
                        sp.dma_start(dst, x2[SH * r:SH * r + SH, g % 3]).then_inc(stored, 16)
            sp.wait_ge(stored, 16 * BPT * NG)
            sp.wait_ge(nm_stored, 16 * NG)

        @block.gpsimd
        def _(pool):
            own = [0]

            def then(ins):
                own[0] += 1
                ins.then_inc(pool_own, 1)

            def settle():
                pool.wait_ge(pool_own, own[0])

            def rstd(var_in, ve, dst, seen, n, width, scale, signal):
                pool.wait_ge(seen, n)
                then(pool.tensor_scalar(ve, var_in, scale, LN_EPS, ALU.mult, ALU.add))
                settle()
                pool.tensor_tensor(dst, ve, minus_half[:, 0:width], ALU.pow).then_inc(signal, 1)

            def rstd_chunk(c):
                rstd(mv_tb[:, :, 1], var_tb[:], rstd_tb[:], p_var, c + 1, NTL, 1.0, p_rstd)

            def values(q):
                pool.wait_ge(v_mean_ready, q + 1)
                pool.tensor_tensor(v_ones[:, 4 * q:4 * q + 4, :, 0:DH].rearrange("p n h d -> p (n h) d"),
                                   ctx_nat[:, q % 4].rearrange("p n (h d) -> p (n h) d", h=NH),
                                   v_mean[:, q].unsqueeze(2).to_broadcast([P, NTL * NH, DH]), ALU.subtract).then_inc(v_ready, 1)

            def residual_base(i):
                d = i % 2
                pool.wait_ge(x_g_loaded[d], 16 * BPT * (i // 2 + 1))
                pool.tensor_tensor(x_g[:, d], x_g[:, d], b_out_rows[:].unsqueeze(1).to_broadcast([P, NTL, D]),
                                   ALU.add).then_inc(xb_ready, 1)

            def states(i):
                b0, t0 = first_batch(i), SH * half(i)
                pool.wait_ge(w_ready, t0 + SH)
                pool.wait_ge(c2_ready, (t0 + SH) // CT)
                if i >= 1:
                    pool.wait_ge(op_done, i)
                pool.tensor_tensor(s_t[:], c2[:, t0 + 1:t0 + SH + 1, b0:b0 + GB].rearrange("p t b -> p b t"),
                                   w2n[:, t0:t0 + SH, b0:b0 + GB].rearrange("p t b -> p b t"),
                                   ALU.subtract).then_inc(s_ready, 1)

            then(pool.memset(ident[:], 0.0))
            then(pool.memset(causal[:], 0.0))
            then(pool.memset(seg_keep[:], 1.0))
            then(pool.memset(seg_drop[:], 0.0))
            then(pool.memset(minus_half[:], -0.5))
            settle()
            then(pool.affine_select(out=ident[:], in_=ident[:], compare_op=ALU.not_equal, fill=1.0, base=0,
                                    pattern=[[-1, P]], channel_multiplier=1))
            settle()
            pool.memset(c2[:, 0, :], 0.0).then_inc(consts_ready, 1)
            rstd_chunk(0)
            for j in range(2):
                part = causal[S * j:S * j + S, :]
                settle()
                then(pool.affine_select(out=part, in_=part, compare_op=ALU.is_ge, fill=NEG, base=0,
                                        pattern=[[1, S]], channel_multiplier=-1))
            settle()
            then(pool.memset(seg_keep[:, :, 0:1], 0.0))
            then(pool.memset(seg_drop[:, :, 0:1], NEG))
            settle()
            rstd_chunk(1)
            for t, v in ((q_heads, 0.0), (c_diag, 0.0), (a_cols, 0.0), (cs_carry, 0.0), (m_carry, NEG)):
                pool.memset(t[:], v).then_inc(pool_zero, 1)
            pool.memset(v_ones[:, :, :, DH:DH + 1], 1.0).then_inc(pool_zero, 1)
            pool.wait_ge(pool_zero, 6)
            for n in range(SLOTS):
                for q in CTX_AT:
                    if CTX_AT[q] + VALUES_LAG == n:
                        values(q)
                for c in at("prep_rstd", n):
                    rstd_chunk(c)
                if n == ROWS_B_SLOT:
                    pool.wait_ge(f_loaded, 16 * 9)
                    then(pool.tensor_scalar(ow1_rows[:], ow_rows[:], 1.0, None, ALU.add))
                    pool.tensor_tensor(route_diff[:], route_rows[:, 1, :], route_rows[:, 0, :], ALU.subtract).then_inc(rows_b_ready, 1)
                    pool.wait_ge(rows_b_ready, 1)
                    settle()
                for j in W_AT:
                    if W_AT[j] + W_LO_LAG == n:
                        pool.wait_ge(w_hi_ready, j + 1)
                        pool.tensor_tensor(w1_lo[:, j], w1_nat[:, j], w1_hi[:, j].bitcast(F32), ALU.subtract).then_inc(w_lo_ready, 1)
                for g in at("e0", n):
                    pool.wait_ge(e1_lo_ready, g + 1)
                    if g >= 1:
                        pool.wait_ge(l1_done, NK * (g - 1) + 2 * NHC)
                    for part in (x3_hi, x3_lo):
                        last = pool.tensor_tensor(part[:, 1, :], part[:, 0, :].bitcast(F32), part[:, 2, :].bitcast(F32), ALU.subtract)
                        then(last) if part is x3_hi else last.then_inc(e0_t_ready, 1)
                for g in at("residual_base", n):
                    residual_base(g)
                for g in at("states", n):
                    states(g)
                for g in at("ln1_rstd", n):
                    rstd(mv_g[0][:, :, 1], var_g[0][:], rstd_g[0][:], ln1_var, g + 1, NTL, 1.0, ln1_rstd)
                for g in at("mask", n):
                    pool.wait_ge(a_cols_ready, 2 * (g + 1))
                    if g >= 1:
                        pool.wait_ge(c_ready, g)
                    h0 = SH * half(g)
                    pool.tensor_tensor(decay[:], causal[:, h0:h0 + SH].unsqueeze(1).to_broadcast([P, 2 * R, SH]),
                                       a_cols[:, g % NBG].unsqueeze(2).to_broadcast([P, 2 * R, SH]),
                                       ALU.add).then_inc(a_masked, 1)
                for g in at("h_rstd", n):
                    rstd(h_var[:], h_ve[:], h_rstd[:], h_var_ready, g + 1, R, 1.0 / DH, h_rstd_ready)
                for g in at("h_out", n):
                    pool.wait_ge(h_y_ready, g + 1)
                    pool.tensor_tensor(h_y[:].rearrange("p (k h) d -> p k (h d)", k=NTL), h_y[:].rearrange("p (k h) d -> p k (h d)", k=NTL),
                                       ow1_rows[:].unsqueeze(1).to_broadcast([P, NTL, D]), ALU.mult).then_inc(h_o_ready, 1)
                for g in at("ln2_rstd", n):
                    rstd(mv_g[1][:, :, 1], var_g[1][:], rstd_g[1][:], ln2_var, g + 1, NTL, 1.0, ln2_rstd)

        @block.scalar
        def _(act):
            own = [0]

            def then(ins):
                own[0] += 1
                ins.then_inc(act_own, 1)

            def settle():
                act.wait_ge(act_own, own[0])

            def prep_t(c):
                act.wait_ge(xn_t_done, c + 1)
                act.activation(xn_t[:, c % 2, :], ps_l1[0][:], ACT.Copy).then_inc(xn_t_ready, 1)

            def prep_inp(c):
                act.wait_ge(inp_done, c + 1)
                act.activation(inp[:, c * CT:(c + 1) * CT, :].rearrange("p t b -> p (t b)"), ps_l1[1][:], ACT.Identity,
                               bias=io_cols[:, 0:1]).then_inc(inp_ready, 1)

            def prep_gate(c):
                act.wait_ge(pgate_done, c + 1)
                act.activation(neg_tg[:, c * CT:(c + 1) * CT, :].rearrange("p t b -> p (t b)"), ps_l2[:], ACT.Tanh,
                               bias=half_neg_bgate[:], scale=-0.5).then_inc(tg_ready, 1)

            def ctx_evac(q):
                act.wait_ge(ctx_t_done, q + 1)
                act.activation(ctx_t[:, 8 * q:8 * q + 8, :].rearrange("p b t -> p (b t)"), ps_l1[0][:],
                               ACT.Copy).then_inc(ctx_t_ready, 1)

            def step(t):
                act.wait_ge(pre_ready, t + 1)
                col = (t % CT) * NB
                act.activation(th[:, t % 2, :], ps_pre[t // CT % 2][:, col:col + NB], ACT.Tanh).then_inc(th_ready, 1)

            act.wait_ge(io_turned, 1)
            act.activation(io_cols[:], ps_att[:, 0, 2 * P:2 * P + 2], ACT.Copy).then_inc(io_copied, 1)
            act.activation(w_in_t[:], ps_att[:, 0, 0:P], ACT.Copy).then_inc(io_copied, 1)
            act.activation(w_gate_t[:], ps_att[:, 0, P:2 * P], ACT.Copy).then_inc(io_copied, 1)
            act.wait_ge(io_copied, 1)
            act.activation(half_neg_bgate[:], io_cols[:, 1:2], ACT.Copy, scale=-0.5).then_inc(io_copied, 1)
            act.wait_ge(io_copied, 4)
            for m in range(NTL):
                tile_wait(act, first_turned, xn_t_done, m)
                tile_done(act.activation(xn_t[:, 0, cols[m]], first_t_banks[m % 2], ACT.Copy), first_xt, xn_t_ready, m)

            def first_inp_tile(m):
                tile_wait(act, first_product, inp_done, m)
                tile_done(act.activation(first(inp, m), first_inp_banks[m % 2], ACT.Identity, bias=io_cols[:, 0:1]),
                          first_inp, inp_ready, m)

            def first_gate_tile(m):
                tile_wait(act, first_gate, pgate_done, m)
                tile_done(act.activation(first(neg_tg, m), first_gate_banks[m % 2], ACT.Tanh, bias=half_neg_bgate[:], scale=-0.5),
                          first_tg, tg_ready, m)

            act.wait_ge(ab_turned, 1)
            act.activation(b_t[:], ps_att[:, 1, 0:P], ACT.Copy).then_inc(ab_copied, 1)
            act.activation(a_pos[:], ps_att[:, 1, P:2 * P], ACT.Copy, scale=0.5).then_inc(ab_copied, 1)
            act.activation(a_neg[:], ps_att[:, 1, P:2 * P], ACT.Copy, scale=-0.5).then_inc(ab_copied, 1)
            first_inp_tile(0)
            first_inp_tile(1)
            first_gate_tile(0)
            first_inp_tile(2)
            first_gate_tile(1)
            first_inp_tile(3)
            first_gate_tile(2)
            first_gate_tile(3)
            for n in range(SLOTS):
                if n == TABLE_SLOT:
                    act.preload_act_table_set("natural_log_exp_and_others")
                for t in STEPS_AT.get(n, ()):
                    step(t)
                for c in at("prep_xt", n):
                    prep_t(c)
                for c in at("prep_inp_out", n):
                    prep_inp(c)
                for c in at("prep_gate_out", n):
                    prep_gate(c)
                for q in CTX_AT:
                    if CTX_AT[q] == n:
                        ctx_evac(q)
                if n == REST_SLOT:
                    act.wait_ge(rest_turned, 1)
                    act.activation(bias_cols[:], ps_att[:, 0, 3 * P:3 * P + 15], ACT.Copy).then_inc(rest_copied, 1)
                    act.activation(w_out_t[:], ps_att[:, 1, 2 * P:3 * P], ACT.Copy, scale=0.5).then_inc(rest_copied, 1)
                    act.activation(gw_t[:], ps_att[:, 1, 3 * P:3 * P + 24].rearrange("p (n g) -> p n g", n=3),
                                   ACT.Copy).then_inc(rest_copied, 1)
                if n == REST_SLOT + 4:
                    act.wait_ge(rest_copied, 3)
                    then(act.activation(b2_part[:], bias_cols[:, NK:NK + 1], ACT.Identity, bias=bias_cols[:, NK + 1:NK + 2]))
                    settle()
                    act.activation(b2_sum[:], b2_part[:], ACT.Identity, bias=bias_cols[:, NK + 2:NK + 3]).then_inc(b2_ready, 1)
                for j in W_AT:
                    if W_AT[j] == n:
                        act.wait_ge(f_loaded, 16 * 9)
                        act.activation(w1_hi[:, j], w1_nat[:, j], ACT.Copy).then_inc(w_hi_ready, 1)
                for g, k in chunk_at("relu", n):
                    m = NK * g + k
                    act.wait_ge(l1_done, m + 1)
                    if m >= 3:
                        act.wait_ge(l2_done, m - 2)
                    if m == 0:
                        act.wait_ge(b2_ready, 1)
                        act.wait_ge(v_ready, 8)
                    act.activation(hid[:, m % 3, :], ps_l1[k % 2][:], ACT.Relu, bias=bias_cols[:, k:k + 1]).then_inc(hid_ready, 1)
                for g in at("y_out", n):
                    act.wait_ge(l2_done, NK * (g + 1))
                    if g >= 1:
                        act.wait_ge(y_done, g)
                    act.activation(y_t[:], ps_l2[:], ACT.Identity, bias=b2_sum[:]).then_inc(y_t_ready, 1)
                for g in at("x3_out", n):
                    act.wait_ge(x3_t_done, g + 1)
                    if g >= 1:
                        act.wait_ge(l1_done, NK * (g - 1) + NHC)
                    else:
                        act.wait_ge(w_lo_ready, NE)
                    act.activation(x3_hi[:, 0, :], ps_mix[:], ACT.Copy).then_inc(x3_t_ready, 1)
                for g in at("e1_out", n):
                    act.wait_ge(e1_t_done, g + 1)
                    if g >= 1:
                        act.wait_ge(l1_done, NK * g)
                    act.activation(x3_hi[:, 2, :], ps_mix[:], ACT.Copy).then_inc(e1_t_ready, 1)
                for g in at("q_out", n):
                    act.wait_ge(q_t_done, g + 1)
                    if g >= 1:
                        act.wait_ge(gates_done, g)
                        act.wait_ge(q_heads_ready, g)
                    act.activation(q_t[:].rearrange("p b s -> p (b s)"), ps_mix[:], ACT.Copy).then_inc(q_t_ready, 1)
                for g in at("softplus", n):
                    act.wait_ge(gates_ready, g + 1)
                    then(act.activation(abs_f[:], g_f[:], ACT.Abs))
                    settle()
                    then(act.activation(exp_f[:], abs_f[:], ACT.Exp, scale=-1.0))
                    settle()
                    act.activation(ln_f[:], exp_f[:], ACT.Ln, bias=1.0).then_inc(ln_f_ready, 1)
                for g in at("a_cols_out", n):
                    act.wait_ge(a_done, g + 1)
                    if g >= 1:
                        act.wait_ge(h_n_ready, g)
                    for j in range(2):
                        r0 = S * j + SH * half(g)
                        act.activation(a_cols[r0:r0 + SH, g % NBG, :], ps_mix[r0:r0 + SH, 256:256 + 2 * R],
                                       ACT.Copy).then_inc(a_cols_ready, 1)
                    act.activation(floor_exp[:], ps_mix[:, 320:320 + R], ACT.Exp).then_inc(floor_ready, 1)
                for g in at("decay_exp", n):
                    act.wait_ge(arg_ready, g + 1)
                    act.activation(decay[:], decay[:], ACT.Exp).then_inc(decay_ready, 1)
                for g in at("h_square", n):
                    act.wait_ge(h_n_ready, g + 1)
                    if g >= 1:
                        act.wait_ge(x2_ready, g)
                    act.activation(h_y[:], h_n[:], ACT.Square).then_inc(h_sq_ready, 1)

        @block.tensor
        def _(pe):
            flat = "p t b -> p (t b)"

            def transposes(dst, src, n=NTL):
                for k in range(n):
                    last = pe.transpose(dst[:, k * P:(k + 1) * P], src[:, k, :], ident[:])
                return last

            turned = [0, 0]

            def bank_free():
                if turned[0]:
                    pe.wait_ge(xn_t_ready, turned[0])
                if turned[1]:
                    pe.wait_ge(ctx_t_ready, turned[1])

            def prep_t(c):
                pe.wait_ge(xn_ready, c + 1)
                bank_free()
                transposes(ps_l1[0], x_tb[:, c % 2]).then_inc(xn_t_done, 1)
                turned[0] += 1

            def ctx_trans(q):
                pe.wait_ge(ctx_loaded[q], 16)
                bank_free()
                transposes(ps_l1[0], ctx_nat[:, q % 4]).then_inc(ctx_t_done, 1)
                turned[1] += 1

            def halves(h):
                return [slice(n * TOK // 2, (n + 1) * TOK // 2) for n in ((0, 1) if h is None else (h,))]

            def prep_inp(c, h=None):
                pe.wait_ge(xn_t_ready, c + 1)
                if c >= 1:
                    pe.wait_ge(inp_ready, c)
                for r in halves(h):
                    last = pe.matmul(ps_l1[1][:, r], w_in_t[:], xn_t[:, c % 2, r], start=True, stop=True)
                if h != 0:
                    last.then_inc(inp_done, 1)

            def prep_gate(c, h=None):
                pe.wait_ge(inp_ready, c + 1)
                if c >= 1:
                    pe.wait_ge(tg_ready, c)
                for r in halves(h):
                    last = pe.matmul(ps_l2[:, r], w_gate_t[:], inp[:, c * CT:(c + 1) * CT, :].rearrange(flat)[:, r],
                                     start=True, stop=True)
                if h != 0:
                    last.then_inc(pgate_done, 1)

            def base_b(c, h=None):
                pe.wait_ge(inp_ready, c + 1)
                if c >= 2:
                    pe.wait_ge(th_ready, CT * (c - 1))
                for r in halves(h):
                    pe.matmul(ps_pre[c % 2][:, r], b_t[:], inp[:, c * CT:(c + 1) * CT, :].rearrange(flat)[:, r],
                              start=(r.start == 0), stop=False, skip_group_check=True)

            def base_a(c, h=None):
                pe.wait_ge(c2_ready, c + 1)
                for r in halves(h):
                    last = pe.matmul(ps_pre[c % 2][:, r], a_pos[:], c2[:, c * CT:(c + 1) * CT, :].rearrange(flat)[:, r],
                                     start=False, stop=False, skip_group_check=True)
                if c == 0:
                    last.then_inc(pre_ready, 1)

            def step(t):
                if t == 0:
                    return
                pe.wait_ge(w_ready, t)
                col = (t % CT) * NB
                pe.matmul(ps_pre[t // CT % 2][:, col:col + NB], a_neg[:], w2n[:, t - 1, :], start=False, stop=True,
                          skip_group_check=True).then_inc(pre_ready, 1)

            pe.wait_ge(consts_ready, 1)
            pe.wait_ge(io_loaded, 16 * 4)
            pe.transpose(ps_att[:, 0, 2 * P:2 * P + 2], io_rows[:], ident[0:2, 0:2])
            transposes(ps_att[:, 0, :], w_nat, 2).then_inc(io_turned, 1)
            for m in range(NTL):
                tile_wait(pe, first_xn, xn_ready, m)
                if m >= 2:
                    pe.wait_ge(first_xt, m - 1)
                tile_done(pe.transpose(first_t_banks[m % 2], x_tb[:, 0, m, :], ident[:]), first_turned, xn_t_done, m)
                if m == 1:
                    pe.wait_ge(ab_loaded, 16 * 2)
                    transposes(ps_att[:, 1, :], w_nat[:, 2:4, :], 2).then_inc(ab_turned, 1)
            turned[0] += 1
            pe.wait_ge(io_copied, 4)

            def first_inp_tile(m):
                tile_wait(pe, first_xt, xn_t_ready, m)
                if m >= 2:
                    pe.wait_ge(first_inp, m - 1)
                tile_done(pe.matmul(first_inp_banks[m % 2], w_in_t[:], xn_t[:, 0, cols[m]], start=True, stop=True),
                          first_product, inp_done, m)

            def first_gate_tile(m):
                tile_wait(pe, first_inp, inp_ready, m)
                if m == 1:
                    pe.wait_ge(ab_copied, 3)
                if m >= 2:
                    pe.wait_ge(first_tg, m - 1)
                tile_done(pe.matmul(first_gate_banks[m % 2], w_gate_t[:], first(inp, m), start=True, stop=True), first_gate, pgate_done, m)

            def first_b_tile(m):
                pe.matmul(ps_pre[0][:, cols[m]], b_t[:], first(inp, m), start=(m == 0), stop=False, skip_group_check=True)

            def first_a_tile(m):
                tile_wait(pe, first_c2, c2_ready, m)
                last = pe.matmul(ps_pre[0][:, cols[m]], a_pos[:], first(c2, m), start=False, stop=False, skip_group_check=True)
                if m == NTL - 1:
                    last.then_inc(pre_ready, 1)

            first_inp_tile(0)
            first_inp_tile(1)
            first_gate_tile(0)
            first_inp_tile(2)
            first_gate_tile(1)
            first_b_tile(0)
            first_inp_tile(3)
            first_gate_tile(2)
            first_b_tile(1)
            first_gate_tile(3)
            first_b_tile(2)
            first_b_tile(3)
            for m in range(NTL):
                first_a_tile(m)

            def l1(g, k):
                n = NK * g + k
                if n == 0:
                    pe.wait_ge(w_lo_ready, NE)
                    pe.wait_ge(tg_ready, NC)
                    pe.wait_ge(ctx_t_ready, 8)
                if k == 0:
                    pe.wait_ge(x3_lo_ready, g + 1)
                if k == NHC:
                    pe.wait_ge(e0_t_ready, g + 1)
                if k == 2 * NHC:
                    pe.wait_ge(e1_lo_ready, g + 1)
                if n >= 2:
                    pe.wait_ge(hid_ready, n - 1)
                e = k // NHC
                col = (k % NHC) * P
                pe.matmul(ps_l1[k % 2][:], w1_hi[:, e, col:col + P], x3_hi[:, e, :], start=True, stop=False)
                pe.matmul(ps_l1[k % 2][:], w1_hi[:, e, col:col + P], x3_lo[:, e, :], start=False, stop=False)
                pe.matmul(ps_l1[k % 2][:], w1_lo[:, e, col:col + P], x3_hi[:, e, :], start=False, stop=True).then_inc(l1_done, 1)

            def l2(g, k):
                n = NK * g + k
                pe.wait_ge(hid_ready, n + 1)
                if k == 0 and g >= 1:
                    pe.wait_ge(y_t_ready, g)
                pe.matmul(ps_l2[:], w2_sb[:, k, :], hid[:, n % 3, :], start=(k == 0), stop=(k == NK - 1)).then_inc(l2_done, 1)

            def mix_free(op, g):
                m = mix_uses.index((op, g))
                if m >= 1:
                    before, g_before = mix_uses[m - 1]
                    pe.wait_ge(mix_reader[before], (ctx_no(g_before) if before == "ctx_gates" else g_before) + 1)

            for n in range(SLOTS):
                for t in STEPS_AT.get(n, ()):
                    step(t)
                for c in at("prep_turn", n):
                    prep_t(c)
                for h in range(2):
                    for c in at(f"prep_inp{h}", n):
                        prep_inp(c, h)
                    for c in at(f"prep_gate{h}", n):
                        prep_gate(c, h)
                for h in range(2):
                    for c in at(f"base_b{h}", n):
                        base_b(c, h)
                for c in at("base_a", n):
                    base_a(c)
                for q in CTX_AT:
                    if CTX_AT[q] == n:
                        ctx_trans(q)
                if n == REST_SLOT:
                    pe.wait_ge(w_loaded, 16 * 7)
                    pe.transpose(ps_att[:, 0, 3 * P:3 * P + 15], bias_rows[:], ident[0:15, 0:15])
                    pe.transpose(ps_att[:, 1, 2 * P:3 * P], w_nat[:, 4, :], ident[:])
                    for m in range(3):
                        last = pe.transpose(ps_att[:, 1, 3 * P + 8 * m:3 * P + 8 * m + 8], gw_nat[:, m * P:(m + 1) * P],
                                            ident[0:8, 0:8])
                    last.then_inc(rest_turned, 1)
                for g, k in chunk_at("l1", n):
                    l1(g, k)
                for g, k in chunk_at("l2", n):
                    l2(g, k)
                for g in at("out_product", n):
                    mix_free("out_product", g)
                    pe.wait_ge(s_ready, g + 1)
                    if g == 0:
                        pe.wait_ge(rest_copied, 3)
                    for m in range(NTL):
                        last = pe.matmul(ps_mix[:, m * P:(m + 1) * P],
                                         s_t[:, BPT * m:BPT * (m + 1), :].rearrange("p b s -> p (b s)"),
                                         w_out_t[:], start=True, stop=True)
                    last.then_inc(op_done, 1)
                for g in at("y_turn", n):
                    mix_free("y_turn", g)
                    pe.wait_ge(y_t_ready, g + 1)
                    transposes(ps_mix, y_t[:].rearrange("p (k m) -> p k m", k=NTL)).then_inc(y_done, 1)
                for g in at("e1_turn", n):
                    mix_free("e1_turn", g)
                    pe.wait_ge(x3_e1_ready, g + 1)
                    transposes(ps_mix, x3_e1).then_inc(e1_t_done, 1)
                for g in at("q_turn", n):
                    mix_free("q_turn", g)
                    pe.wait_ge(q_ready, g + 1)
                    transposes(ps_mix, q_nat).then_inc(q_t_done, 1)
                for g in at("gates", n):
                    mix_free("gates", g)
                    pe.wait_ge(q_t_ready, g + 1)
                    for m in range(NTL):
                        last = pe.matmul(ps_mix[:, 8 * m:8 * m + 8], q_t[:, BPT * m:BPT * (m + 1), :].rearrange("p b s -> p (b s)"),
                                         gw_t[:, 0, :], start=True, stop=True)
                    last.then_inc(gates_done, 1)
                for g in at("ctx_gates", n):
                    mix_free("ctx_gates", g)
                    pe.wait_ge(ctx_g_ready, ctx_no(g) + 1)
                    if g == 0:
                        pe.wait_ge(gw_kv_ready, 1)
                    for m in range(NTL):
                        last = pe.matmul(ps_mix[:, 8 * m:8 * m + 8], ctx_g[:, BPT * m:BPT * (m + 1), :].rearrange("p b s -> p (b s)"),
                                         gw_kv[:], start=True, stop=True)
                    last.then_inc(ctx_gates_done, 1)
                for g in at("rows", n):
                    mix_free("rows", g)
                    pe.wait_ge(log_f_ready, g + 1)
                    pe.transpose(ps_mix[0:R, 0:P], log_f[:].rearrange("p k h -> p (k h)"), ident[:])
                    pe.transpose(ps_mix[0:R, P:2 * P], g_i[:].rearrange("p k h -> p (k h)"), ident[:]).then_inc(rows_done, 1)
                for g in at("a_cols", n):
                    mix_free("a_cols", g)
                    h0 = SH * half(g)
                    pe.wait_ge(scans_ready, g + 1)
                    for b in range(BPT):
                        r0 = S * (b % 2) + h0
                        pe.matmul(ps_mix[r0:r0 + SH, 256 + R * (b // 2):256 + R * (b // 2 + 1)],
                                  a_rows[:, g % 2, b, 1:SH + 1], ident[0:R, 0:R], start=True, stop=True)
                    pe.transpose(ps_mix[:, 320:320 + R], nmc_rows[:, g % 2].rearrange("r b s -> r (b s)"),
                                 ident[0:R, 0:R]).then_inc(a_done, 1)
                for g in at("qk", n):
                    b0 = first_batch(g)
                    pe.wait_ge(q_heads_ready, g + 1)
                    if g < NBG:
                        pe.wait_ge(ctx_t_ready, 2 * g + 2)
                    if g >= 1:
                        pe.wait_ge(h_n_ready, g)
                    for b in range(GB):
                        m, r = b // BPT, b % BPT
                        j = r % 2
                        last = pe.matmul(ps_att[S * j:S * j + S, r // 2, m * P:(m + 1) * P], ctx_t[:, b0 + b, :],
                                         q_heads[:, b].rearrange("p h s -> p (h s)"), start=True, stop=True)
                    last.then_inc(qk_done, 1)
                for g in at("pv", n):
                    b0 = first_batch(g)
                    pe.wait_ge(c_ready, g + 1)
                    if g < NBG:
                        pe.wait_ge(v_ready, 2 * g + 2)
                    for m in range(NTL):
                        for h in range(NH):
                            for b in range(2):
                                col = ((m % 2) * NH + h) * (DH + 1)
                                last = pe.matmul(ps_att[S * b:S * b + S, m // 2, col:col + DH + 1],
                                                 c_diag[:, R * b + NH * m + h].rearrange("p j s -> p (j s)"),
                                                 v_ones[:, b0 // 2 + 2 * m + b, h, :], start=True, stop=True)
                    last.then_inc(pv_done, 1)
                for g in at("x3_turn", n):
                    mix_free("x3_turn", g)
                    pe.wait_ge(x3_ready, g + 1)
                    transposes(ps_mix, x3).then_inc(x3_t_done, 1)

        @block.vector
        def _(dve):
            flat = "p t b -> p (t b)"
            own = [0]

            def then(ins):
                own[0] += 1
                ins.then_inc(dve_own, 1)

            def settle():
                dve.wait_ge(dve_own, own[0])

            def statistics(src, bn, h):
                for k in range(2 * h, 2 * h + 2):
                    then(dve.bn_stats(bn[:, k, :], src[:, k, :]))

            def aggregate(bn, mv, signal):
                settle()
                for k in range(NTL):
                    last = dve.bn_aggr(mv[:, k, :], bn[:, k, :])
                last.then_inc(signal, 1)

            def normalise(dst, src, mv, rs, signal, h):
                for k in range(2 * h, 2 * h + 2):
                    last = dve.tensor_scalar(dst[:, k, :], src[:, k, :], mv[:, k, 0:1], rs[:, k:k + 1],
                                             ALU.subtract, ALU.mult)
                if h == 1:
                    last.then_inc(signal, 1)

            def prep_stats(c, h):
                dve.wait_ge(x_tb_loaded[c % 2], 32 * (c // 2 + 1))
                statistics(x_tb[:, c % 2], bn_tb, h)

            def prep_aggr(c):
                aggregate(bn_tb, mv_tb, p_var)

            def prep_norm(c, h):
                dve.wait_ge(p_rstd, c + 1)
                dve.wait_ge(p_var, c + 1)
                normalise(x_tb[:, c % 2], x_tb[:, c % 2], mv_tb, rstd_tb, xn_ready, h)

            def prep_c2(c):
                dve.wait_ge(tg_ready, c + 1)
                dve.wait_ge(inp_ready, c + 1)
                dve.scalar_tensor_tensor(c2[:, c * CT + 1:(c + 1) * CT + 1, :].rearrange(flat),
                                         neg_tg[:, c * CT:(c + 1) * CT, :].rearrange(flat), 1.0,
                                         inp[:, c * CT:(c + 1) * CT, :].rearrange(flat), ALU.add, ALU.mult).then_inc(c2_ready, 1)

            def value_means(q):
                dve.wait_ge(ctx_loaded[q], 16)
                then(dve.reduce_sum(v_sum[:, q], ctx_nat[:, q % 4].rearrange("p n (h d) -> p (n h) d", h=NH), AX_X))
                settle()
                dve.tensor_scalar(v_mean[:, q], v_sum[:, q], 1.0 / DH, None, ALU.mult).then_inc(v_mean_ready, 1)

            def step(t):
                dve.wait_ge(th_ready, t + 1)
                dve.scalar_tensor_tensor(w2n[:, t, :], neg_tg[:, t, :], 1.0, th[:, t % 2, :],
                                         ALU.subtract, ALU.mult).then_inc(w_ready, 1)

            def first_c2_tile(m):
                tile_wait(dve, first_tg, tg_ready, m)
                tile_wait(dve, first_inp, inp_ready, m)
                tile_done(dve.scalar_tensor_tensor(c2[:, m * SPT + 1:(m + 1) * SPT + 1, :].rearrange(flat), first(neg_tg, m), 1.0,
                                                   first(inp, m), ALU.add, ALU.mult), first_c2, c2_ready, m)

            prep_stats(0, 0)
            prep_stats(0, 1)
            prep_aggr(0)
            dve.wait_ge(p_rstd, 1)
            dve.wait_ge(p_var, 1)
            for m in range(NTL):
                tile_done(dve.tensor_scalar(x_tb[:, 0, m, :], x_tb[:, 0, m, :], mv_tb[:, m, 0:1], rstd_tb[:, m:m + 1],
                                            ALU.subtract, ALU.mult), first_xn, xn_ready, m)
            prep_stats(1, 0)
            prep_stats(1, 1)
            prep_aggr(1)
            for m in range(NTL):
                first_c2_tile(m)
            prep_norm(1, 0)
            prep_norm(1, 1)
            for n in range(SLOTS):
                for t in STEPS_AT.get(n, ()):
                    step(t)
                for q in CTX_AT:
                    if CTX_AT[q] + MEANS_LAG == n:
                        value_means(q)
                for h in range(2):
                    for c in at(f"prep_stats{h}", n):
                        prep_stats(c, h)
                for c in at("prep_aggr", n):
                    prep_aggr(c)
                for h in range(2):
                    for c in at(f"prep_norm{h}", n):
                        prep_norm(c, h)
                for c in at("prep_c2", n):
                    prep_c2(c)
                if n == REST_SLOT + 6:
                    dve.wait_ge(rest_copied, 3)
                    dve.tensor_tensor(gw_kv[:], gw_t[:, 1, :], gw_t[:, 2, :], ALU.add).then_inc(gw_kv_ready, 1)
                for g in at("ctx_copy", n):
                    b0, h0 = first_batch(g), SH * half(g)
                    dve.wait_ge(ctx_t_ready, 2 * (g % NBG) + 2)
                    if ctx_no(g) >= 1:
                        dve.wait_ge(ctx_gates_done, ctx_no(g))
                    dve.tensor_copy(ctx_g[:], ctx_t[:, b0:b0 + GB, h0:h0 + SH]).then_inc(ctx_g_ready, 1)
                for g in at("x1", n):
                    d = g % 2
                    dve.wait_ge(op_done, g + 1)
                    dve.wait_ge(xb_ready, g + 1)
                    dve.tensor_tensor(x1[:, g % 3], ps_mix[:].rearrange("p (k m) -> p k m", k=NTL), x_g[:, d],
                                      ALU.add).then_inc(x1_ready, 1)
                for h in range(2):
                    for g in at(f"x1_stats{h}", n):
                        dve.wait_ge(x1_ready, g + 1)
                        statistics(x1[:, g % 3], bn_g[0], h)
                for g in at("x1_aggr", n):
                    aggregate(bn_g[0], mv_g[0], ln1_var)
                for g in at("o", n):
                    dve.wait_ge(y_done, g + 1)
                    dve.tensor_tensor(x2[:, g % 3], ps_mix[:].rearrange("p (k m) -> p k m", k=NTL), x2[:, g % 3],
                                      ALU.add).then_inc(o_ready, 1)
                for h in range(2):
                    for g in at(f"q{h}", n):
                        dve.wait_ge(ln1_rstd, g + 1)
                        dve.wait_ge(ln1_var, g + 1)
                        if g >= 1:
                            dve.wait_ge(q_t_done, g)
                        normalise(q_nat, x1[:, g % 3], mv_g[0], rstd_g[0], q_ready, h)
                for g in at("x3_rest", n):
                    dve.wait_ge(x3_t_ready, g + 1)
                    dve.tensor_tensor(x3_lo[:, 0, :], ps_mix[:], x3_hi[:, 0, :].bitcast(F32), ALU.subtract).then_inc(x3_lo_ready, 1)
                for g in at("e1_rest", n):
                    dve.wait_ge(e1_t_ready, g + 1)
                    dve.tensor_tensor(x3_lo[:, 2, :], ps_mix[:], x3_hi[:, 2, :].bitcast(F32), ALU.subtract).then_inc(e1_lo_ready, 1)
                for j in range(2):
                    for g in at(f"q_heads{j}", n):
                        dve.wait_ge(q_t_ready, g + 1)
                        if g == 0:
                            dve.wait_ge(pool_zero, 6)
                        else:
                            dve.wait_ge(qk_done, g)
                        for h in range(2 * j, 2 * j + 2):
                            r = slice(DH * h, DH * h + DH)
                            last = dve.tensor_copy(q_heads[r, :, h, :], q_t[r])
                        if j == 1:
                            last.then_inc(q_heads_ready, 1)
                for g in at("gates_bias", n):
                    dve.wait_ge(gates_done, g + 1)
                    if g >= 1:
                        dve.wait_ge(rows_done, g)
                    pre = ps_mix[:, 0:8 * NTL].rearrange("p (k g) -> p k g", g=8)
                    dve.wait_ge(ctx_gates_ready, ctx_no(g) + 1)
                    then(dve.tensor_tensor(g_i[:], pre[:, :, NH:], ctx_gates[:, g, :, NH:], ALU.add))
                    dve.tensor_tensor(g_f[:], pre[:, :, 0:NH], ctx_gates[:, g, :, 0:NH], ALU.add).then_inc(gates_ready, 1)
                for g in at("ctx_gates_out", n):
                    dve.wait_ge(ctx_gates_done, ctx_no(g) + 1)
                    if g == 0:
                        dve.wait_ge(f_loaded, 16 * 9)
                    dve.tensor_tensor(ctx_gates[:, g], ps_mix[:, 0:8 * NTL].rearrange("p (k g) -> p k g", g=8),
                                      gate_bias_rows[:].unsqueeze(1).to_broadcast([P, NTL, 2 * NH]), ALU.add).then_inc(ctx_gates_ready, 1)
                for g in at("log_sigmoid", n):
                    dve.wait_ge(ln_f_ready, g + 1)
                    dve.wait_ge(gates_ready, g + 1)
                    settle()
                    kh = "p k h -> p (k h)"
                    dve.scalar_tensor_tensor(log_f[:].rearrange(kh), g_f[:].rearrange(kh), 0.0, ln_f[:].rearrange(kh),
                                             ALU.min, ALU.subtract).then_inc(log_f_ready, 1)
                for g in at("scans", n):
                    d, b = g % 2, g % NBG
                    dve.wait_ge(rows_done, g + 1)
                    if g >= 2:
                        dve.wait_ge(a_done, g - 1)
                        dve.wait_ge(nm_stored, 16 * (g - 1))
                    lf_ps = ps_mix[0:R, 0:P].rearrange("r (b s) -> r b s", b=BPT)
                    ig_ps = ps_mix[0:R, P:2 * P].rearrange("r (b s) -> r b s", b=BPT)
                    rows = "r b s -> r (b s)"
                    settle()
                    then(dve.tensor_copy(lf_rows[:, :, 0:1], cs_carry[:, b].unsqueeze(2)))
                    then(dve.tensor_copy(lf_rows[:, :, 1:], lf_ps))
                    then(dve.tensor_copy(a_rows[:, d, :, 0:1], m_carry[:, b].unsqueeze(2)))
                    settle()
                    then(dve.tensor_tensor_scan(cs_rows[:].rearrange(rows), seg_keep[:].rearrange(rows), lf_rows[:].rearrange(rows),
                                                0.0, ALU.mult, ALU.add))
                    settle()
                    then(dve.tensor_tensor(a_rows[:, d, :, 1:], ig_ps, cs_rows[:, :, 0:SH], ALU.subtract))
                    settle()
                    then(dve.tensor_tensor_scan(m_rows[:].rearrange(rows), seg_drop[:].rearrange(rows), a_rows[:, d].rearrange(rows),
                                                0.0, ALU.add, ALU.max))
                    settle()
                    dve.tensor_scalar(nm_rows[:, d], m_rows[:, :, 1:], -1.0, None, ALU.mult).then_inc(nm_ready, 1)
                    dve.wait_ge(nm_ready, g + 1)
                    then(dve.tensor_copy(cs_carry[:, b].unsqueeze(2), cs_rows[:, :, SH:]))
                    then(dve.tensor_copy(m_carry[:, b].unsqueeze(2), m_rows[:, :, SH:]))
                    dve.tensor_tensor(nmc_rows[:, d], nm_rows[:, d], cs_rows[:, :, 1:], ALU.subtract).then_inc(scans_ready, 1)
                for g in at("arg", n):
                    dve.wait_ge(a_masked, g + 1)
                    dve.wait_ge(arg_loaded, 32 * (g + 1))
                    dve.tensor_tensor(decay[:], decay[:], arg[:], ALU.add).then_inc(arg_ready, 1)
                for j in range(2):
                    for g in at(f"c_diag{j}", n):
                        dve.wait_ge(qk_done, g + 1)
                        dve.wait_ge(decay_ready, g + 1)
                        if g >= 1:
                            dve.wait_ge(pv_done, g)
                        r = slice(S * j, S * j + S)
                        last = dve.scalar_tensor_tensor(c_diag[r, :, j, :], ps_att[r].rearrange("p a (c s) -> p (a c) s", s=SH),
                                                        DH ** -0.5, decay[r], ALU.mult, ALU.mult)
                        if j == 1:
                            last.then_inc(c_ready, 1)
                for g in at("h_n", n):
                    dve.wait_ge(pv_done, g + 1)
                    dve.wait_ge(floor_ready, g + 1)
                    hp = ps_att[:, :, 0:2 * NH * (DH + 1)].rearrange("p a (g c) -> p a g c", c=DH + 1)
                    total = hp[:, :, :, DH]
                    two = "p (a g) -> p a g"
                    nv = [norm[:, m].rearrange(two, a=2) for m in range(4)]
                    then(dve.tensor_tensor(nv[0], total, floor_exp[:].rearrange(two, a=2), ALU.max))
                    settle()
                    then(dve.scalar_tensor_tensor(nv[1], total, -1.0, nv[0], ALU.mult, ALU.max))
                    settle()
                    then(dve.tensor_scalar(norm[:, 2], norm[:, 1], N_EPS, None, ALU.add))
                    settle()
                    then(dve.reciprocal(norm[:, 3], norm[:, 2]))
                    settle()
                    dve.tensor_tensor(h_n[:].rearrange("p (a g) d -> p a g d", a=2), hp[:, :, :, 0:DH],
                                      nv[3].unsqueeze(3).to_broadcast([P, 2, 2 * NH, DH]), ALU.mult).then_inc(h_n_ready, 1)
                for g in at("h_var", n):
                    dve.wait_ge(h_sq_ready, g + 1)
                    dve.reduce_sum(h_var[:], h_y[:], AX_X).then_inc(h_var_ready, 1)
                for g in at("h_y", n):
                    dve.wait_ge(h_rstd_ready, g + 1)
                    dve.wait_ge(h_var_ready, g + 1)
                    dve.tensor_tensor(h_y[:], h_n[:], h_rstd[:].unsqueeze(2).to_broadcast([P, R, DH]), ALU.mult).then_inc(h_y_ready, 1)
                for g in at("x2", n):
                    dve.wait_ge(h_o_ready, g + 1)
                    if g >= 3:
                        dve.wait_ge(stored, 16 * BPT * (g - 2))
                    dve.tensor_tensor(x2[:, g % 3], x1[:, g % 3], h_y[:].rearrange("p (k h) d -> p k (h d)", k=NTL), ALU.add).then_inc(x2_ready, 1)
                for h in range(2):
                    for g in at(f"x2_stats{h}", n):
                        dve.wait_ge(x2_ready, g + 1)
                        statistics(x2[:, g % 3], bn_g[1], h)
                for g in at("x2_aggr", n):
                    aggregate(bn_g[1], mv_g[1], ln2_var)
                for h in range(2):
                    for g in at(f"x3_{h}", n):
                        dve.wait_ge(ln2_rstd, g + 1)
                        dve.wait_ge(ln2_var, g + 1)
                        if g >= 1:
                            dve.wait_ge(x3_t_done, g)
                        normalise(x3, x2[:, g % 3], mv_g[1], rstd_g[1], x3_ready, h)
                for g in at("route", n):
                    dve.wait_ge(x3_ready, g + 1)
                    if g == 0:
                        dve.wait_ge(rows_b_ready, 1)
                    else:
                        dve.wait_ge(e1_t_done, g)
                    for m in range(NTL):
                        last = dve.tensor_tensor_reduce(x3_e1[:, m, :], x3[:, m, :], route_diff[:], 1.0, 0.0, ALU.mult, ALU.add,
                                                        route[:, m:m + 1])
                        then(last)
                    settle()
                    then(dve.tensor_scalar(pick[:], route[:], 0.0, None, ALU.is_gt))
                    settle()
                    dve.tensor_tensor(x3_e1[:], x3[:], pick[:].unsqueeze(2).to_broadcast([P, NTL, D]), ALU.mult).then_inc(x3_e1_ready, 1)


_INS = ['x', 'ctx_1024', 'L0_attn_A', 'L0_attn_B', 'L0_attn_W_in', 'L0_attn_b_in', 'L0_attn_W_gate', 'L0_attn_b_gate',
        'L0_attn_W_out', 'L0_attn_b_out', 'L0_xattn_igate_w', 'L0_xattn_igate_b', 'L0_xattn_fgate_w', 'L0_xattn_fgate_b',
        'L0_xattn_out_w', 'L0_ffn_gate_w', 'L0_ffn_w1', 'L0_ffn_b1', 'L0_ffn_w2', 'L0_ffn_b2', 'L0_ffn_sw1', 'L0_ffn_sb1',
        'L0_ffn_sw2', 'L0_ffn_sb2']


def kernel(**inputs):
    import numpy as np
    import concourse.bacc as bacc
    from concourse.bass_utils import run_bass_kernel_spmd

    nc = bacc.Bacc("TRN2", target_bir_lowering=False, num_devices=1)
    arrays, args = {}, []
    for name in _INS:
        a = np.ascontiguousarray(inputs[name])
        arrays[f"in_{name}"] = a
        args.append(nc.dram_tensor(f"in_{name}", a.shape, mybir.dt.from_np(a.dtype), kind="ExternalInput").ap())
    out = nc.dram_tensor("out_x", (NB, S, D), F32, kind="ExternalOutput").ap()
    decoder_layer(nc, *args, out)
    r = run_bass_kernel_spmd(nc, [arrays], core_ids=[0])
    return r.results[0]["out_x"]
```
